# Optimizing a Trainium2 kernel written in Bass

```python
import numpy as np
import jax
import jax.numpy as jnp

def _softmax(x, axis=-1):
    return jax.nn.softmax(x, axis=axis)

def _gelu(x):
    return jax.nn.gelu(x, approximate=True)

def _silu(x):
    return jax.nn.silu(x)

def _sigmoid(x):
    return jax.nn.sigmoid(x)

def _layernorm(x, axis=-1, eps=1e-05):
    m = jnp.mean(x, axis=axis, keepdims=True)
    v = jnp.var(x, axis=axis, keepdims=True)
    return (x - m) / jnp.sqrt(v + eps)

def _scatter_add(tgt, idx, src, axis=0):
    return tgt.at[idx].add(src)

def _segment_sum(src, seg, n):
    return jax.ops.segment_sum(src, seg, n)
kernel_name = 'mk_gnn_ffn_d2_gnn_r8_4bd527'

def setup_inputs(seed: int=0):
    np.random.seed(seed)
    _w = jnp.asarray

    def _rec_inputs():
        import jax
        import jax.numpy as jnp
        _gk = jax.random.key(seed)
        x = -8.776e-05 + 1 * jax.random.normal(jax.random.fold_in(_gk, 1), (2500, 256), jnp.float32)
        src = jax.random.randint(jax.random.fold_in(_gk, 2), (40000,), 0, 2500, jnp.int32)
        dst = jnp.minimum((2500 * jax.random.uniform(jax.random.fold_in(_gk, 3), (40000,)) ** 2.0).astype(jnp.int32), 19999)
        _o = jnp.argsort(dst, stable=True)
        src = src[_o]
        dst = dst[_o]
        edge_attr_256 = -8.513e-05 + 0.999844 * jax.random.normal(jax.random.fold_in(_gk, 12), (40000, 256), jnp.float32)
        return (x, src, dst, edge_attr_256)
    x, src, dst, edge_attr_256 = _rec_inputs()

    def _L0_gnn_setup():
        import jax, jax.numpy as jnp
        import numpy as np
        N_NODES = 2500
        N_EDGES = 40000
        IN_F = 256
        OUT_F = 256
        EDGE_F = 256

        def _mlp2(x, W1, b1, W2, b2):
            return jax.nn.relu(x @ W1 + b1) @ W2 + b2
        key = jax.random.key(seed)
        ks = jax.random.split(key, 12)

        def lin(k, fan_in, shape):
            bound = 1.0 / np.sqrt(fan_in)
            return jax.random.uniform(k, shape, jnp.float32, -bound, bound)
        node_feat = jax.random.normal(ks[0], (N_NODES, IN_F), jnp.float32)
        edge_feat = jax.random.normal(ks[1], (N_EDGES, EDGE_F), jnp.float32)
        src = jax.random.randint(ks[2], (N_EDGES,), 0, N_NODES, jnp.int32)
        dst = jax.random.randint(ks[3], (N_EDGES,), 0, N_NODES, jnp.int32)
        We1 = lin(ks[4], EDGE_F, (EDGE_F, 2 * EDGE_F))
        be1 = lin(ks[5], EDGE_F, (2 * EDGE_F,))
        We2 = lin(ks[6], 2 * EDGE_F, (2 * EDGE_F, IN_F))
        be2 = lin(ks[7], 2 * EDGE_F, (IN_F,))
        Wn1 = lin(ks[8], IN_F, (IN_F, 2 * IN_F))
        bn1 = lin(ks[9], IN_F, (2 * IN_F,))
        Wn2 = lin(ks[10], 2 * IN_F, (2 * IN_F, OUT_F))
        bn2 = lin(ks[11], 2 * IN_F, (OUT_F,))
        eps = jnp.zeros((1,), jnp.float32)
        return {'node_feat': node_feat, 'edge_feat': edge_feat, 'src': src, 'dst': dst, 'We1': We1, 'be1': be1, 'We2': We2, 'be2': be2, 'Wn1': Wn1, 'bn1': bn1, 'Wn2': Wn2, 'bn2': bn2, 'eps': eps}
    _L0_gnn_all = _L0_gnn_setup()
    _L0_gnn_in = {k: v for k, v in _L0_gnn_all.items() if k in ('We1', 'be1', 'We2', 'be2', 'Wn1', 'bn1', 'Wn2', 'bn2', 'eps')}
    del _L0_gnn_all

    def _L0_ffn_setup():
        import jax, jax.numpy as jnp
        import numpy as np
        D_MODEL = 256
        N_EXPERTS = 16
        HIDDEN = 512
        SCALE = 0.02
        key = jax.random.key(seed)
        ks = jax.random.split(key, 5)
        x = jax.random.normal(ks[0], (4, 1024, D_MODEL), dtype=jnp.float32)
        gate_w = jax.random.normal(ks[1], (D_MODEL, N_EXPERTS), dtype=jnp.float32) * SCALE
        gate_b = jnp.zeros((N_EXPERTS,), dtype=jnp.float32)
        w1 = jax.random.normal(ks[2], (N_EXPERTS, D_MODEL, HIDDEN), dtype=jnp.float32) * SCALE
        w2 = jax.random.normal(ks[3], (N_EXPERTS, D_MODEL, HIDDEN), dtype=jnp.float32) * SCALE
        w3 = jax.random.normal(ks[4], (N_EXPERTS, HIDDEN, D_MODEL), dtype=jnp.float32) * SCALE
        return {'x': x, 'gate_w': gate_w, 'gate_b': gate_b, 'w1': w1, 'w2': w2, 'w3': w3}
    _L0_ffn_all = _L0_ffn_setup()
    _L0_ffn_in = {k: v for k, v in _L0_ffn_all.items() if k in ('gate_w', 'gate_b', 'w1', 'w2', 'w3')}
    del _L0_ffn_all

    def _L1_gnn_setup():
        import jax, jax.numpy as jnp
        import numpy as np
        ALPHA = 0.2

        def _gat_head(node_feats, W, a, src, dst, N):
            h = node_feats @ W
            C = W.shape[1]
            a_l, a_r = (a[0, :C], a[0, C:])
            s_l = h @ a_l
            s_r = h @ a_r
            logits = s_l[src] + s_r[dst]
            e = jnp.exp(-jax.nn.leaky_relu(logits, negative_slope=ALPHA))
            row_sum = jax.ops.segment_sum(e, src, num_segments=N)
            h_prime = jax.ops.segment_sum(e[:, None] * h[dst], src, num_segments=N)
            return jax.nn.elu(h_prime / row_sum[:, None])
        key = jax.random.key(seed)
        k1, k2, k3, k4, k5, k6 = jax.random.split(key, 6)
        N, E, c_in, c_head = (6250, 100000, 256, 128)
        node_feats = jax.random.normal(k1, (N, c_in), dtype=jnp.float32)
        edge_index = jax.random.randint(k2, (2, E), 0, N, dtype=jnp.int64)
        std_W = 1.414 * np.sqrt(2.0 / (c_in + c_head))
        std_a = 1.414 * np.sqrt(2.0 / (1 + 2 * c_head))
        W1 = jax.random.normal(k3, (c_in, c_head), dtype=jnp.float32) * std_W
        a1 = jax.random.normal(k4, (1, 2 * c_head), dtype=jnp.float32) * std_a
        W2 = jax.random.normal(k5, (c_in, c_head), dtype=jnp.float32) * std_W
        a2 = jax.random.normal(k6, (1, 2 * c_head), dtype=jnp.float32) * std_a
        return {'node_feats': node_feats, 'W1': W1, 'a1': a1, 'W2': W2, 'a2': a2, 'edge_index': edge_index, 'N': N}
    _L1_gnn_all = _L1_gnn_setup()
    _L1_gnn_in = {k: v for k, v in _L1_gnn_all.items() if k in ('W1', 'a1', 'W2', 'a2')}
    del _L1_gnn_all

    def _L1_ffn_setup():
        import jax, jax.numpy as jnp
        import numpy as np
        DIM = 256
        H = 8
        D = 64
        G = 64
        INNER = H * D
        SCALE = D ** (-0.5)
        key = jax.random.key(seed)
        ks = jax.random.split(key, 12)
        B, N = (4, 2048)
        x = jax.random.normal(ks[0], (B, N, DIM), dtype=jnp.float32)
        s = lambda fan_in: 1.0 / np.sqrt(fan_in)
        W_fx = jax.random.normal(ks[1], (DIM, INNER), dtype=jnp.float32) * s(DIM)
        b_fx = jnp.zeros((INNER,), dtype=jnp.float32)
        W_x = jax.random.normal(ks[2], (DIM, INNER), dtype=jnp.float32) * s(DIM)
        b_x = jnp.zeros((INNER,), dtype=jnp.float32)
        A = jax.random.normal(ks[3], (G, D), dtype=jnp.float32)
        Q, _ = jnp.linalg.qr(A.T)
        W_slice = Q[:, :G].astype(jnp.float32)
        b_slice = jnp.zeros((G,), dtype=jnp.float32)
        W_q = jax.random.normal(ks[4], (D, D), dtype=jnp.float32) * s(D)
        W_k = jax.random.normal(ks[5], (D, D), dtype=jnp.float32) * s(D)
        W_v = jax.random.normal(ks[6], (D, D), dtype=jnp.float32) * s(D)
        W_out = jax.random.normal(ks[7], (INNER, DIM), dtype=jnp.float32) * s(INNER)
        b_out = jnp.zeros((DIM,), dtype=jnp.float32)
        temperature = jnp.ones((1, H, 1, 1), dtype=jnp.float32) * 0.5
        return {'x': x, 'W_fx': W_fx, 'b_fx': b_fx, 'W_x': W_x, 'b_x': b_x, 'W_slice': W_slice, 'b_slice': b_slice, 'W_q': W_q, 'W_k': W_k, 'W_v': W_v, 'W_out': W_out, 'b_out': b_out, 'temperature': temperature}
    _L1_ffn_all = _L1_ffn_setup()
    _L1_ffn_in = {k: v for k, v in _L1_ffn_all.items() if k in ('W_fx', 'b_fx', 'W_x', 'b_x', 'W_slice', 'b_slice', 'W_q', 'W_k', 'W_v', 'W_out', 'b_out', 'temperature')}
    del _L1_ffn_all
    return {'x': x, 'src': src, 'dst': dst, 'edge_attr_256': edge_attr_256, 'L0_gnn_We1': _L0_gnn_in['We1'], 'L0_gnn_be1': _L0_gnn_in['be1'], 'L0_gnn_We2': _L0_gnn_in['We2'], 'L0_gnn_be2': _L0_gnn_in['be2'], 'L0_gnn_Wn1': _L0_gnn_in['Wn1'], 'L0_gnn_bn1': _L0_gnn_in['bn1'], 'L0_gnn_Wn2': _L0_gnn_in['Wn2'], 'L0_gnn_bn2': _L0_gnn_in['bn2'], 'L0_gnn_eps': _L0_gnn_in['eps'], 'L0_ffn_gate_w': _L0_ffn_in['gate_w'], 'L0_ffn_gate_b': _L0_ffn_in['gate_b'], 'L0_ffn_w1': _L0_ffn_in['w1'], 'L0_ffn_w2': _L0_ffn_in['w2'], 'L0_ffn_w3': _L0_ffn_in['w3'], 'L1_gnn_W1': _L1_gnn_in['W1'], 'L1_gnn_a1': _L1_gnn_in['a1'], 'L1_gnn_W2': _L1_gnn_in['W2'], 'L1_gnn_a2': _L1_gnn_in['a2'], 'L1_ffn_W_fx': _L1_ffn_in['W_fx'], 'L1_ffn_b_fx': _L1_ffn_in['b_fx'], 'L1_ffn_W_x': _L1_ffn_in['W_x'], 'L1_ffn_b_x': _L1_ffn_in['b_x'], 'L1_ffn_W_slice': _L1_ffn_in['W_slice'], 'L1_ffn_b_slice': _L1_ffn_in['b_slice'], 'L1_ffn_W_q': _L1_ffn_in['W_q'], 'L1_ffn_W_k': _L1_ffn_in['W_k'], 'L1_ffn_W_v': _L1_ffn_in['W_v'], 'L1_ffn_W_out': _L1_ffn_in['W_out'], 'L1_ffn_b_out': _L1_ffn_in['b_out'], 'L1_ffn_temperature': _L1_ffn_in['temperature']}

def reference(x, src, dst, edge_attr_256, L0_gnn_We1, L0_gnn_be1, L0_gnn_We2, L0_gnn_be2, L0_gnn_Wn1, L0_gnn_bn1, L0_gnn_Wn2, L0_gnn_bn2, L0_gnn_eps, L0_ffn_gate_w, L0_ffn_gate_b, L0_ffn_w1, L0_ffn_w2, L0_ffn_w3, L1_gnn_W1, L1_gnn_a1, L1_gnn_W2, L1_gnn_a2, L1_ffn_W_fx, L1_ffn_b_fx, L1_ffn_W_x, L1_ffn_b_x, L1_ffn_W_slice, L1_ffn_b_slice, L1_ffn_W_q, L1_ffn_W_k, L1_ffn_W_v, L1_ffn_W_out, L1_ffn_b_out, L1_ffn_temperature):
    import jax
    import jax.numpy as jnp

    def _L0_gnn_ref(node_feat, edge_feat, src, dst, We1, be1, We2, be2, Wn1, bn1, Wn2, bn2, eps):
        import jax, jax.numpy as jnp
        import numpy as np
        N_NODES = 2500
        N_EDGES = 40000
        IN_F = 256
        OUT_F = 256
        EDGE_F = 256

        def _mlp2(x, W1, b1, W2, b2):
            return jax.nn.relu(x @ W1 + b1) @ W2 + b2
        e = _mlp2(edge_feat, We1, be1, We2, be2)
        msg = jax.nn.relu(node_feat[src] + e)
        out_h = jax.ops.segment_sum(msg, dst, num_segments=N_NODES)
        out = _mlp2((1.0 + eps[0]) * node_feat + out_h, Wn1, bn1, Wn2, bn2)
        return out

    def _L0_ffn_ref(x, gate_w, gate_b, w1, w2, w3):
        import jax, jax.numpy as jnp
        import numpy as np
        D_MODEL = 256
        N_EXPERTS = 16
        HIDDEN = 512
        SCALE = 0.02
        n_experts = w1.shape[0]
        logits = jnp.einsum('bsd,de->bse', x, gate_w) + gate_b
        probs = jax.nn.softmax(logits, axis=-1)
        top_probs, top_idx = jax.lax.top_k(probs, 2)
        top_probs = top_probs / jnp.sum(top_probs, axis=-1, keepdims=True)
        dispatch = jnp.sum(jax.nn.one_hot(top_idx, n_experts, dtype=x.dtype) * top_probs[..., None], axis=-2)
        h1 = jnp.einsum('bsd,edh->bseh', x, w1)
        h2 = jnp.einsum('bsd,edh->bseh', x, w2)
        hidden = jax.nn.silu(h1) * h2
        expert_out = jnp.einsum('bseh,eho->bseo', hidden, w3)
        return jnp.einsum('bseo,bse->bso', expert_out, dispatch)

    def _L1_gnn_ref(node_feats, W1, a1, W2, a2, edge_index, N):
        import jax, jax.numpy as jnp
        import numpy as np
        ALPHA = 0.2

        def _gat_head(node_feats, W, a, src, dst, N):
            h = node_feats @ W
            C = W.shape[1]
            a_l, a_r = (a[0, :C], a[0, C:])
            s_l = h @ a_l
            s_r = h @ a_r
            logits = s_l[src] + s_r[dst]
            e = jnp.exp(-jax.nn.leaky_relu(logits, negative_slope=ALPHA))
            row_sum = jax.ops.segment_sum(e, src, num_segments=N)
            h_prime = jax.ops.segment_sum(e[:, None] * h[dst], src, num_segments=N)
            return jax.nn.elu(h_prime / row_sum[:, None])
        src, dst = (edge_index[0], edge_index[1])
        out1 = _gat_head(node_feats, W1, a1, src, dst, N)
        out2 = _gat_head(node_feats, W2, a2, src, dst, N)
        return jnp.concatenate([out1, out2], axis=1)

    def _L1_ffn_ref(x, W_fx, b_fx, W_x, b_x, W_slice, b_slice, W_q, W_k, W_v, W_out, b_out, temperature):
        import jax, jax.numpy as jnp
        import numpy as np
        DIM = 256
        H = 8
        D = 64
        G = 64
        INNER = H * D
        SCALE = D ** (-0.5)
        B, N, _ = x.shape
        fx_mid = (x @ W_fx + b_fx).reshape(B, N, H, D).transpose(0, 2, 1, 3)
        x_mid = (x @ W_x + b_x).reshape(B, N, H, D).transpose(0, 2, 1, 3)
        temp = jnp.clip(temperature, 0.1, 5.0)
        slice_weights = jax.nn.softmax((x_mid @ W_slice + b_slice) / temp, axis=-1)
        slice_norm = slice_weights.sum(axis=2)
        slice_token = jnp.einsum('bhnc,bhng->bhgc', fx_mid, slice_weights)
        slice_token = slice_token / (slice_norm[..., None] + 1e-05)
        q = slice_token @ W_q
        k = slice_token @ W_k
        v = slice_token @ W_v
        attn = jax.nn.softmax(jnp.einsum('bhgc,bhkc->bhgk', q, k) * SCALE, axis=-1)
        out_slice = jnp.einsum('bhgk,bhkc->bhgc', attn, v)
        out_x = jnp.einsum('bhgc,bhng->bhnc', out_slice, slice_weights)
        out_x = out_x.transpose(0, 2, 1, 3).reshape(B, N, INNER)
        return out_x @ W_out + b_out
    edge_index = jnp.stack([src, dst])
    x = x + _L0_gnn_ref(_layernorm(x, axis=-1), edge_attr_256, src, dst, L0_gnn_We1, L0_gnn_be1, L0_gnn_We2, L0_gnn_be2, L0_gnn_Wn1, L0_gnn_bn1, L0_gnn_Wn2, L0_gnn_bn2, L0_gnn_eps)
    x = x + _L0_ffn_ref(_layernorm(x, axis=-1)[None], L0_ffn_gate_w, L0_ffn_gate_b, L0_ffn_w1, L0_ffn_w2, L0_ffn_w3)[0]
    x = x + _L1_gnn_ref(_layernorm(x, axis=-1), L1_gnn_W1, L1_gnn_a1, L1_gnn_W2, L1_gnn_a2, edge_index, 2500)
    x = x + _L1_ffn_ref(_layernorm(x, axis=-1)[None], L1_ffn_W_fx, L1_ffn_b_fx, L1_ffn_W_x, L1_ffn_b_x, L1_ffn_W_slice, L1_ffn_b_slice, L1_ffn_W_q, L1_ffn_W_k, L1_ffn_W_v, L1_ffn_W_out, L1_ffn_b_out, L1_ffn_temperature)[0]
    return x

_drawn_inputs = setup_inputs


def setup_inputs(seed=0):
    import zlib

    import numpy as np

    out = dict(_drawn_inputs(seed))
    spreads = {'L0_ffn_gate_b': (0.0, 0.8),
     'L1_ffn_b_fx': (0.0, 0.27),
     'L1_ffn_b_x': (0.0, 2.0),
     'L1_ffn_b_slice': (0.0, 2.0),
     'L1_ffn_b_out': (0.0, 1.174),
     'L1_ffn_temperature': (0.5, 0.6)}
    factors = {'L0_gnn_be1': 5.218,
     'L0_gnn_bn1': 8.0,
     'L0_gnn_bn2': 5.69,
     'L0_ffn_gate_w': 8.0,
     'L0_ffn_w1': 8.0,
     'L0_ffn_w2': 8.0,
     'L0_ffn_w3': 8.0,
     'L1_gnn_a1': 3.651,
     'L1_ffn_W_x': 8.0,
     'L1_ffn_W_slice': 8.0,
     'L1_ffn_W_q': 8.0,
     'L1_ffn_W_k': 8.0,
     'L1_gnn_a2': 3.221}
    for name, (base, spread) in spreads.items():
        noise = np.random.default_rng([zlib.crc32(name.encode()), seed]).standard_normal(out[name].shape)
        drawn = base * np.exp(spread * noise) if base else spread * noise
        out[name] = jnp.asarray(drawn.astype(out[name].dtype))
    for name, factor in factors.items():
        out[name] = (out[name] * factor).astype(out[name].dtype)
    return out
```

```python
from contextlib import ExitStack

import concourse.bass as bass
from concourse import mybir

F32 = mybir.dt.float32
F16 = mybir.dt.float16
I32 = mybir.dt.int32
ALU = mybir.AluOpType
ACT = mybir.ActivationFunctionType
AX_X = mybir.AxisListType.X

N_NODES, DIM = 2500, 256
N_EDGES = 40000
P = 128
LANES = 125
TILES = N_NODES // LANES
EDGE_COLS = N_EDGES // LANES
KD = DIM // P
HID = 2 * DIM
KH = HID // P
LN_EPS = 1e-5

EXPERTS, TOP = 16, 2
GROUP = 4
EDGE_BLOCKS = -(-((N_EDGES + TILES * (P - 1)) // P) // (2 * GROUP)) * 2 * GROUP
MOE_BLOCKS = -(-((N_NODES * TOP + EXPERTS * (P - 1)) // P) // 2) * 2
NODE_MID = N_NODES // 2

HEADS, HEAD_C = 2, 128
NEG_SLOPE = 0.2
ROW = HEADS * (HEAD_C + 1)
SA_HEADS, SA_D, SLICES = 8, 64, 64
INNER = SA_HEADS * SA_D
PAIRS = INNER // P
CHUNK = 4
CHUNKS = TILES // CHUNK
CW = CHUNK * LANES


class Slots:

    def __init__(self, pos, blk, tile_row):
        self.pos, self.blk, self.tile_row = pos, blk, tile_row


class Ends:

    def __init__(self, other, lane, tile_row, edge=None):
        self.other, self.lane, self.tile_row, self.edge = other, lane, tile_row, edge


class Shared:

    def __init__(self, nc, sb, sem):
        self.constants_made = sem("constants_made")
        self.gathers_begun = sem("gathers_begun")
        self.ident = sb("ident", [P, P])
        self.before = sb("before", [P, P])
        self.ones = sb("ones", [P, P])
        self.count_i = sb("count_i", [P, EDGE_BLOCKS], I32)
        self.count = sb("count", [P, EDGE_BLOCKS])
        self.count16 = sb("count16", [P, EDGE_BLOCKS], F16)
        self.lane_i = sb("lane_i", [P, 1], I32)
        self.lane = sb("lane", [P, 1])
        self.node_i = sb("node_i", [LANES, TILES], I32)
        self.node = sb("node", [LANES, TILES])
        self.x = sb("x", [LANES, TILES, DIM])
        self.y = sb("y", [LANES, TILES, DIM])
        self.row_a = sb("row_a", [LANES, 2, DIM])
        self.eps = sb("eps", [LANES, 1])
        self.dst_i = sb("dst_i", [LANES, EDGE_COLS], I32)
        self.src_i = sb("src_i", [LANES, EDGE_COLS], I32)
        self.node_table = nc.dram_tensor("node_table", [N_NODES, DIM], F32, kind="Internal").ap()
        self.routed = nc.dram_tensor("routed", [MOE_BLOCKS * P, DIM], F32, kind="Internal").ap()
        self.head_table = nc.dram_tensor("head_table", [N_NODES, ROW], F32, kind="Internal").ap()


def own_waits(pool, m):
    pool.sem_inc(m.gathers_begun, 1)


class Chain:

    def __init__(self, eng, sem):
        self.eng, self.sem, self.n = eng, sem, 0

    def link(self, ins):
        self.n += 1
        ins.then_inc(self.sem, 1)
        self.eng.wait_ge(self.sem, self.n)


def constants(nc, m, sem):
    made = m.constants_made
    with nc.Block() as block:

        @block.gpsimd
        def _(pool):
            chain = Chain(pool, made)
            chain.link(pool.memset(m.ident[:], 0.0))
            chain.link(pool.affine_select(out=m.ident[:], in_=m.ident[:], compare_op=ALU.not_equal, fill=1.0,
                                     base=0, pattern=[[-1, P]], channel_multiplier=1))
            chain.link(pool.memset(m.before[:], 1.0))
            chain.link(pool.affine_select(out=m.before[:], in_=m.before[:], compare_op=ALU.is_gt, fill=0.0,
                                     base=0, pattern=[[1, P]], channel_multiplier=-1))
            chain.link(pool.memset(m.ones[:], 1.0))
            chain.link(pool.iota(m.count_i[:], pattern=[[1, EDGE_BLOCKS]], base=0, channel_multiplier=0))
            chain.link(pool.iota(m.lane_i[:], pattern=[[0, 1]], base=0, channel_multiplier=1))
            chain.link(pool.iota(m.node_i[:], pattern=[[1, TILES]], base=0, channel_multiplier=TILES))

        @block.vector
        def _(dve):
            dve.wait_ge(made, 8)
            nc.vector.tensor_copy(m.count[:], m.count_i[:])
            nc.vector.tensor_copy(m.count16[:], m.count_i[:])
            nc.vector.tensor_copy(m.lane[:], m.lane_i[:])
            nc.vector.tensor_copy(m.node[:], m.node_i[:])


def slots_of_buckets(nc, sem, m, name, bucket, cols, buckets, blocks, out):
    done = sem(name + "_dve")
    counted = sem(name + "_counted")
    summed = sem(name + "_summed")
    with ExitStack() as ctx:
        def sb(n, shape, dt=F32):
            return ctx.enter_context(nc.sbuf_tensor(f"{name}_{n}", shape, dt))

        mask = sb("mask", [LANES, buckets, cols])
        seen = sb("seen", [LANES, buckets, cols])
        ends = sb("ends", [LANES, buckets + 1])
        mine = sb("mine", [LANES, buckets])
        nblk = sb("nblk", [LANES, buckets])
        nblk_i = sb("nblk_i", [LANES, buckets], I32)
        last = sb("last", [LANES, buckets])
        off = sb("off", [LANES, buckets])
        slot = sb("slot", [LANES, cols])
        slot_i = sb("slot_i", [LANES, cols], I32)
        part_i = sb("part_i", [LANES, cols], I32)
        past = sb("past", [1, blocks, buckets])
        tile_f = sb("tile_f", [1, blocks])
        sums = ctx.enter_context(nc.psum_tensor(name + "_sums", [P, 2, 512], F32))
        with nc.Block() as block:

            @block.tensor
            def _(pe):
                pe.wait_ge(counted, 1)
                nc.tensor.matmul(sums[0:LANES, 0, 0:buckets], m.before[0:LANES, 0:LANES], mine[:], start=True, stop=True)
                nc.tensor.matmul(sums[0:LANES, 1, 0:buckets], m.ones[0:LANES, 0:LANES], mine[:], start=True, stop=True).then_inc(summed, 1)

            @block.vector
            def _(dve):
                chain = Chain(dve, done)
                chain.link(nc.vector.memset(ends[:], 0.0))
                chain.link(nc.vector.tensor_tensor(
                    mask[:], bucket.unsqueeze(1).to_broadcast([LANES, buckets, cols]),
                    m.count[0:LANES, 0:buckets].unsqueeze(2).to_broadcast([LANES, buckets, cols]), ALU.is_equal))
                flat = mask[:].rearrange("p b c -> p (b c)")
                chain.link(nc.vector.tensor_tensor_scan(seen[:].rearrange("p b c -> p (b c)"), flat, flat, 0.0, ALU.add, ALU.max))
                chain.link(nc.vector.tensor_copy(ends[:, 1:], seen[:, :, cols - 1]))
                nc.vector.tensor_tensor(mine[:], ends[:, 1:], ends[:, 0:buckets], ALU.subtract).then_inc(counted, 1)
                dve.wait_ge(summed, 1)
                chain.link(nc.vector.tensor_scalar(nblk_i[:], sums[0:LANES, 1, 0:buckets], (P - 1) / 2, 1 / P, ALU.add, ALU.mult))
                chain.link(nc.vector.tensor_copy(nblk[:], nblk_i[:]))
                chain.link(nc.vector.tensor_tensor_scan(last[:], nblk[:], nblk[:], 0.0, ALU.add, ALU.max))
                chain.link(nc.vector.tensor_tensor(off[:], last[:], nblk[:], ALU.subtract))
                chain.link(nc.vector.tensor_scalar(off[:], off[:], float(P), -1.0, ALU.mult, ALU.add))
                chain.link(nc.vector.tensor_tensor(off[:], off[:], sums[0:LANES, 0, 0:buckets], ALU.add))
                chain.link(nc.vector.tensor_tensor(off[:], off[:], ends[:, 0:buckets], ALU.subtract))
                chain.link(nc.vector.tensor_tensor(seen[:], seen[:], off[:].unsqueeze(2).to_broadcast([LANES, buckets, cols]), ALU.add))
                chain.link(nc.vector.tensor_tensor(seen[:], seen[:], mask[:], ALU.mult))
                chain.link(nc.vector.tensor_reduce(slot[:], seen[:].rearrange("p b c -> p c b"), AX_X, ALU.add))
                chain.link(nc.vector.tensor_copy(slot_i[:], slot[:]))
                chain.link(nc.vector.tensor_scalar(part_i[:], slot_i[:], 7, None, ALU.arith_shift_right))
                chain.link(nc.vector.tensor_copy(out.blk, part_i[:]))
                chain.link(nc.vector.tensor_scalar(slot_i[:], slot_i[:], P - 1, None, ALU.bitwise_and))
                chain.link(nc.vector.tensor_copy(out.pos, slot_i[:]))
                chain.link(nc.vector.tensor_tensor(
                    past[:], m.count[0:1, 0:blocks].unsqueeze(2).to_broadcast([1, blocks, buckets]),
                    last[0:1, :].unsqueeze(1).to_broadcast([1, blocks, buckets]), ALU.is_ge))
                chain.link(nc.vector.tensor_reduce(tile_f[:], past[:], AX_X, ALU.add))
                chain.link(nc.vector.tensor_scalar(out.tile_row, tile_f[:], float(buckets - 1), None, ALU.min))


def place_in_slots(nc, sem, m, name, pos, blk, values, cols, blocks, finish):
    nv = len(values)
    made = sem(name + "_made")
    used = sem(name + "_used")
    fin = sem(name + "_fin")
    with ExitStack() as ctx:
        rows = [ctx.enter_context(nc.sbuf_tensor(f"{name}_rows{u}", [LANES, nv, P], F16)) for u in range(2)]
        which = [ctx.enter_context(nc.sbuf_tensor(f"{name}_which{u}", [LANES, blocks], F16)) for u in range(2)]
        tables = ctx.enter_context(nc.psum_tensor(name + "_tables", [P, nv, 512], F32))

        def factors(c, u):
            one = bass.DynSlice(c, 1)
            for v, value in enumerate(values):
                nc.vector.tensor_scalar(rows[u][:, v, :], m.count16[0:LANES, 0:P], pos[:, one], value[:, one],
                                        ALU.is_equal, ALU.mult)
            return nc.vector.tensor_scalar(which[u][:], m.count16[0:LANES, 0:blocks], blk[:, one], None, ALU.is_equal)

        def products(u, start, stop):
            for v in range(nv):
                last = nc.tensor.matmul(tables[:, v, 0:blocks], rows[u][:, v, :], which[u][:], start=start, stop=stop)
            return last

        with nc.Block() as block:

            @block.vector
            def _(dve):
                for u in range(2):
                    factors(u, u).then_inc(made, 1)
                with dve.Fori(1, cols // 2) as i:
                    for u in range(2):
                        dve.wait_ge(used, 2 * i + (u - 1))
                        factors(2 * i + u, u).then_inc(made, 1)
                dve.wait_ge(used, cols)
                finish(dve, Chain(dve, fin), tables)

            @block.tensor
            def _(pe):
                for u in range(2):
                    pe.wait_ge(made, u + 1)
                    products(u, u == 0, False).then_inc(used, 1)
                with pe.Fori(1, cols // 2 - 1) as i:
                    for u in range(2):
                        pe.wait_ge(made, 2 * i + (u + 1))
                        products(u, False, False).then_inc(used, 1)
                for u in range(2):
                    pe.wait_ge(made, cols - 1 + u)
                    products(u, False, u == 1).then_inc(used, 1)


def layer_norm(nc, sem, m, name, x, y):
    done = sem(name + "_dve")
    var_ready = sem(name + "_var_ready")
    std_ready = sem(name + "_std_ready")
    with ExitStack() as ctx:
        stats = ctx.enter_context(nc.sbuf_tensor(name + "_stats", [LANES, TILES, 6], F32))
        mv = ctx.enter_context(nc.sbuf_tensor(name + "_mv", [LANES, TILES, 2], F32))
        var = ctx.enter_context(nc.sbuf_tensor(name + "_var", [LANES, TILES], F32))
        std = ctx.enter_context(nc.sbuf_tensor(name + "_std", [LANES, TILES], F32))
        rstd = ctx.enter_context(nc.sbuf_tensor(name + "_rstd", [LANES, TILES], F32))
        with nc.Block() as block:

            @block.scalar
            def _(act):
                act.wait_ge(var_ready, 1)
                nc.scalar.activation(std[:], var[:], ACT.Sqrt).then_inc(std_ready, 1)

            @block.vector
            def _(dve):
                for t in range(TILES):
                    nc.vector.bn_stats(stats[:, t, :], x[:, t, :]).then_inc(done, 1)
                for t in range(TILES):
                    dve.wait_ge(done, t + 1)
                    nc.vector.bn_aggr(mv[:, t, :], stats[:, t, :]).then_inc(done, 1)
                dve.wait_ge(done, 2 * TILES)
                nc.vector.tensor_scalar(var[:], mv[:, :, 1], LN_EPS, None, ALU.add).then_inc(var_ready, 1)
                dve.wait_ge(std_ready, 1)
                nc.vector.reciprocal(rstd[:], std[:]).then_inc(done, 1)
                dve.wait_ge(done, 2 * TILES + 1)
                for t in range(TILES):
                    nc.vector.tensor_scalar(y[:, t, :], x[:, t, :], mv[:, t, 0:1], rstd[:, t:t + 1],
                                            ALU.subtract, ALU.mult)


def edge_messages(nc, sem, m, io):
    w_in = sem("edge_weights_in")
    edge_idx_ready = sem("edge_edge_idx_ready")
    node_idx_ready = sem("edge_node_idx_ready")
    ea_landed = [sem(f"edge_ea_landed{u}") for u in range(2)]
    nf_landed = [sem(f"edge_nf_landed{u}") for u in range(2)]
    turned = sem("edge_turned")
    turned_in = sem("edge_turned_in")
    hid_up = sem("edge_hid_up")
    hid_ready = sem("edge_hid_ready")
    e_up = sem("edge_e_up")
    summed = sem("edge_msg_summed")
    msg_ready = sem("edge_msg_ready")
    hot_ready = sem("edge_hot_ready")
    scattered = sem("edge_scattered")
    added = sem("edge_added")
    G = GROUP
    groups = EDGE_BLOCKS // G
    with ExitStack() as ctx:
        def sb(n, shape, dt=F32):
            return ctx.enter_context(nc.sbuf_tensor(f"edge_{n}", shape, dt))

        def ps(n, shape):
            return ctx.enter_context(nc.psum_tensor(f"edge_{n}", shape, F32))

        w1 = sb("w1", [P, KD, HID])
        b1 = sb("b1", [P, KH])
        w2 = sb("w2", [P, KH, DIM])
        edge_idx = [sb(f"edge_idx{u}", [P, G], I32) for u in range(2)]
        node_idx = [sb(f"node_idx{u}", [P, G], I32) for u in range(2)]
        ea = [sb(f"ea{u}", [P, G, DIM]) for u in range(2)]
        nf = [sb(f"nf{u}", [P, G, DIM]) for u in range(2)]
        eat = [sb(f"eat{u}", [P, KD, G * P]) for u in range(2)]
        hid = [sb(f"hid{u}", [P, KH, G * P]) for u in range(2)]
        pre = [sb(f"pre{u}", [P, G, DIM]) for u in range(2)]
        msg = [sb(f"msg{u}", [P, G, DIM]) for u in range(2)]
        hot = [sb(f"hot{u}", [P, G, LANES]) for u in range(2)]
        t_ps = ps("t_ps", [P, KD, G * P])
        h_ps = ps("h_ps", [P, 2, G * P])
        e_ps = ps("e_ps", [P, G, DIM])
        s_ps = ps("s_ps", [P, G, DIM])

        with nc.Block() as block:

            @block.sync
            def _(sp):
                sp.dma_start(w1[:], io["We1"].rearrange("(k p) h -> p k h", p=P)).then_inc(w_in, 16)
                sp.dma_start(w2[:], io["We2"].rearrange("(k p) h -> p k h", p=P)).then_inc(w_in, 16)
                sp.dma_start(b1[:], io["be1"]).then_inc(w_in, 16)

            def gather_edges(u):
                own_waits(nc.gpsimd, m)
                for j in range(G):
                    nc.gpsimd.indirect_dma_start(ea[u][:, j, :], None, io["edge_attr_256"][:, :],
                                                 bass.IndirectOffsetOnAxis(ap=edge_idx[u][:, j:j + 1], axis=0)).then_inc(ea_landed[u], 16)

            def gather_nodes(u):
                own_waits(nc.gpsimd, m)
                for j in range(G):
                    nc.gpsimd.indirect_dma_start(nf[u][:, j, :], None, m.node_table[:, :],
                                                 bass.IndirectOffsetOnAxis(ap=node_idx[u][:, j:j + 1], axis=0)).then_inc(nf_landed[u], 16)

            @block.gpsimd
            def _(pool):
                def edges_then_nodes(g, u, wait_summed):
                    pool.wait_ge(edge_idx_ready, g + (u + 1))
                    pool.wait_ge(turned, g + (u - 1))
                    gather_edges(u)
                    pool.wait_ge(node_idx_ready, g + u)
                    if wait_summed:
                        pool.wait_ge(summed, g + (u - 2))
                    gather_nodes(1 - u)

                for u in range(2):
                    pool.wait_ge(edge_idx_ready, u + 1)
                    gather_edges(u)
                pool.wait_ge(node_idx_ready, 1)
                gather_nodes(0)
                edges_then_nodes(2, 0, False)
                edges_then_nodes(2, 1, True)
                with pool.Fori(2, groups // 2) as turn:
                    for u in range(2):
                        edges_then_nodes(turn * 2, u, True)
                pool.wait_ge(node_idx_ready, groups)
                pool.wait_ge(summed, groups - 2)
                gather_nodes(1)

            def transposes(u, landed):
                pe = nc.tensor
                pe.wait_ge(ea_landed[u], landed)
                for j in range(G):
                    for k in range(KD):
                        last = pe.transpose(t_ps[:, k, j * P:(j + 1) * P], ea[u][:, j, k * P:(k + 1) * P], m.ident[:])
                last.then_inc(turned, 1)

            def hidden(u, g, first):
                pe = nc.tensor
                pe.wait_ge(turned_in, g + 1)
                for c in range(KH):
                    if not (first and c < 2):
                        pe.wait_ge(hid_ready, g * KH + (c - 1))
                    for k in range(KD):
                        last = pe.matmul(h_ps[:, c % 2, :], w1[:, k, c * P:(c + 1) * P], eat[u][:, k, :],
                                         start=k == 0, stop=k == KD - 1)
                    last.then_inc(hid_up, 1)

            def edges_out(u, g, first):
                pe = nc.tensor
                pe.wait_ge(hid_ready, g * KH + KH)
                if not first:
                    pe.wait_ge(summed, g)
                for j in range(G):
                    for k in range(KH):
                        last = pe.matmul(e_ps[:, j, :], hid[u][:, k, j * P:(j + 1) * P], w2[:, k, :],
                                         start=k == 0, stop=k == KH - 1)
                last.then_inc(e_up, 1)

            def scatter(u, g, first):
                pe = nc.tensor
                pe.wait_ge(msg_ready, g + 1)
                pe.wait_ge(hot_ready, g + 1)
                if not first:
                    pe.wait_ge(added, g * G)
                for j in range(G):
                    last = pe.matmul(s_ps[0:LANES, j, :], hot[u][:, j, :], msg[u][:, j, :], start=True, stop=True)
                last.then_inc(scattered, 1)

            @block.tensor
            def _(pe):
                pe.wait_ge(w_in, 48)
                transposes(0, 16 * G)
                hidden(0, 0, True)
                pe.wait_ge(turned_in, 1)
                transposes(1, 16 * G)
                edges_out(0, 0, True)
                hidden(1, 1, False)
                scatter(0, 0, True)
                pe.wait_ge(turned_in, 2)
                transposes(0, 2 * 16 * G)
                edges_out(1, 1, False)
                with pe.Fori(1, groups // 2 - 1) as turn:
                    g = turn * 2
                    for u in range(2):
                        hidden(u, g + u, False)
                        scatter(1 - u, g + (u - 1), False)
                        transposes(1 - u, (g + 2 * u) * (8 * G) + 16 * G)
                        edges_out(u, g + u, False)
                last = groups - 2
                hidden(0, last, False)
                scatter(1, last - 1, False)
                transposes(1, groups // 2 * 16 * G)
                edges_out(0, last, False)
                hidden(1, last + 1, False)
                scatter(0, last, False)
                edges_out(1, last + 1, False)
                scatter(1, last + 1, False)

            def hidden_relu(u, g):
                act = nc.scalar
                for c in range(KH):
                    act.wait_ge(hid_up, g * KH + (c + 1))
                    act.activation(hid[u][:, c, :], h_ps[:, c % 2, :], ACT.Relu, bias=b1[:, c:c + 1]).then_inc(hid_ready, 1)

            def message_relu(u, g):
                act = nc.scalar
                act.wait_ge(summed, g + 1)
                act.activation(msg[u][:], pre[u][:], ACT.Relu).then_inc(msg_ready, 1)

            @block.scalar
            def _(act):
                hidden_relu(0, 0)
                message_relu(0, 0)
                hidden_relu(1, 1)
                message_relu(1, 1)
                with act.Fori(1, groups // 2) as turn:
                    g = turn * 2
                    for u in range(2):
                        hidden_relu(u, g + u)
                        act.wait_ge(scattered, g + (u - 1))
                        message_relu(u, g + u)

            def stage_edge_idx(u, g):
                nc.vector.tensor_copy(edge_idx[u][:], m.edge_of_slot[:, bass.DynSlice(g * G, G)]).then_inc(edge_idx_ready, 1)

            def stage_node_idx(u, g):
                nc.vector.tensor_copy(node_idx[u][:], m.src_of_slot[:, bass.DynSlice(g * G, G)]).then_inc(node_idx_ready, 1)

            def one_hots(u, g):
                for j in range(G):
                    last = nc.vector.tensor_scalar(hot[u][:, j, :], m.count[:, 0:LANES],
                                                   m.dst_lane[:, bass.DynSlice(g * G + j, 1)], None, ALU.is_equal)
                last.then_inc(hot_ready, 1)

            def take_turned(u, g):
                nc.vector.wait_ge(turned, g + 1)
                nc.vector.tensor_copy(eat[u][:], t_ps[:]).then_inc(turned_in, 1)

            def add_nodes(u, g):
                nc.vector.wait_ge(e_up, g + 1)
                nc.vector.wait_ge(nf_landed[u], (g - u) * (8 * G) + 16 * G)
                nc.vector.tensor_tensor(pre[u][:], e_ps[:], nf[u][:], ALU.add).then_inc(summed, 1)

            def accumulate(g, first=False):
                dve = nc.vector
                tiles = [dve.value_load(m.dst_tile[0:1, bass.DynSlice(g * G + j, 1)], min_val=0, max_val=TILES - 1)
                         for j in range(G)]
                dve.wait_ge(scattered, g + 1)
                for j, tile in enumerate(tiles):
                    if not first or j > 0:
                        dve.wait_ge(added, g * G + j)
                    dve.tensor_tensor(m.acc[:, tile, :], s_ps[0:LANES, j, :], m.acc[:, tile, :], ALU.add).then_inc(added, 1)

            @block.vector
            def _(dve):
                zeroed = sem("edge_acc_zeroed")
                nc.vector.memset(m.acc[:], 0.0).then_inc(zeroed, 1)
                for u in range(2):
                    stage_edge_idx(u, u)
                    stage_node_idx(u, u)
                dve.wait_ge(zeroed, 1)
                take_turned(0, 0)
                stage_edge_idx(0, 2)

                def one_group(g, u, start=False, ahead=3):
                    if not start:
                        accumulate(g + (u - 2))
                    one_hots(u, g + u)
                    if ahead > 0:
                        take_turned(1 - u, g + (u + 1))
                    if ahead > 2:
                        stage_edge_idx(1 - u, g + (u + 3))
                    add_nodes(u, g + u)
                    if ahead > 1:
                        stage_node_idx(u, g + (u + 2))

                one_group(0, 0, start=True)
                one_group(0, 1, start=True)
                accumulate(0, first=True)
                one_group(2, 0, start=True)
                one_group(2, 1)
                with dve.Fori(2, groups // 2 - 2) as turn:
                    for u in range(2):
                        one_group(turn * 2, u)
                last = groups - 4
                one_group(last, 0)
                one_group(last, 1, ahead=2)
                one_group(last + 2, 0, ahead=1)
                one_group(last + 2, 1, ahead=0)
                for u in range(2):
                    accumulate(last + 2 + u)


def load_inputs(nc, sem, m, io):
    done = sem("load_done")
    with nc.Block() as block:

        @block.sync
        def _(sp):
            sp.dma_start(m.x[:], io["x"].rearrange("(p t) d -> p t d", t=TILES)).then_inc(done, 16)
            sp.dma_start(m.dst_i[:], io["dst"].rearrange("(p c) -> p c", c=EDGE_COLS)).then_inc(done, 16)
            sp.dma_start(m.src_i[:], io["src"].rearrange("(p c) -> p c", c=EDGE_COLS)).then_inc(done, 16)
            sp.dma_start(m.row_a[:, 0, :], io["be2"].partition_broadcast(LANES)).then_inc(done, 16)
            sp.dma_start(m.row_a[:, 1, :], io["bn2"].partition_broadcast(LANES)).then_inc(done, 16)
            sp.dma_start(m.eps[:], io["eps"].partition_broadcast(LANES)).then_inc(done, 16)
            sp.wait_ge(done, 96)


def node_table(nc, sem, m, name, y, rows, table, bias=None):
    ready = sem(name + "_ready")
    stored = sem(name + "_stored")
    with nc.Block() as block:

        @block.vector
        def _(dve):
            if bias is not None:
                nc.vector.tensor_tensor(rows[:], y[:], bias.unsqueeze(1).to_broadcast(list(y.shape)), ALU.add).then_inc(ready, 1)

        @block.sync
        def _(sp):
            if bias is not None:
                sp.wait_ge(ready, 1)
            sp.dma_start(table.rearrange("(p t) d -> p t d", t=TILES), rows[:] if bias is not None else y[:]).then_inc(stored, 16)
            sp.wait_ge(stored, 16)


def edge_tables(nc, sem, m, name, key_i, other_i, with_edge, out):
    keys = sem(name + "_keys")
    with ExitStack() as ctx:
        def sb(n, dt=F32):
            return ctx.enter_context(nc.sbuf_tensor(f"{name}_{n}", [LANES, EDGE_COLS], dt))

        lane = sb("lane")
        lane1 = sb("lane1")
        key = sb("key")
        bucket = sb("bucket")
        other = sb("other")
        pos = sb("pos")
        blk = sb("blk")
        lane_i = sb("lane_i", I32)
        at = sb("at")
        with nc.Block() as block:

            @block.vector
            def _(dve):
                chain = Chain(dve, keys)
                chain.link(nc.vector.tensor_copy(key[:], key_i[:]))
                chain.link(nc.vector.tensor_copy(other[:], other_i[:]))
                chain.link(nc.vector.tensor_scalar(lane_i[:], key[:], 1 / TILES, -(TILES - 1) / 2 / TILES, ALU.mult, ALU.add))
                chain.link(nc.vector.tensor_copy(lane[:], lane_i[:]))
                chain.link(nc.vector.scalar_tensor_tensor(bucket[:], lane[:], -float(TILES), key[:], ALU.mult, ALU.add))
                chain.link(nc.vector.tensor_scalar(lane1[:], lane[:], 1.0, None, ALU.add))
                chain.link(nc.vector.tensor_scalar(other[:], other[:], -float(NODE_MID), None, ALU.add))
                chain.link(nc.vector.tensor_scalar(at[:], m.count[0:LANES, 0:EDGE_COLS], 0.0, m.lane[0:LANES, :], ALU.mult, ALU.add))
        slots_of_buckets(nc, sem, m, name + "_sort", bucket[:], EDGE_COLS, TILES, EDGE_BLOCKS,
                         Slots(pos=pos[:], blk=blk[:], tile_row=out.tile_row))
        values = [other, lane1]
        if with_edge:
            values += [at, m.count[0:LANES, 0:EDGE_COLS]]
        column = ctx.enter_context(nc.sbuf_tensor(f"{name}_column", [P, EDGE_BLOCKS], F32))

        def finish(dve, chain, tables):
            chain.link(nc.vector.tensor_scalar(out.other, tables[:, 0, 0:EDGE_BLOCKS], float(NODE_MID), None, ALU.add))
            chain.link(nc.vector.tensor_scalar(out.lane, tables[:, 1, 0:EDGE_BLOCKS], -1.0, None, ALU.add))
            if with_edge:
                chain.link(nc.vector.tensor_copy(column[:], tables[:, 3, 0:EDGE_BLOCKS]))
                chain.link(nc.vector.scalar_tensor_tensor(out.edge, tables[:, 2, 0:EDGE_BLOCKS], float(EDGE_COLS), column[:],
                                                     ALU.mult, ALU.add))

        place_in_slots(nc, sem, m, name + "_place", pos, blk, values, EDGE_COLS, EDGE_BLOCKS, finish)


def node_mlp(nc, sem, m, io):
    w_in = sem("nmlp_weights_in")
    chain_s = sem("nmlp_dve")
    z_ready = sem("nmlp_z_ready")
    turned = sem("nmlp_turned")
    turned_in = sem("nmlp_turned_in")
    hid_up = sem("nmlp_hid_up")
    hid_ready = sem("nmlp_hid_ready")
    out_up = sem("nmlp_out_up")
    out_taken = sem("nmlp_out_taken")
    with ExitStack() as ctx:
        def sb(n, shape, dt=F32):
            return ctx.enter_context(nc.sbuf_tensor(f"nmlp_{n}", shape, dt))

        def ps(n, shape):
            return ctx.enter_context(nc.psum_tensor(f"nmlp_{n}", shape, F32))

        w1 = sb("w1", [P, KD, HID])
        b1 = sb("b1", [P, KH])
        w2 = sb("w2", [P, KH, DIM])
        eps1 = sb("eps1", [LANES, 1])
        z = sb("z", [LANES, CHUNK, DIM])
        zt = sb("zt", [P, KD, CW])
        hid = sb("hid", [P, KH, CW])
        t_ps = ps("t_ps", [P, KD, 512])
        h_ps = ps("h_ps", [P, KH, 512])
        o_ps = ps("o_ps", [P, CHUNK, DIM])
        with nc.Block() as block:

            @block.sync
            def _(sp):
                sp.dma_start(w1[:], io["Wn1"].rearrange("(k p) h -> p k h", p=P)).then_inc(w_in, 16)
                sp.dma_start(w2[:], io["Wn2"].rearrange("(k p) h -> p k h", p=P)).then_inc(w_in, 16)
                sp.dma_start(b1[:], io["bn1"]).then_inc(w_in, 16)

            @block.vector
            def _(dve):
                chain = Chain(dve, chain_s)
                chain.link(nc.vector.tensor_scalar(eps1[:], m.eps[:], 1.0, None, ALU.add))
                chain.link(nc.vector.tensor_tensor(m.x[:], m.x[:], m.row_a[:, 1, :].unsqueeze(1).to_broadcast([LANES, TILES, DIM]), ALU.add))
                with dve.Fori(0, CHUNKS) as c:
                    tiles = bass.DynSlice(c * CHUNK, CHUNK)
                    nc.vector.scalar_tensor_tensor(z[:], m.y[:, tiles, :], eps1[:, 0:1], m.acc[:, tiles, :],
                                                   ALU.mult, ALU.add).then_inc(z_ready, 1)
                    dve.wait_ge(turned, c + 1)
                    nc.vector.tensor_copy(zt[:], t_ps[:, :, 0:CW]).then_inc(turned_in, 1)
                    dve.wait_ge(out_up, c + 1)
                    nc.vector.tensor_tensor(m.x[:, tiles, :], m.x[:, tiles, :], o_ps[0:LANES, :, :], ALU.add).then_inc(out_taken, 1)

            @block.scalar
            def _(act):
                act.wait_ge(w_in, 48)
                with act.Fori(0, CHUNKS) as c:
                    for k in range(KH):
                        act.wait_ge(hid_up, c * KH + (k + 1))
                        nc.scalar.activation(hid[:, k, :], h_ps[:, k, 0:CW], ACT.Relu, bias=b1[:, k:k + 1]).then_inc(hid_ready, 1)

            @block.tensor
            def _(pe):
                pe.wait_ge(w_in, 48)
                with pe.Fori(0, CHUNKS) as c:
                    pe.wait_ge(z_ready, c + 1)
                    for t in range(CHUNK):
                        for k in range(KD):
                            last = nc.tensor.transpose(t_ps[:, k, t * LANES:(t + 1) * LANES], z[:, t, k * P:(k + 1) * P],
                                                       m.ident[0:LANES, 0:LANES])
                    last.then_inc(turned, 1)
                    pe.wait_ge(turned_in, c + 1)
                    for h in range(KH):
                        for k in range(KD):
                            last = nc.tensor.matmul(h_ps[:, h, 0:CW], w1[:, k, h * P:(h + 1) * P], zt[:, k, :],
                                                    start=k == 0, stop=k == KD - 1)
                        last.then_inc(hid_up, 1)
                    pe.wait_ge(hid_ready, c * KH + KH)
                    for t in range(CHUNK):
                        for k in range(KH):
                            last = nc.tensor.matmul(o_ps[0:LANES, t, :], hid[:, k, t * LANES:(t + 1) * LANES], w2[:, k, :],
                                                    start=k == 0, stop=k == KH - 1)
                    last.then_inc(out_up, 1)


class Routing:
    def __init__(self, sb):
        self.gate = sb("gate", [LANES, TOP, TILES])
        self.expert = sb("expert", [LANES, TOP, TILES])
        self.slot_i = sb("slot_i", [LANES, TOP, TILES], I32)
        self.node_of_slot = sb("node_of_slot", [P, MOE_BLOCKS], I32)
        self.block_expert = sb("block_expert", [1, MOE_BLOCKS], I32)


def moe_gates(nc, sem, m, io, r):
    in_ = sem("gate_in")
    staged = sem("gate_staged")
    turned = sem("gate_turned")
    turned_in = sem("gate_turned_in")
    up = sem("gate_up")
    taken = sem("gate_taken")
    logits_ready = sem("gate_logits_ready")
    exp_ready = sem("gate_exp_ready")
    chain_s = sem("gate_chain")
    with ExitStack() as ctx:
        def sb(n, shape, dt=F32):
            return ctx.enter_context(nc.sbuf_tensor(f"gate_{n}", shape, dt))

        w = sb("w", [P, KD, EXPERTS])
        b = sb("b", [LANES, EXPERTS])
        z = sb("z", [LANES, CHUNK, DIM])
        zt = sb("zt", [P, KD, CW])
        logits = sb("logits", [LANES, TILES, EXPERTS])
        top = sb("top", [LANES, TILES, 8])
        which = sb("which", [LANES, TILES, 8], mybir.dt.uint32)
        big = sb("big", [LANES, TILES])
        t_ps = ctx.enter_context(nc.psum_tensor("gate_t_ps", [P, KD, 512], F32))
        g_ps = ctx.enter_context(nc.psum_tensor("gate_g_ps", [P, CHUNK, EXPERTS], F32))
        wide = [LANES, TILES, EXPERTS]
        with nc.Block() as block:

            @block.sync
            def _(sp):
                sp.dma_start(w[:], io["gate_w"].rearrange("(k p) e -> p k e", p=P)).then_inc(in_, 16)
                sp.dma_start(b[:], io["gate_b"].partition_broadcast(LANES)).then_inc(in_, 16)

            @block.tensor
            def _(pe):
                pe.wait_ge(in_, 32)
                with pe.Fori(0, CHUNKS) as c:
                    pe.wait_ge(staged, c + 1)
                    for t in range(CHUNK):
                        for k in range(KD):
                            last = nc.tensor.transpose(t_ps[:, k, t * LANES:(t + 1) * LANES], z[:, t, k * P:(k + 1) * P],
                                                       m.ident[0:LANES, 0:LANES])
                    last.then_inc(turned, 1)
                    pe.wait_ge(turned_in, c + 1)
                    for t in range(CHUNK):
                        for k in range(KD):
                            last = nc.tensor.matmul(g_ps[0:LANES, t, :], zt[:, k, t * LANES:(t + 1) * LANES], w[:, k, :],
                                                    start=k == 0, stop=k == KD - 1)
                    last.then_inc(up, 1)

            @block.scalar
            def _(act):
                act.wait_ge(logits_ready, 1)
                nc.scalar.activation(logits[:], logits[:], ACT.Exp).then_inc(exp_ready, 1)

            @block.vector
            def _(dve):
                dve.wait_ge(in_, 32)
                with dve.Fori(0, CHUNKS) as c:
                    tiles = bass.DynSlice(c * CHUNK, CHUNK)
                    nc.vector.tensor_copy(z[:], m.y[:, tiles, :]).then_inc(staged, 1)
                    dve.wait_ge(turned, c + 1)
                    nc.vector.tensor_copy(zt[:], t_ps[:, :, 0:CW]).then_inc(turned_in, 1)
                    dve.wait_ge(up, c + 1)
                    nc.vector.tensor_tensor(logits[:, tiles, :], g_ps[0:LANES, :, :],
                                            b[:].unsqueeze(1).to_broadcast([LANES, CHUNK, EXPERTS]), ALU.add).then_inc(taken, 1)
                dve.wait_ge(taken, CHUNKS)
                chain = Chain(dve, chain_s)
                chain.link(nc.vector.tensor_reduce(big[:], logits[:], AX_X, ALU.max))
                nc.vector.tensor_tensor(logits[:], logits[:], big[:].unsqueeze(2).to_broadcast(wide), ALU.subtract).then_inc(logits_ready, 1)
                dve.wait_ge(exp_ready, 1)
                chain.link(nc.vector.tensor_reduce(big[:], logits[:], AX_X, ALU.add))
                chain.link(nc.vector.reciprocal(big[:], big[:]))
                chain.link(nc.vector.tensor_tensor(logits[:], logits[:], big[:].unsqueeze(2).to_broadcast(wide), ALU.mult))
                for t in range(TILES):
                    chain.link(nc.vector.max(top[:, t, :], logits[:, t, :]))
                for t in range(TILES):
                    last = nc.vector.max_index(which[:, t, :], top[:, t, :], logits[:, t, :])
                chain.link(last)
                chain.link(nc.vector.tensor_tensor(big[:], top[:, :, 0], top[:, :, 1], ALU.add))
                chain.link(nc.vector.reciprocal(big[:], big[:]))
                for k in range(TOP):
                    chain.link(nc.vector.tensor_tensor(r.gate[:, k, :], top[:, :, k], big[:], ALU.mult))
                    chain.link(nc.vector.tensor_copy(r.expert[:, k, :], which[:, :, k]))


def moe_experts(nc, sem, m, io, r):
    idx_ready = sem("moe_idx_ready")
    rows_in = [sem(f"moe_rows_in{u}") for u in range(2)]
    w_in = [sem(f"moe_w_in{u}") for u in range(2)]
    turned = sem("moe_turned")
    turned_in = sem("moe_turned_in")
    h_up = sem("moe_h_up")
    silu_ready = sem("moe_silu_ready")
    hid_ready = sem("moe_hid_ready")
    y_up = sem("moe_y_up")
    y_ready = sem("moe_y_ready")
    stored = [sem(f"moe_stored{u}") for u in range(2)]
    nb = MOE_BLOCKS
    with ExitStack() as ctx:
        def sb(n, shape, dt=F32):
            return [ctx.enter_context(nc.sbuf_tensor(f"moe_{n}{u}", shape, dt)) for u in range(2)]

        def ps(n, shape):
            return [ctx.enter_context(nc.psum_tensor(f"moe_{n}{u}", shape, F32)) for u in range(2)]

        idx = sb("idx", [P, 1], I32)
        rows = sb("rows", [P, DIM])
        xt = sb("xt", [P, KD, P])
        w1 = sb("w1", [P, KD, HID])
        w2 = sb("w2", [P, KD, HID])
        w3 = sb("w3", [P, KH, DIM])
        silu = sb("silu", [P, KH, P])
        hid = sb("hid", [P, KH, P])
        out = sb("out", [P, DIM])
        t_ps = ps("t_ps", [P, KD, 256])
        h1_ps = ps("h1_ps", [P, KH, P])
        h2_ps = ps("h2_ps", [P, KH, P])
        y_ps = ps("y_ps", [P, 512])
        turns = nb // 2
        with nc.Block() as block:

            @block.gpsimd
            def _(pool):
                def gather(u):
                    own_waits(nc.gpsimd, m)
                    nc.gpsimd.indirect_dma_start(rows[u][:], None, m.node_table[:, :],
                                                 bass.IndirectOffsetOnAxis(ap=idx[u][:, 0:1], axis=0)).then_inc(rows_in[u], 16)

                for u in range(2):
                    pool.wait_ge(idx_ready, u + 1)
                    gather(u)
                with pool.Fori(1, turns) as i:
                    for u in range(2):
                        pool.wait_ge(idx_ready, 2 * i + (u + 1))
                        pool.wait_ge(turned, 2 * i + (u - 1))
                        gather(u)

            @block.sync
            def _(sp):
                def load(b, u):
                    e = sp.value_load(r.block_expert[0:1, bass.DynSlice(b, 1)], min_val=0, max_val=EXPERTS - 1)
                    one = bass.DynSlice(e, 1)
                    sp.dma_start(w1[u][:], io["w1"][one, :, :].rearrange("a (k p) h -> p (a k) h", p=P)).then_inc(w_in[u], 16)
                    sp.dma_start(w2[u][:], io["w2"][one, :, :].rearrange("a (k p) h -> p (a k) h", p=P)).then_inc(w_in[u], 16)
                    sp.dma_start(w3[u][:], io["w3"][one, :, :].rearrange("a (k p) h -> p (a k) h", p=P)).then_inc(w_in[u], 16)

                def store(b, u):
                    sp.dma_start(m.routed[bass.DynSlice(b * P, P), :], out[u][:]).then_inc(stored[u], 16)

                for u in range(2):
                    load(u, u)
                with sp.Fori(1, turns) as i:
                    for u in range(2):
                        sp.wait_ge(y_up, 2 * i + (u - 1))
                        load(2 * i + u, u)
                        sp.wait_ge(y_ready, 2 * i + (u - 1))
                        store(2 * i + (u - 2), u)
                for u in range(2):
                    sp.wait_ge(y_ready, nb - 1 + u)
                    store(nb - 2 + u, u)
                for u in range(2):
                    sp.wait_ge(stored[u], turns * 16)

            @block.tensor
            def _(pe):
                def transposes(u, in_count):
                    pe.wait_ge(rows_in[u], in_count)
                    for k in range(KD):
                        last = nc.tensor.transpose(t_ps[u][:, k, 0:P], rows[u][:, k * P:(k + 1) * P], m.ident[:])
                    last.then_inc(turned, 1)

                def hidden(b, u, turn):
                    pe.wait_ge(turned_in, b + 1)
                    pe.wait_ge(w_in[u], (turn + 1) * 48)
                    for w, h_ps in ((w1[u], h1_ps[u]), (w2[u], h2_ps[u])):
                        for c in range(KH):
                            for k in range(KD):
                                last = nc.tensor.matmul(h_ps[:, c, :], w[:, k, c * P:(c + 1) * P], xt[u][:, k, :],
                                                        start=k == 0, stop=k == KD - 1)
                        last.then_inc(h_up, 1)

                def rows_out(b, u):
                    pe.wait_ge(hid_ready, b + 1)
                    if not isinstance(b, int) or b >= 2:
                        pe.wait_ge(y_ready, b - 1)
                    for k in range(KH):
                        last = nc.tensor.matmul(y_ps[u][:, 0:DIM], hid[u][:, k, :], w3[u][:, k, :], start=k == 0, stop=k == KH - 1)
                    last.then_inc(y_up, 1)

                for u in range(2):
                    transposes(u, 16)
                hidden(0, 0, 0)
                pe.wait_ge(turned_in, 2)
                transposes(0, 32)
                hidden(1, 1, 0)
                rows_out(0, 0)
                transposes(1, 32)
                hidden(2, 0, 1)
                rows_out(1, 1)
                transposes(0, 48)
                hidden(3, 1, 1)
                rows_out(2, 0)
                transposes(1, 48)
                with pe.Fori(2, turns - 1) as i:
                    for u in range(2):
                        hidden(2 * i + u, u, i)
                        rows_out(2 * i + (u - 1), 1 - u)
                        transposes(u, 16 * i + 32)
                hidden(nb - 2, 0, turns - 1)
                rows_out(nb - 3, 1)
                hidden(nb - 1, 1, turns - 1)
                rows_out(nb - 2, 0)
                rows_out(nb - 1, 1)

            @block.scalar
            def _(act):
                def silus(b, u):
                    act.wait_ge(h_up, 2 * b + 1)
                    if not isinstance(b, int) or b >= 2:
                        act.wait_ge(hid_ready, b - 1)
                    nc.scalar.activation(silu[u][:], h1_ps[u][:], ACT.Silu).then_inc(silu_ready, 1)

                def take_out(b, u, stores):
                    act.wait_ge(y_up, b + 1)
                    if stores is not None:
                        act.wait_ge(stored[u], stores)
                    nc.scalar.activation(out[u][:], y_ps[u][:, 0:DIM], ACT.Copy).then_inc(y_ready, 1)

                silus(0, 0)
                silus(1, 1)
                take_out(0, 0, None)
                silus(2, 0)
                take_out(1, 1, None)
                silus(3, 1)
                take_out(2, 0, 16)
                with act.Fori(2, turns) as i:
                    silus(2 * i, 0)
                    take_out(2 * i - 1, 1, 16 * i - 16)
                    silus(2 * i + 1, 1)
                    take_out(2 * i, 0, 16 * i)
                take_out(nb - 1, 1, 16 * (turns - 1))

            @block.vector
            def _(dve):
                def stage(b, u):
                    nc.vector.tensor_copy(idx[u][:], r.node_of_slot[:, bass.DynSlice(b, 1)]).then_inc(idx_ready, 1)

                def take_turned(b, u):
                    dve.wait_ge(turned, b + 1)
                    nc.vector.tensor_copy(xt[u][:], t_ps[u][:, :, 0:P]).then_inc(turned_in, 1)

                def multiply(b, u):
                    dve.wait_ge(silu_ready, b + 1)
                    dve.wait_ge(h_up, 2 * b + 2)
                    nc.vector.tensor_tensor(hid[u][:], silu[u][:], h2_ps[u][:], ALU.mult).then_inc(hid_ready, 1)

                for u in range(2):
                    stage(u, u)
                for u in range(2):
                    take_turned(u, u)
                    stage(u + 2, u)
                with dve.Fori(0, turns - 2) as i:
                    for u in range(2):
                        multiply(2 * i + u, u)
                        take_turned(2 * i + (u + 2), u)
                        stage(2 * i + (u + 4), u)
                for u in range(2):
                    multiply(nb - 4 + u, u)
                    take_turned(nb - 2 + u, u)
                for u in range(2):
                    multiply(nb - 2 + u, u)


def moe_combine(nc, sem, m, r):
    idx_ready = sem("comb_idx_ready")
    landed = [sem(f"comb_landed{u}") for u in range(4)]
    done = sem("comb_done")
    with ExitStack() as ctx:
        idx = [ctx.enter_context(nc.sbuf_tensor(f"comb_idx{u}", [LANES, 1], I32)) for u in range(4)]
        got = [ctx.enter_context(nc.sbuf_tensor(f"comb_got{u}", [LANES, DIM], F32)) for u in range(4)]
        with nc.Block() as block:

            @block.gpsimd
            def _(pool):
                def gather(u):
                    own_waits(nc.gpsimd, m)
                    nc.gpsimd.indirect_dma_start(got[u][:], None, m.routed[:, :],
                                                 bass.IndirectOffsetOnAxis(ap=idx[u][:, 0:1], axis=0)).then_inc(landed[u], 16)

                with pool.Fori(0, TILES // 2) as i:
                    for u in range(4):
                        pool.wait_ge(idx_ready, 4 * i + (u + 1))
                        gather(u)

            @block.vector
            def _(dve):
                def stage(i, u):
                    nc.vector.tensor_copy(idx[u][:], r.slot_i[:, u % 2, bass.DynSlice(2 * i + u // 2, 1)]).then_inc(idx_ready, 1)

                def take(i, u):
                    t = bass.DynSlice(2 * i + u // 2, 1)
                    dve.wait_ge(landed[u], 16 * i + 16)
                    if u % 2:
                        dve.wait_ge(done, 4 * i + u)
                    nc.vector.scalar_tensor_tensor(m.x[:, t, :], got[u][:].unsqueeze(1), r.gate[:, u % 2, t], m.x[:, t, :],
                                                   ALU.mult, ALU.add).then_inc(done, 1)

                for u in range(4):
                    stage(0, u)
                with dve.Fori(0, TILES // 2 - 1) as i:
                    for u in range(4):
                        take(i, u)
                        stage(i + 1, u)
                for u in range(4):
                    take(TILES // 2 - 1, u)


def mixture(nc, sem, m, io):
    items = TOP * TILES
    with ExitStack() as ctx:
        def sb(n, shape, dt=F32):
            return ctx.enter_context(nc.sbuf_tensor(f"mix_{n}", shape, dt))

        r = Routing(sb)
        pos = sb("pos", [LANES, items])
        blk = sb("blk", [LANES, items])
        node = sb("node", [LANES, items])
        layer_norm(nc, sem, m, "ln_b", m.x, m.y)
        node_table(nc, sem, m, "norm_table", m.y, None, m.node_table)
        moe_gates(nc, sem, m, io, r)
        slots_of_buckets(nc, sem, m, "mix_sort", r.expert[:].rearrange("p a t -> p (a t)"), items, EXPERTS, MOE_BLOCKS,
                         Slots(pos=pos[:], blk=blk[:], tile_row=r.block_expert[:]))
        steps = sem("mix_steps")
        with nc.Block() as block:

            @block.vector
            def _(dve):
                chain = Chain(dve, steps)
                for a in range(TOP):
                    chain.link(nc.vector.tensor_scalar(node[:, a * TILES:(a + 1) * TILES], m.node[:], -float(NODE_MID), None, ALU.add))
                chain.link(nc.vector.scalar_tensor_tensor(r.slot_i[:].rearrange("p a t -> p (a t)"), blk[:], float(P), pos[:], ALU.mult, ALU.add))

        def finish(dve, chain, tables):
            chain.link(nc.vector.tensor_scalar(r.node_of_slot[:], tables[:, 0, 0:MOE_BLOCKS], float(NODE_MID), None, ALU.add))

        place_in_slots(nc, sem, m, "mix_place", pos, blk, [node], items, MOE_BLOCKS, finish)
        moe_experts(nc, sem, m, io, r)
        moe_combine(nc, sem, m, r)


def attention_rows(nc, sem, m, io, sl):
    in_ = sem("hrow_in")
    staged = sem("hrow_staged")
    turned = sem("hrow_turned")
    turned_in = sem("hrow_turned_in")
    up = sem("hrow_up")
    chain_s = sem("hrow_chain")
    stored = sem("hrow_stored")
    with ExitStack() as ctx:
        def sb(n, shape, dt=F32):
            return ctx.enter_context(nc.sbuf_tensor(f"hrow_{n}", shape, dt))

        w = sb("w", [P, KD, HEADS * HEAD_C])
        a = sb("a", [LANES, 2, HEADS * HEAD_C])
        z = sb("z", [LANES, CHUNK, DIM])
        zt = sb("zt", [P, KD, CW])
        rows = sb("rows", [LANES, TILES, ROW])
        prod = sb("prod", [LANES, CHUNK, DIM])
        t_ps = ctx.enter_context(nc.psum_tensor("hrow_t_ps", [P, KD, 512], F32))
        h_ps = ctx.enter_context(nc.psum_tensor("hrow_h_ps", [P, CHUNK, DIM], F32))
        with nc.Block() as block:

            @block.sync
            def _(sp):
                for h, (wd, ad) in enumerate(((io["W1"], io["a1"]), (io["W2"], io["a2"]))):
                    part = slice(h * HEAD_C, (h + 1) * HEAD_C)
                    sp.dma_start(w[:, :, part], wd.rearrange("(k p) c -> p k c", p=P)).then_inc(in_, 16)
                    for side in range(2):
                        sp.dma_start(a[:, side, part], ad[0, side * HEAD_C:(side + 1) * HEAD_C].partition_broadcast(LANES)).then_inc(in_, 16)
                sp.wait_ge(chain_s, 5 * CHUNKS)
                sp.dma_start(m.head_table.rearrange("(p t) d -> p t d", t=TILES), rows[:]).then_inc(stored, 16)
                sp.wait_ge(stored, 16)

            @block.tensor
            def _(pe):
                pe.wait_ge(in_, 96)
                with pe.Fori(0, CHUNKS) as c:
                    pe.wait_ge(staged, c + 1)
                    for t in range(CHUNK):
                        for k in range(KD):
                            last = nc.tensor.transpose(t_ps[:, k, t * LANES:(t + 1) * LANES], z[:, t, k * P:(k + 1) * P],
                                                       m.ident[0:LANES, 0:LANES])
                    last.then_inc(turned, 1)
                    pe.wait_ge(turned_in, c + 1)
                    for t in range(CHUNK):
                        for k in range(KD):
                            last = nc.tensor.matmul(h_ps[0:LANES, t, :], zt[:, k, t * LANES:(t + 1) * LANES], w[:, k, :],
                                                    start=k == 0, stop=k == KD - 1)
                    last.then_inc(up, 1)

            @block.vector
            def _(dve):
                dve.wait_ge(in_, 96)
                with dve.Fori(0, CHUNKS) as c:
                    tiles = bass.DynSlice(c * CHUNK, CHUNK)
                    nc.vector.tensor_copy(z[:], m.y[:, tiles, :]).then_inc(staged, 1)
                    dve.wait_ge(turned, c + 1)
                    nc.vector.tensor_copy(zt[:], t_ps[:, :, 0:CW]).then_inc(turned_in, 1)
                    dve.wait_ge(up, c + 1)
                    nc.vector.tensor_copy(rows[:, tiles, 0:DIM], h_ps[0:LANES, :, :]).then_inc(chain_s, 1)
                    for side in range(2):
                        dve.wait_ge(chain_s, 5 * c + (1 + 2 * side))
                        nc.vector.tensor_tensor(prod[:], h_ps[0:LANES, :, :],
                                                a[:, side, :].unsqueeze(1).to_broadcast([LANES, CHUNK, DIM]), ALU.mult).then_inc(chain_s, 1)
                        dve.wait_ge(chain_s, 5 * c + (2 + 2 * side))
                        to = sl[:, tiles, :] if side == 0 else rows[:, tiles, DIM:ROW]
                        nc.vector.tensor_reduce(to, prod[:].rearrange("p t (h c) -> p t h c", h=HEADS), AX_X, ALU.add).then_inc(chain_s, 1)


def attend_edges(nc, sem, m, r, sl, acc):
    idx_ready = sem("att_idx_ready")
    landed = [sem(f"att_landed{u}") for u in range(2)]
    hot_ready = sem("att_hot_ready")
    turned = sem("att_turned")
    turned_in = sem("att_turned_in")
    sl_up = sem("att_sl_up")
    logit = sem("att_logit")
    lrelu_ready = sem("att_lrelu_ready")
    e_ready = sem("att_e_ready")
    scaled = sem("att_scaled")
    scattered = sem("att_scattered")
    added = sem("att_added")
    G = GROUP
    groups = EDGE_BLOCKS // G
    turns = groups // 2
    with ExitStack() as ctx:
        def sb(n, shape, dt=F32):
            return [ctx.enter_context(nc.sbuf_tensor(f"att_{n}{u}", shape, dt)) for u in range(2)]

        def ps(n, shape):
            return ctx.enter_context(nc.psum_tensor(f"att_{n}", shape, F32))

        idx = sb("idx", [P, G], I32)
        got = sb("got", [P, G, ROW])
        hot = sb("hot", [P, G, LANES])
        hot_t = sb("hot_t", [LANES, G, P])
        z = sb("z", [P, G, HEADS])
        lrelu = sb("lrelu", [P, G, HEADS])
        e = sb("e", [P, G, HEADS])
        w = sb("w", [P, G, ROW])
        t_ps = ps("t_ps", [P, G, P])
        sl_ps = ps("sl_ps", [P, 512])
        s_ps = ps("s_ps", [P, G, 512])
        with nc.Block() as block:

            @block.gpsimd
            def _(pool):
                def gather(u):
                    own_waits(nc.gpsimd, m)
                    for j in range(G):
                        nc.gpsimd.indirect_dma_start(got[u][:, j, :], None, m.head_table[:, :],
                                                     bass.IndirectOffsetOnAxis(ap=idx[u][:, j:j + 1], axis=0)).then_inc(landed[u], 16)

                for u in range(2):
                    pool.wait_ge(idx_ready, u + 1)
                    gather(u)
                with pool.Fori(1, turns) as i:
                    for u in range(2):
                        pool.wait_ge(idx_ready, 2 * i + (u + 1))
                        gather(u)

            @block.tensor
            def _(pe):
                def source_scores(g, u):
                    tiles = [pe.value_load(r.tile_row[0:1, bass.DynSlice(g * G + j, 1)], min_val=0, max_val=TILES - 1)
                             for j in range(G)]
                    pe.wait_ge(hot_ready, g + 1)
                    for j in range(G):
                        last = nc.tensor.transpose(t_ps[0:LANES, j, :], hot[u][:, j, :], m.ident[:])
                    last.then_inc(turned, 1)
                    pe.wait_ge(turned_in, g + 1)
                    for j, tile in enumerate(tiles):
                        last = nc.tensor.matmul(sl_ps[:, j * HEADS:(j + 1) * HEADS], hot_t[u][:, j, :], sl[:, tile, :],
                                                start=True, stop=True)
                    last.then_inc(sl_up, 1)

                def scatter(g, u, first=False):
                    pe.wait_ge(scaled, g + 1)
                    if not first:
                        pe.wait_ge(added, g * G)
                    for j in range(G):
                        last = nc.tensor.matmul(s_ps[0:LANES, j, 0:ROW], hot[u][:, j, :], w[u][:, j, :], start=True, stop=True)
                    last.then_inc(scattered, 1)

                source_scores(0, 0)
                pe.wait_ge(logit, 1)
                source_scores(1, 1)
                scatter(0, 0, True)
                with pe.Fori(1, turns) as i:
                    for u in range(2):
                        pe.wait_ge(logit, 2 * i + u)
                        source_scores(2 * i + u, u)
                        scatter(2 * i + (u - 1), 1 - u)
                scatter(groups - 1, 1)

            @block.scalar
            def _(act):
                def one_group(g, u):
                    act.wait_ge(turned, g + 1)
                    nc.scalar.activation(hot_t[u][:], t_ps[0:LANES, :, :], ACT.Copy).then_inc(turned_in, 1)
                    act.wait_ge(lrelu_ready, g + 1)
                    nc.scalar.activation(e[u][:], lrelu[u][:], ACT.Exp, scale=-1.0).then_inc(e_ready, 1)

                with act.Fori(0, turns) as i:
                    for u in range(2):
                        one_group(2 * i + u, u)

            @block.vector
            def _(dve):
                def stage_idx(g, u):
                    nc.vector.tensor_copy(idx[u][:], r.other[:, bass.DynSlice(g * G, G)]).then_inc(idx_ready, 1)

                def one_hots(g, u):
                    for j in range(G):
                        last = nc.vector.tensor_scalar(hot[u][:, j, :], m.count[:, 0:LANES],
                                                       r.lane[:, bass.DynSlice(g * G + j, 1)], None, ALU.is_equal)
                    last.then_inc(hot_ready, 1)

                def scale_rows(g, u):
                    dve.wait_ge(sl_up, g + 1)
                    dve.wait_ge(landed[u], (g - u) * (8 * G) + 16 * G)
                    nc.vector.tensor_tensor(z[u][:], sl_ps[:, 0:G * HEADS].rearrange("p (j h) -> p j h", h=HEADS),
                                            got[u][:, :, DIM:ROW], ALU.add).then_inc(logit, 1)
                    dve.wait_ge(logit, g + 1)
                    nc.vector.scalar_tensor_tensor(lrelu[u][:], z[u][:], NEG_SLOPE, z[u][:], ALU.mult, ALU.max).then_inc(lrelu_ready, 1)
                    dve.wait_ge(e_ready, g + 1)
                    nc.vector.tensor_tensor(w[u][:, :, 0:DIM].rearrange("p j (h c) -> p j h c", h=HEADS),
                                            got[u][:, :, 0:DIM].rearrange("p j (h c) -> p j h c", h=HEADS),
                                            e[u][:].unsqueeze(3).to_broadcast([P, G, HEADS, HEAD_C]), ALU.mult)
                    nc.vector.tensor_copy(w[u][:, :, DIM:ROW], e[u][:]).then_inc(scaled, 1)

                def accumulate(g, first=False):
                    tiles = [dve.value_load(r.tile_row[0:1, bass.DynSlice(g * G + j, 1)], min_val=0, max_val=TILES - 1)
                             for j in range(G)]
                    dve.wait_ge(scattered, g + 1)
                    for j, tile in enumerate(tiles):
                        if not first or j > 0:
                            dve.wait_ge(added, g * G + j)
                        dve.tensor_tensor(acc[:, tile, :], s_ps[0:LANES, j, 0:ROW], acc[:, tile, :], ALU.add).then_inc(added, 1)

                zeroed = sem("att_acc_zeroed")
                nc.vector.memset(acc[:], 0.0).then_inc(zeroed, 1)
                dve.wait_ge(zeroed, 1)
                for u in range(2):
                    stage_idx(u, u)
                    one_hots(u, u)
                scale_rows(0, 0)
                stage_idx(2, 0)
                scale_rows(1, 1)
                stage_idx(3, 1)
                accumulate(0, True)
                one_hots(2, 0)
                scale_rows(2, 0)
                stage_idx(4, 0)
                accumulate(1)
                one_hots(3, 1)
                scale_rows(3, 1)
                stage_idx(5, 1)
                with dve.Fori(2, turns - 1) as i:
                    for u in range(2):
                        accumulate(2 * i + (u - 2))
                        one_hots(2 * i + u, u)
                        scale_rows(2 * i + u, u)
                        stage_idx(2 * i + (u + 2), u)
                for u in range(2):
                    accumulate(groups - 4 + u)
                    one_hots(groups - 2 + u, u)
                    scale_rows(groups - 2 + u, u)
                for u in range(2):
                    accumulate(groups - 2 + u)


def attention_out(nc, sem, m, acc):
    chain_s = sem("atto_chain")
    low_ready = sem("atto_low_ready")
    exp_ready = sem("atto_exp_ready")
    with ExitStack() as ctx:
        def sb(n, shape, dt=F32):
            return ctx.enter_context(nc.sbuf_tensor(f"atto_{n}", shape, dt))

        inv = sb("inv", [LANES, TILES, HEADS])
        low = sb("low", [LANES, TILES, DIM])
        feats = acc[:, :, 0:DIM]
        by_head = [LANES, TILES, HEADS, HEAD_C]
        with nc.Block() as block:

            @block.scalar
            def _(act):
                act.wait_ge(low_ready, 1)
                nc.scalar.activation(low[:], low[:], ACT.Exp).then_inc(exp_ready, 1)

            @block.vector
            def _(dve):
                chain = Chain(dve, chain_s)
                chain.link(nc.vector.reciprocal(inv[:], acc[:, :, DIM:ROW]))
                chain.link(nc.vector.tensor_tensor(feats.rearrange("p t (h c) -> p t h c", h=HEADS),
                                              feats.rearrange("p t (h c) -> p t h c", h=HEADS),
                                              inv[:].unsqueeze(3).to_broadcast(by_head), ALU.mult))
                nc.vector.tensor_scalar(low[:], feats, 0.0, None, ALU.min).then_inc(low_ready, 1)
                chain.link(nc.vector.scalar_tensor_tensor(m.x[:], feats, 0.0, m.x[:], ALU.max, ALU.add))
                dve.wait_ge(exp_ready, 1)
                chain.link(nc.vector.scalar_tensor_tensor(m.x[:], low[:], -1.0, m.x[:], ALU.add, ALU.add))


def graph_attention(nc, sem, m, io):
    with ExitStack() as ctx:
        def sb(n, shape, dt=F32):
            return ctx.enter_context(nc.sbuf_tensor(f"gat_{n}", shape, dt))

        r = Ends(sb("other", [P, EDGE_BLOCKS], I32), sb("lane", [P, EDGE_BLOCKS]), sb("tile_row", [1, EDGE_BLOCKS], I32))
        sl = sb("sl", [LANES, TILES, HEADS])
        edge_tables(nc, sem, m, "by_src", m.src_i, m.dst_i, False,
                    Ends(r.other[:], r.lane[:], r.tile_row[:]))
        layer_norm(nc, sem, m, "ln_c", m.x, m.y)
        attention_rows(nc, sem, m, io, sl)
        acc = sb("acc", [LANES, TILES, ROW])
        attend_edges(nc, sem, m, r, sl, acc)
        attention_out(nc, sem, m, acc)


class SliceState:
    def __init__(self, sb):
        self.weights = sb("weights", [LANES, TILES, INNER])
        self.mixed = sb("mixed", [P, PAIRS, DIM])
        self.b_out = sb("b_out", [LANES, DIM])
        self.tokens = sb("tokens", [P, PAIRS, P])
        self.norm = sb("norm", [P, PAIRS])


def slice_attention(nc, sem, m, io):
    with ExitStack() as ctx:
        def sb(n, shape, dt=F32):
            return ctx.enter_context(nc.sbuf_tensor(f"sa_{n}", shape, dt))

        layer_norm(nc, sem, m, "ln_d", m.x, m.y)
        s = SliceState(sb)
        slice_tokens(nc, sem, m, io, s)
        token_attention(nc, sem, m, io, s)
        slices_out(nc, sem, m, io, s)


def slice_tokens(nc, sem, m, io, s):
    in_ = sem("st_in")
    consts = sem("st_consts")
    staged = sem("st_staged")
    turned = sem("st_turned")
    turned_in = sem("st_turned_in")
    xm_up = sem("st_xm_up")
    xm_ready = sem("st_xm_ready")
    logits_up = sem("st_logits_up")
    chain_s = sem("st_chain")
    shifted = sem("st_shifted")
    exp_ready = sem("st_exp_ready")
    fx_up = sem("st_fx_up")
    fx_ready = sem("st_fx_ready")
    w_ready = sem("st_w_ready")
    summed = sem("st_summed")
    taken = sem("st_taken")
    with ExitStack() as ctx:
        def sb(n, shape, dt=F32):
            return ctx.enter_context(nc.sbuf_tensor(f"st_{n}", shape, dt))

        def ps(n, shape):
            return ctx.enter_context(nc.psum_tensor(f"st_{n}", shape, F32))

        wx = sb("wx", [P, KD, INNER])
        wf = sb("wf", [P, KD, INNER])
        bx = sb("bx", [P, PAIRS])
        bf = sb("bf", [LANES, INNER])
        ws = sb("ws", [P, P])
        bs = sb("bs", [LANES, SLICES])
        temp = sb("temp", [LANES, SA_HEADS])
        z = sb("z", [LANES, CHUNK, DIM])
        zt = sb("zt", [P, KD, CW])
        xm = sb("xm", [P, PAIRS, CW])
        fx = sb("fx", [LANES, INNER])
        lg = sb("lg", [LANES, INNER])
        w = sb("w", [LANES, INNER])
        big = sb("big", [LANES, SA_HEADS])
        total = sb("total", [LANES, SA_HEADS])
        ab_ps = ps("ab_ps", [P, 2, 512])
        lg_ps = ps("lg_ps", [P, 512])
        fx_ps = ps("fx_ps", [P, 512])
        tok_ps = ps("tok_ps", [P, PAIRS, 512])
        heads = [LANES, SA_HEADS, SLICES]

        def by_head(ap):
            return ap.rearrange("p (h g) -> p h g", h=SA_HEADS)

        with nc.Block() as block:

            @block.sync
            def _(sp):
                sp.wait_ge(consts, 1)
                sp.dma_start(wx[:], io["W_x"].rearrange("(k p) i -> p k i", p=P)).then_inc(in_, 16)
                sp.dma_start(wf[:], io["W_fx"].rearrange("(k p) i -> p k i", p=P)).then_inc(in_, 16)
                sp.dma_start(bx[:], io["b_x"]).then_inc(in_, 16)
                sp.dma_start(bf[:], io["b_fx"].partition_broadcast(LANES)).then_inc(in_, 16)
                for h in range(2):
                    part = slice(h * SA_D, (h + 1) * SA_D)
                    sp.dma_start(ws[part, part], io["W_slice"]).then_inc(in_, 16)
                sp.dma_start(bs[:], io["b_slice"].partition_broadcast(LANES)).then_inc(in_, 16)
                sp.dma_start(temp[:], io["temperature"].rearrange("a h b c -> (a h b c)").partition_broadcast(LANES)).then_inc(in_, 16)
                sp.dma_start(s.b_out[:], io["b_out"].partition_broadcast(LANES)).then_inc(in_, 16)

            @block.gpsimd
            def _(pool):
                nc.gpsimd.memset(ws[:], 0.0).then_inc(consts, 1)

            @block.tensor
            def _(pe):
                pe.wait_ge(in_, 144)
                with pe.Fori(0, CHUNKS) as c:
                    pe.wait_ge(staged, c + 1)
                    for t in range(CHUNK):
                        for k in range(KD):
                            last = nc.tensor.transpose(ab_ps[:, k, t * LANES:(t + 1) * LANES], z[:, t, k * P:(k + 1) * P],
                                                       m.ident[0:LANES, 0:LANES])
                    last.then_inc(turned, 1)
                    pe.wait_ge(turned_in, c + 1)
                    for p in range(PAIRS):
                        if p >= 2:
                            pe.wait_ge(xm_ready, c * PAIRS + (p - 1))
                        for k in range(KD):
                            last = nc.tensor.matmul(ab_ps[:, p % 2, 0:CW], wx[:, k, p * P:(p + 1) * P], zt[:, k, :],
                                                    start=k == 0, stop=k == KD - 1)
                        last.then_inc(xm_up, 1)
                    pe.wait_ge(xm_ready, c * PAIRS + PAIRS)
                    for t in range(CHUNK):
                        nodes = slice(t * LANES, (t + 1) * LANES)
                        for p in range(PAIRS):
                            last = nc.tensor.matmul(lg_ps[0:LANES, p * P:(p + 1) * P], xm[:, p, nodes], ws[:], start=True, stop=True)
                        last.then_inc(logits_up, 1)
                        for k in range(KD):
                            last = nc.tensor.matmul(fx_ps[0:LANES, :], zt[:, k, nodes], wf[:, k, :], start=k == 0, stop=k == KD - 1)
                        last.then_inc(fx_up, 1)
                        pe.wait_ge(fx_ready, c * CHUNK + (t + 1))
                        pe.wait_ge(w_ready, c * CHUNK + (t + 1))
                        for p in range(PAIRS):
                            part = slice(p * P, (p + 1) * P)
                            nc.tensor.matmul(tok_ps[:, p, 0:P], w[:, part], fx[:, part], start=True, stop=True)
                            last = nc.tensor.matmul(tok_ps[:, p, P:P + 1], w[:, part], m.ones[0:LANES, 0:1], start=True, stop=True)
                        last.then_inc(summed, 1)
                        pe.wait_ge(taken, 2 * (c * CHUNK + t) + 2)

            @block.scalar
            def _(act):
                act.wait_ge(in_, 144)
                with act.Fori(0, CHUNKS) as c:
                    for p in range(PAIRS):
                        act.wait_ge(xm_up, c * PAIRS + (p + 1))
                        nc.scalar.activation(xm[:, p, :], ab_ps[:, p % 2, 0:CW], ACT.Identity, bias=bx[:, p:p + 1]).then_inc(xm_ready, 1)
                    for t in range(CHUNK):
                        act.wait_ge(shifted, c * CHUNK + (t + 1))
                        nc.scalar.activation(lg[:], lg[:], ACT.Exp).then_inc(exp_ready, 1)

            @block.vector
            def _(dve):
                dve.wait_ge(in_, 144)
                setup = Chain(dve, sem("st_setup"))
                setup.link(nc.vector.memset(s.tokens[:], 0.0))
                setup.link(nc.vector.memset(s.norm[:], 0.0))
                setup.link(nc.vector.tensor_scalar(temp[:], temp[:], 0.1, 5.0, ALU.max, ALU.min))
                setup.link(nc.vector.reciprocal(temp[:], temp[:]))
                with dve.Fori(0, CHUNKS) as c:
                    nc.vector.tensor_copy(z[:], m.y[:, bass.DynSlice(c * CHUNK, CHUNK), :]).then_inc(staged, 1)
                    dve.wait_ge(turned, c + 1)
                    nc.vector.tensor_copy(zt[:], ab_ps[:, :, 0:CW]).then_inc(turned_in, 1)
                    for t in range(CHUNK):
                        tile = c * CHUNK + t
                        steps = [6 * tile + n for n in range(1, 7)]
                        dve.wait_ge(logits_up, tile + 1)
                        nc.vector.tensor_tensor(by_head(lg[:]), by_head(lg_ps[0:LANES, :]),
                                                bs[:].unsqueeze(1).to_broadcast(heads), ALU.add).then_inc(chain_s, 1)
                        dve.wait_ge(chain_s, steps[0])
                        nc.vector.tensor_tensor(by_head(lg[:]), by_head(lg[:]), temp[:].unsqueeze(2).to_broadcast(heads),
                                                ALU.mult).then_inc(chain_s, 1)
                        dve.wait_ge(chain_s, steps[1])
                        nc.vector.tensor_reduce(big[:], by_head(lg[:]), AX_X, ALU.max).then_inc(chain_s, 1)
                        dve.wait_ge(chain_s, steps[2])
                        nc.vector.tensor_tensor(by_head(lg[:]), by_head(lg[:]), big[:].unsqueeze(2).to_broadcast(heads),
                                                ALU.subtract).then_inc(shifted, 1)
                        dve.wait_ge(fx_up, tile + 1)
                        nc.vector.tensor_tensor(fx[:], fx_ps[0:LANES, :], bf[:], ALU.add).then_inc(fx_ready, 1)
                        dve.wait_ge(exp_ready, tile + 1)
                        nc.vector.tensor_reduce(total[:], by_head(lg[:]), AX_X, ALU.add).then_inc(chain_s, 1)
                        dve.wait_ge(chain_s, steps[3])
                        nc.vector.reciprocal(total[:], total[:]).then_inc(chain_s, 1)
                        dve.wait_ge(chain_s, steps[4])
                        nc.vector.tensor_tensor(by_head(w[:]), by_head(lg[:]), total[:].unsqueeze(2).to_broadcast(heads),
                                                ALU.mult).then_inc(w_ready, 1)
                        dve.wait_ge(w_ready, tile + 1)
                        nc.vector.tensor_copy(s.weights[:, bass.DynSlice(tile, 1), :], w[:].unsqueeze(1)).then_inc(chain_s, 1)
                        dve.wait_ge(summed, tile + 1)
                        nc.vector.tensor_tensor(s.tokens[:], tok_ps[:, :, 0:P], s.tokens[:], ALU.add).then_inc(taken, 1)
                        nc.vector.tensor_tensor(s.norm[:], tok_ps[:, :, P], s.norm[:], ALU.add).then_inc(taken, 1)


def token_attention(nc, sem, m, io, s):
    in_ = sem("ta_in")
    consts = sem("ta_consts")
    chain_s = sem("ta_dve")
    tok_ready = sem("ta_tok_ready")
    pe_up = sem("ta_pe_up")
    taken = sem("ta_taken")
    exp_in = sem("ta_exp_in")
    exp_ready = sem("ta_exp_ready")
    with ExitStack() as ctx:
        def sb(n, shape, dt=F32):
            return ctx.enter_context(nc.sbuf_tensor(f"ta_{n}", shape, dt))

        wq, wk, wv = (sb(n, [P, P]) for n in ("wq", "wk", "wv"))
        wo = sb("wo", [P, PAIRS, DIM])
        inv = sb("inv", [P, PAIRS])
        tok = sb("tok", [P, PAIRS, P])
        tok_t = sb("tok_t", [P, PAIRS, P])
        q_t = sb("q_t", [P, PAIRS, P])
        k_t = sb("k_t", [P, PAIRS, P])
        v = sb("v", [P, PAIRS, P])
        at = sb("at", [P, PAIRS, P])
        at_t = sb("at_t", [P, PAIRS, P])
        mix_t = sb("mix_t", [P, PAIRS, P])
        big = sb("big", [P, PAIRS])
        total = sb("total", [P, PAIRS])
        ps = [ctx.enter_context(nc.psum_tensor(f"ta_ps{n}", [P, PAIRS, P], F32)) for n in range(4)]
        mo_ps = ctx.enter_context(nc.psum_tensor("ta_mo_ps", [P, PAIRS, DIM], F32))
        halves = [slice(0, SA_D), slice(SA_D, P)]
        with nc.Block() as block:

            @block.sync
            def _(sp):
                sp.wait_ge(consts, 3)
                for w, wd in ((wq, io["W_q"]), (wk, io["W_k"]), (wv, io["W_v"])):
                    for part in halves:
                        sp.dma_start(w[part, part], wd).then_inc(in_, 16)
                sp.dma_start(wo[:], io["W_out"].rearrange("(k p) d -> p k d", p=P)).then_inc(in_, 16)

            @block.gpsimd
            def _(pool):
                for w in (wq, wk, wv):
                    nc.gpsimd.memset(w[:], 0.0).then_inc(consts, 1)

            @block.tensor
            def _(pe):
                pe.wait_ge(in_, 112)

                def pairwise(to, left, right, transpose=False):
                    for p in range(PAIRS):
                        if transpose:
                            last = nc.tensor.transpose(to[:, p, :], left(p), m.ident[:])
                        else:
                            last = nc.tensor.matmul(to[:, p, :], left(p), right(p), start=True, stop=True)
                    last.then_inc(pe_up, 1)

                pe.wait_ge(tok_ready, 1)
                pairwise(ps[0], lambda p: tok[:, p, :], None, True)
                pe.wait_ge(taken, 1)
                pairwise(ps[1], lambda p: wq[:], lambda p: tok_t[:, p, :])
                pairwise(ps[2], lambda p: wk[:], lambda p: tok_t[:, p, :])
                pairwise(ps[3], lambda p: tok_t[:, p, :], lambda p: wv[:])
                pe.wait_ge(taken, 3)
                pairwise(ps[0], lambda p: q_t[:, p, :], lambda p: k_t[:, p, :])
                pe.wait_ge(taken, 5)
                pairwise(ps[1], lambda p: at[:, p, :], None, True)
                pe.wait_ge(taken, 6)
                pairwise(ps[2], lambda p: v[:, p, :], lambda p: at_t[:, p, :])
                pe.wait_ge(taken, 7)
                for p in range(PAIRS):
                    last = nc.tensor.matmul(mo_ps[:, p, :], mix_t[:, p, :], wo[:, p, :], start=True, stop=True)
                last.then_inc(pe_up, 1)

            @block.scalar
            def _(act):
                act.wait_ge(exp_in, 1)
                for part in halves:
                    last = nc.scalar.activation(at[part, :, part], at[part, :, part], ACT.Exp)
                last.then_inc(exp_ready, 1)

            @block.vector
            def _(dve):
                chain = Chain(dve, chain_s)
                chain.link(nc.vector.tensor_scalar(inv[:], s.norm[:], 1e-5, None, ALU.add))
                chain.link(nc.vector.reciprocal(inv[:], inv[:]))
                chain.link(nc.vector.memset(tok[:], 0.0))
                chain.link(nc.vector.memset(at[:], 0.0))
                for part in halves:
                    chain.link(nc.vector.tensor_tensor(tok[part, :, part], s.tokens[part, :, part],
                                                  inv[part, :].unsqueeze(2).to_broadcast([SA_D, PAIRS, SA_D]), ALU.mult))
                nc.vector.memset(total[:], 0.0).then_inc(tok_ready, 1)
                for n, (to, src) in enumerate(((tok_t, ps[0]), (q_t, ps[1]), (k_t, ps[2]), (v, ps[3]))):
                    dve.wait_ge(pe_up, n + 1)
                    nc.vector.tensor_copy(to[:], src[:]).then_inc(taken, 1)
                dve.wait_ge(pe_up, 5)
                for part in halves:
                    wide = [SA_D, PAIRS, SA_D]
                    chain.link(nc.vector.tensor_scalar(at[part, :, part], ps[0][part, :, part], SA_D ** -0.5, None, ALU.mult))
                    chain.link(nc.vector.tensor_reduce(big[part, :], at[part, :, part], AX_X, ALU.max))
                    last = nc.vector.tensor_tensor(at[part, :, part], at[part, :, part], big[part, :].unsqueeze(2).to_broadcast(wide),
                                                   ALU.subtract)
                last.then_inc(exp_in, 1)
                dve.wait_ge(exp_ready, 1)
                for part in halves:
                    chain.link(nc.vector.tensor_reduce(total[part, :], at[part, :, part], AX_X, ALU.add))
                chain.link(nc.vector.reciprocal(total[:], total[:]))
                nc.vector.tensor_tensor(at[:], at[:], total[:].unsqueeze(2).to_broadcast([P, PAIRS, P]), ALU.mult).then_inc(taken, 1)
                dve.wait_ge(pe_up, 6)
                nc.vector.tensor_copy(at_t[:], ps[1][:]).then_inc(taken, 1)
                dve.wait_ge(pe_up, 7)
                nc.vector.tensor_copy(mix_t[:], ps[2][:]).then_inc(taken, 1)
                dve.wait_ge(pe_up, 8)
                nc.vector.tensor_copy(s.mixed[:], mo_ps[:]).then_inc(taken, 1)


def slices_out(nc, sem, m, io, s):
    staged = sem("so_staged")
    turned = sem("so_turned")
    turned_in = sem("so_turned_in")
    up = sem("so_up")
    taken = sem("so_taken")
    biased = sem("so_biased")
    with ExitStack() as ctx:
        w = [ctx.enter_context(nc.sbuf_tensor(f"so_w{u}", [LANES, INNER], F32)) for u in range(2)]
        w_t = [ctx.enter_context(nc.sbuf_tensor(f"so_w_t{u}", [P, PAIRS, P], F32)) for u in range(2)]
        t_ps = [ctx.enter_context(nc.psum_tensor(f"so_t_ps{u}", [P, PAIRS, P], F32)) for u in range(2)]
        o_ps = [ctx.enter_context(nc.psum_tensor(f"so_o_ps{u}", [P, 512], F32)) for u in range(2)]
        turns = TILES // 2
        with nc.Block() as block:

            @block.tensor
            def _(pe):
                with pe.Fori(0, turns) as i:
                    for u in range(2):
                        pe.wait_ge(staged, 2 * i + (u + 1))
                        for p in range(PAIRS):
                            last = nc.tensor.transpose(t_ps[u][:, p, 0:LANES], w[u][:, p * P:(p + 1) * P], m.ident[0:LANES, 0:LANES])
                        last.then_inc(turned, 1)
                    for u in range(2):
                        pe.wait_ge(turned_in, 2 * i + (u + 1))
                        for p in range(PAIRS):
                            last = nc.tensor.matmul(o_ps[u][0:LANES, 0:DIM], w_t[u][:, p, 0:LANES], s.mixed[:, p, :],
                                                    start=p == 0, stop=p == PAIRS - 1)
                        last.then_inc(up, 1)

            @block.scalar
            def _(act):
                with act.Fori(0, turns) as i:
                    for u in range(2):
                        act.wait_ge(turned, 2 * i + (u + 1))
                        nc.scalar.activation(w_t[u][:, :, 0:LANES], t_ps[u][:, :, 0:LANES], ACT.Copy).then_inc(turned_in, 1)

            @block.vector
            def _(dve):
                nc.vector.tensor_tensor(m.x[:], m.x[:], s.b_out[:].unsqueeze(1).to_broadcast([LANES, TILES, DIM]), ALU.add).then_inc(biased, 1)
                dve.wait_ge(biased, 1)

                def stage(t, u):
                    nc.vector.tensor_copy(w[u][:].unsqueeze(1), s.weights[:, bass.DynSlice(t, 1), :]).then_inc(staged, 1)

                def take(t, u):
                    one = bass.DynSlice(t, 1)
                    dve.wait_ge(up, t + 1)
                    nc.vector.tensor_tensor(m.x[:, one, :], o_ps[u][0:LANES, 0:DIM].unsqueeze(1), m.x[:, one, :], ALU.add).then_inc(taken, 1)

                for u in range(2):
                    stage(u, u)
                with dve.Fori(0, turns - 1) as i:
                    for u in range(2):
                        take(2 * i + u, u)
                        stage(2 * i + (u + 2), u)
                for u in range(2):
                    take(TILES - 2 + u, u)


def gather_and_update(nc, sem, m, io):
    with ExitStack() as ctx:
        def sb(n, shape, dt=F32):
            return ctx.enter_context(nc.sbuf_tensor(f"gine_{n}", shape, dt))

        m.edge_of_slot = sb("edge_of_slot", [P, EDGE_BLOCKS], I32)
        m.src_of_slot = sb("src_of_slot", [P, EDGE_BLOCKS], I32)
        m.dst_lane = sb("dst_lane", [P, EDGE_BLOCKS])
        m.dst_tile = sb("dst_tile", [1, EDGE_BLOCKS], I32)
        edge_tables(nc, sem, m, "by_dst", m.dst_i, m.src_i, True,
                    Ends(m.src_of_slot[:], m.dst_lane[:], m.dst_tile[:], edge=m.edge_of_slot[:]))
        m.acc = sb("acc", [LANES, TILES, DIM])
        layer_norm(nc, sem, m, "ln_a", m.x, m.y)
        node_table(nc, sem, m, "biased_table", m.y, m.acc, m.node_table, m.row_a[:, 0, :])
        edge_messages(nc, sem, m, io)
        node_mlp(nc, sem, m, io)


def store_output(nc, sem, m, out):
    stored = sem("out_stored")
    with nc.Block() as block:

        @block.sync
        def _(sp):
            sp.dma_start(out.rearrange("(p t) d -> p t d", t=TILES), m.x[:]).then_inc(stored, 16)
            sp.wait_ge(stored, 16)


def gnn_moe_gat_slice_kernel(nc, io_gine, io_moe, io_gat, io_slice, out):
    with ExitStack() as ctx:
        def sb(n, shape, dt=F32):
            return ctx.enter_context(nc.sbuf_tensor(n, shape, dt))

        def sem(n):
            return ctx.enter_context(nc.semaphore(n))

        m = Shared(nc, sb, sem)
        constants(nc, m, sem)
        load_inputs(nc, sem, m, io_gine)
        gather_and_update(nc, sem, m, io_gine)
        mixture(nc, sem, m, io_moe)
        graph_attention(nc, sem, m, io_gat)
        slice_attention(nc, sem, m, io_slice)
        store_output(nc, sem, m, out)


GINE = ["x", "src", "dst", "edge_attr_256"] + ["L0_gnn_" + n for n in
                                               ("We1", "be1", "We2", "be2", "Wn1", "bn1", "Wn2", "bn2", "eps")]
MOE = ["L0_ffn_" + n for n in ("gate_w", "gate_b", "w1", "w2", "w3")]
GAT = ["L1_gnn_" + n for n in ("W1", "a1", "W2", "a2")]
SLICE = ["L1_ffn_" + n for n in ("W_fx", "b_fx", "W_x", "b_x", "W_slice", "b_slice", "W_q", "W_k", "W_v", "W_out", "b_out",
                                 "temperature")]
BY_PARTITION = ("L0_gnn_be1", "L0_gnn_bn1", "L1_ffn_b_x")


def kernel(**inputs):
    import numpy as _np
    import concourse.bacc as _bacc
    from concourse import mybir as _mybir
    from concourse.bass_utils import run_bass_kernel_spmd as _run

    nc = _bacc.Bacc("TRN2", target_bir_lowering=False, num_devices=1)
    arrays, ios = {}, []
    for names in (GINE, MOE, GAT, SLICE):
        io = {}
        for name in names:
            a = _np.asarray(inputs[name])
            if name in BY_PARTITION:
                a = a.reshape(-1, P).T
            a = _np.ascontiguousarray(a)
            arrays[f"in_{name}_dram"] = a
            io[name.split("_", 2)[2] if name[0] == "L" else name] = nc.dram_tensor(
                f"in_{name}_dram", a.shape, _mybir.dt.from_np(a.dtype), kind="ExternalInput").ap()
        ios.append(io)
    out = nc.dram_tensor("out_0_dram", (N_NODES, DIM), F32, kind="ExternalOutput").ap()
    gnn_moe_gat_slice_kernel(nc, *ios, out)
    r = _run(nc, [arrays], core_ids=[0])
    return r.results[0]["out_0_dram"]
```

```python
from contextlib import ExitStack

import concourse.bass as bass
from concourse import mybir

F32 = mybir.dt.float32
F16 = mybir.dt.float16
BF16 = mybir.dt.bfloat16
I32 = mybir.dt.int32
ALU = mybir.AluOpType
ACT = mybir.ActivationFunctionType
AX_X = mybir.AxisListType.X

N_NODES, DIM = 2500, 256
N_EDGES = 40000
P = 128
LANES = 125
TILES = N_NODES // LANES
EDGE_COLS = N_EDGES // LANES
KD = DIM // P
HID = 2 * DIM
KH = HID // P
LN_EPS = 1e-5

EXPERTS, TOP = 16, 2
GROUP = 4
EDGE_BLOCKS = -(-((N_EDGES + TILES * (P - 1)) // P) // (2 * GROUP)) * 2 * GROUP
PAIR = 2 * P
PAIR_BLOCKS = -(-((N_EDGES + TILES * (PAIR - 1)) // PAIR * 2) // (2 * GROUP)) * 2 * GROUP
MOE_BLOCKS = -(-((N_NODES * TOP + EXPERTS * (P - 1)) // P) // 6) * 6
NODE_MID = N_NODES // 2

HEADS, HEAD_C = 2, 128
NEG_SLOPE = 0.2
ROW = HEADS * (HEAD_C + 1)
SA_HEADS, SA_D, SLICES = 8, 64, 64
INNER = SA_HEADS * SA_D
PAIRS = INNER // P
CHUNK = 4
CHUNKS = TILES // CHUNK
CW = CHUNK * LANES


class Slots:

    def __init__(self, pos, blk, tile_row):
        self.pos, self.blk, self.tile_row = pos, blk, tile_row


class Ends:

    def __init__(self, other, lane, tile_row, edge=None):
        self.other, self.lane, self.tile_row, self.edge = other, lane, tile_row, edge


class Chain:

    def __init__(self, eng, sem):
        self.eng, self.sem, self.n = eng, sem, 0

    def link(self, ins):
        self.n += 1
        ins.then_inc(self.sem, 1)
        self.eng.wait_ge(self.sem, self.n)


class Shared:

    def __init__(self, nc, sb, sem):
        self.constants_made = sem("constants_made")
        self.gathers_begun = sem("gathers_begun")
        self.steps = Chain(nc.vector, sem("vector_steps"))
        self.ident = sb("ident", [P, P])
        self.before = sb("before", [P, P])
        self.ones = sb("ones", [P, P])
        self.count_i = sb("count_i", [P, PAIR_BLOCKS], I32)
        self.count = sb("count", [P, PAIR_BLOCKS])
        self.count16 = sb("count16", [P, PAIR_BLOCKS], F16)
        self.ident16 = sb("ident16", [P, P], BF16)
        self.lane_i = sb("lane_i", [P, 1], I32)
        self.lane = sb("lane", [P, 1])
        self.node_i = sb("node_i", [LANES, TILES], I32)
        self.node = sb("node", [LANES, TILES])
        self.x = sb("x", [LANES, TILES, DIM])
        self.y = sb("y", [LANES, TILES, DIM])
        self.row_a = sb("row_a", [LANES, 2, DIM])
        self.eps = sb("eps", [LANES, 1])
        self.dst_i = sb("dst_i", [LANES, EDGE_COLS], I32)
        self.src_i = sb("src_i", [LANES, EDGE_COLS], I32)
        self.node_table = nc.dram_tensor("node_table", [N_NODES, DIM], F32, kind="Internal").ap()
        self.routed = nc.dram_tensor("routed", [MOE_BLOCKS * P, DIM], F32, kind="Internal").ap()
        self.head_table = nc.dram_tensor("head_table", [N_NODES, ROW], F32, kind="Internal").ap()


def own_waits(pool, m):
    pool.sem_inc(m.gathers_begun, 1)


def constants(nc, m, sem):
    made = m.constants_made
    with nc.Block() as block:

        @block.gpsimd
        def _(pool):
            chain = Chain(pool, made)
            chain.link(pool.memset(m.ident[:], 0.0))
            chain.link(pool.affine_select(out=m.ident[:], in_=m.ident[:], compare_op=ALU.not_equal, fill=1.0,
                                     base=0, pattern=[[-1, P]], channel_multiplier=1))
            chain.link(pool.memset(m.before[:], 1.0))
            chain.link(pool.affine_select(out=m.before[:], in_=m.before[:], compare_op=ALU.is_gt, fill=0.0,
                                     base=0, pattern=[[1, P]], channel_multiplier=-1))
            chain.link(pool.memset(m.ones[:], 1.0))
            chain.link(pool.iota(m.count_i[:], pattern=[[1, PAIR_BLOCKS]], base=0, channel_multiplier=0))
            chain.link(pool.iota(m.lane_i[:], pattern=[[0, 1]], base=0, channel_multiplier=1))
            chain.link(pool.iota(m.node_i[:], pattern=[[1, TILES]], base=0, channel_multiplier=TILES))

        @block.vector
        def _(dve):
            dve.wait_ge(made, 8)
            nc.vector.tensor_copy(m.ident16[:], m.ident[:])
            nc.vector.tensor_copy(m.count[:], m.count_i[:])
            nc.vector.tensor_copy(m.count16[:], m.count_i[:])
            nc.vector.tensor_copy(m.lane[:], m.lane_i[:])
            nc.vector.tensor_copy(m.node[:], m.node_i[:])


def slots_of_buckets(nc, sem, m, name, bucket, cols, buckets, blocks, out, unit=P):
    units = blocks * P // unit
    counted = sem(name + "_counted")
    summed = sem(name + "_summed")
    with ExitStack() as ctx:
        def sb(n, shape, dt=F32):
            return ctx.enter_context(nc.sbuf_tensor(f"{name}_{n}", shape, dt))

        mask = sb("mask", [LANES, buckets, cols])
        seen = sb("seen", [LANES, buckets, cols])
        ends = sb("ends", [LANES, buckets + 1])
        mine = sb("mine", [LANES, buckets])
        nblk = sb("nblk", [LANES, buckets])
        nblk_i = sb("nblk_i", [LANES, buckets], I32)
        last = sb("last", [LANES, buckets])
        off = sb("off", [LANES, buckets])
        slot = sb("slot", [LANES, cols])
        slot_i = sb("slot_i", [LANES, cols], I32)
        part_i = sb("part_i", [LANES, cols], I32)
        past = sb("past", [1, units, buckets])
        tile_f = sb("tile_f", [1, units])
        sums = ctx.enter_context(nc.psum_tensor(name + "_sums", [P, 2, 512], F32))
        with nc.Block() as block:

            @block.tensor
            def _(pe):
                pe.wait_ge(counted, 1)
                nc.tensor.matmul(sums[0:LANES, 0, 0:buckets], m.before[0:LANES, 0:LANES], mine[:], start=True, stop=True)
                nc.tensor.matmul(sums[0:LANES, 1, 0:buckets], m.ones[0:LANES, 0:LANES], mine[:], start=True, stop=True).then_inc(summed, 1)

            @block.vector
            def _(dve):
                chain = m.steps
                chain.link(nc.vector.memset(ends[:], 0.0))
                chain.link(nc.vector.tensor_tensor(
                    mask[:], bucket.unsqueeze(1).to_broadcast([LANES, buckets, cols]),
                    m.count[0:LANES, 0:buckets].unsqueeze(2).to_broadcast([LANES, buckets, cols]), ALU.is_equal))
                flat = mask[:].rearrange("p b c -> p (b c)")
                chain.link(nc.vector.tensor_tensor_scan(seen[:].rearrange("p b c -> p (b c)"), flat, flat, 0.0, ALU.add, ALU.max))
                chain.link(nc.vector.tensor_copy(ends[:, 1:], seen[:, :, cols - 1]))
                nc.vector.tensor_tensor(mine[:], ends[:, 1:], ends[:, 0:buckets], ALU.subtract).then_inc(counted, 1)
                dve.wait_ge(summed, 1)
                chain.link(nc.vector.tensor_scalar(nblk_i[:], sums[0:LANES, 1, 0:buckets], (unit - 1) / 2, 1 / unit, ALU.add, ALU.mult))
                chain.link(nc.vector.tensor_copy(nblk[:], nblk_i[:]))
                chain.link(nc.vector.tensor_tensor_scan(last[:], nblk[:], nblk[:], 0.0, ALU.add, ALU.max))
                chain.link(nc.vector.tensor_tensor(off[:], last[:], nblk[:], ALU.subtract))
                chain.link(nc.vector.tensor_scalar(off[:], off[:], float(unit), -1.0, ALU.mult, ALU.add))
                chain.link(nc.vector.tensor_tensor(off[:], off[:], sums[0:LANES, 0, 0:buckets], ALU.add))
                chain.link(nc.vector.tensor_tensor(off[:], off[:], ends[:, 0:buckets], ALU.subtract))
                chain.link(nc.vector.tensor_tensor(seen[:], seen[:], off[:].unsqueeze(2).to_broadcast([LANES, buckets, cols]), ALU.add))
                chain.link(nc.vector.tensor_tensor(seen[:], seen[:], mask[:], ALU.mult))
                chain.link(nc.vector.tensor_reduce(slot[:], seen[:].rearrange("p b c -> p c b"), AX_X, ALU.add))
                chain.link(nc.vector.tensor_copy(slot_i[:], slot[:]))
                chain.link(nc.vector.tensor_scalar(part_i[:], slot_i[:], 7, None, ALU.arith_shift_right))
                chain.link(nc.vector.tensor_copy(out.blk, part_i[:]))
                chain.link(nc.vector.tensor_scalar(slot_i[:], slot_i[:], P - 1, None, ALU.bitwise_and))
                chain.link(nc.vector.tensor_copy(out.pos, slot_i[:]))
                chain.link(nc.vector.tensor_tensor(
                    past[:], m.count[0:1, 0:units].unsqueeze(2).to_broadcast([1, units, buckets]),
                    last[0:1, :].unsqueeze(1).to_broadcast([1, units, buckets]), ALU.is_ge))
                chain.link(nc.vector.tensor_reduce(tile_f[:], past[:], AX_X, ALU.add))
                chain.link(nc.vector.tensor_scalar(out.tile_row, tile_f[:], float(buckets - 1), None, ALU.min))


def place_in_slots(nc, sem, m, name, pos, blk, values, cols, blocks, finish):
    nv = len(values)
    bufs = 4
    on_dve = 1 if nv != 2 else 0
    hot_made = sem(name + "_hot_made")
    made = sem(name + "_made")
    scaled = sem(name + "_scaled")
    used = sem(name + "_used")
    assert cols % bufs == 0
    with ExitStack() as ctx:
        hot = [ctx.enter_context(nc.sbuf_tensor(f"{name}_hot{u}", [LANES, P], F16)) for u in range(bufs)]
        rows = [ctx.enter_context(nc.sbuf_tensor(f"{name}_rows{u}", [LANES, nv, P], F16)) for u in range(bufs)]
        which = [ctx.enter_context(nc.sbuf_tensor(f"{name}_which{u}", [LANES, blocks], F16)) for u in range(bufs)]
        tables = ctx.enter_context(nc.psum_tensor(name + "_tables", [P, nv, 512], F32))
        with nc.Block() as block:

            @block.vector
            def _(dve):
                def factors(c, u):
                    one = bass.DynSlice(c, 1)
                    nc.vector.tensor_scalar(hot[u][:], m.count16[0:LANES, 0:P], pos[:, one], None, ALU.is_equal).then_inc(hot_made, 1)
                    for v in range(on_dve):
                        nc.vector.tensor_scalar(rows[u][:, v, :], m.count16[0:LANES, 0:P], pos[:, one], values[v][:, one],
                                                ALU.is_equal, ALU.mult)
                    nc.vector.tensor_scalar(which[u][:], m.count16[0:LANES, 0:blocks], blk[:, one], None, ALU.is_equal).then_inc(made, 1)

                for u in range(bufs):
                    factors(u, u)
                with dve.Fori(1, cols // bufs) as i:
                    for u in range(bufs):
                        dve.wait_ge(used, i * bufs + (u + 1 - bufs))
                        factors(i * bufs + u, u)
                dve.wait_ge(used, cols)
                finish(dve, m.steps, tables)

            if nv > on_dve:
                @block.scalar
                def _(act):
                    def scale(c, u, begun):
                        act.wait_ge(hot_made, c + 1)
                        if begun:
                            act.wait_ge(used, c + (1 - bufs))
                        for v in range(on_dve, nv):
                            last = nc.scalar.activation(rows[u][:, v, :], hot[u][:], ACT.Copy, scale=values[v][:, bass.DynSlice(c, 1)])
                        last.then_inc(scaled, 1)

                    for u in range(bufs):
                        scale(u, u, False)
                    with act.Fori(1, cols // bufs) as i:
                        for u in range(bufs):
                            scale(i * bufs + u, u, True)

            @block.tensor
            def _(pe):
                def products(c, u, start=False, stop=False):
                    pe.wait_ge(made, c + 1)
                    if nv > on_dve:
                        pe.wait_ge(scaled, c + 1)
                    for v in range(nv):
                        last = nc.tensor.matmul(tables[:, v, 0:blocks], rows[u][:, v, :], which[u][:], start=start, stop=stop)
                    last.then_inc(used, 1)

                for u in range(bufs):
                    products(u, u, start=u == 0)
                with pe.Fori(1, cols // bufs - 1) as i:
                    for u in range(bufs):
                        products(i * bufs + u, u)
                for u in range(bufs):
                    products(cols - bufs + u, u, stop=u == bufs - 1)


def layer_norm(nc, sem, m, name, x, y):
    var_ready = sem(name + "_var_ready")
    std_ready = sem(name + "_std_ready")
    with ExitStack() as ctx:
        stats = ctx.enter_context(nc.sbuf_tensor(name + "_stats", [LANES, TILES, 6], F32))
        mv = ctx.enter_context(nc.sbuf_tensor(name + "_mv", [LANES, TILES, 2], F32))
        var = ctx.enter_context(nc.sbuf_tensor(name + "_var", [LANES, TILES], F32))
        std = ctx.enter_context(nc.sbuf_tensor(name + "_std", [LANES, TILES], F32))
        rstd = ctx.enter_context(nc.sbuf_tensor(name + "_rstd", [LANES, TILES], F32))
        with nc.Block() as block:

            @block.scalar
            def _(act):
                act.wait_ge(var_ready, 1)
                nc.scalar.activation(std[:], var[:], ACT.Sqrt).then_inc(std_ready, 1)

            @block.vector
            def _(dve):
                for t in range(TILES):
                    last = nc.vector.bn_stats(stats[:, t, :], x[:, t, :])
                m.steps.link(last)
                for t in range(TILES):
                    last = nc.vector.bn_aggr(mv[:, t, :], stats[:, t, :])
                m.steps.link(last)
                nc.vector.tensor_scalar(var[:], mv[:, :, 1], LN_EPS, None, ALU.add).then_inc(var_ready, 1)
                dve.wait_ge(std_ready, 1)
                m.steps.link(nc.vector.reciprocal(rstd[:], std[:]))
                for t in range(TILES):
                    nc.vector.tensor_scalar(y[:, t, :], x[:, t, :], mv[:, t, 0:1], rstd[:, t:t + 1],
                                            ALU.subtract, ALU.mult)


def edge_messages(nc, sem, m, io):
    w_in = sem("edge_weights_in")
    edge_idx_ready = sem("edge_edge_idx_ready")
    node_idx_ready = sem("edge_node_idx_ready")
    ea_landed = [sem(f"edge_ea_landed{u}") for u in range(2)]
    nf_landed = [sem(f"edge_nf_landed{u}") for u in range(2)]
    turned = sem("edge_turned")
    turned_in = sem("edge_turned_in")
    hid_up = sem("edge_hid_up")
    hid_ready = sem("edge_hid_ready")
    e_up = sem("edge_e_up")
    summed = sem("edge_msg_summed")
    msg_ready = sem("edge_msg_ready")
    hot_ready = sem("edge_hot_ready")
    scattered = sem("edge_scattered")
    added = sem("edge_added")
    G = GROUP
    groups = EDGE_BLOCKS // G
    with ExitStack() as ctx:
        def sb(n, shape, dt=F32):
            return ctx.enter_context(nc.sbuf_tensor(f"edge_{n}", shape, dt))

        def ps(n, shape):
            return ctx.enter_context(nc.psum_tensor(f"edge_{n}", shape, F32))

        w1 = sb("w1", [P, KD, HID])
        b1 = sb("b1", [P, KH])
        w2 = sb("w2", [P, KH, DIM])
        edge_idx = [sb(f"edge_idx{u}", [P, G], I32) for u in range(2)]
        node_idx = [sb(f"node_idx{u}", [P, G], I32) for u in range(2)]
        ea = [sb(f"ea{u}", [P, G, DIM]) for u in range(2)]
        nf = [sb(f"nf{u}", [P, G, DIM]) for u in range(2)]
        eat = [sb(f"eat{u}", [P, KD, G * P]) for u in range(2)]
        hid = [sb(f"hid{u}", [P, KH, G * P]) for u in range(2)]
        pre = [sb(f"pre{u}", [P, G, DIM]) for u in range(2)]
        msg = [sb(f"msg{u}", [P, G, DIM]) for u in range(2)]
        hot = [sb(f"hot{u}", [P, G, LANES]) for u in range(2)]
        t_ps = ps("t_ps", [P, KD, G * P])
        h_ps = ps("h_ps", [P, 2, G * P])
        e_ps = ps("e_ps", [P, G, DIM])
        s_ps = ps("s_ps", [P, G, DIM])

        with nc.Block() as block:

            @block.sync
            def _(sp):
                sp.dma_start(w1[:], io["We1"].rearrange("(k p) h -> p k h", p=P)).then_inc(w_in, 16)
                sp.dma_start(w2[:], io["We2"].rearrange("(k p) h -> p k h", p=P)).then_inc(w_in, 16)
                sp.dma_start(b1[:], io["be1"]).then_inc(w_in, 16)

            def gather_edges(u):
                own_waits(nc.gpsimd, m)
                for j in range(G):
                    nc.gpsimd.indirect_dma_start(ea[u][:, j, :], None, io["edge_attr_256"][:, :],
                                                 bass.IndirectOffsetOnAxis(ap=edge_idx[u][:, j:j + 1], axis=0)).then_inc(ea_landed[u], 16)

            def gather_nodes(u):
                own_waits(nc.gpsimd, m)
                for j in range(G):
                    nc.gpsimd.indirect_dma_start(nf[u][:, j, :], None, m.node_table[:, :],
                                                 bass.IndirectOffsetOnAxis(ap=node_idx[u][:, j:j + 1], axis=0)).then_inc(nf_landed[u], 16)

            @block.gpsimd
            def _(pool):
                def edges_then_nodes(g, u, wait_summed):
                    pool.wait_ge(edge_idx_ready, g + (u + 1))
                    pool.wait_ge(turned, g + (u - 1))
                    gather_edges(u)
                    pool.wait_ge(node_idx_ready, g + u)
                    if wait_summed:
                        pool.wait_ge(summed, g + (u - 2))
                    gather_nodes(1 - u)

                for u in range(2):
                    pool.wait_ge(edge_idx_ready, u + 1)
                    gather_edges(u)
                pool.wait_ge(node_idx_ready, 1)
                gather_nodes(0)
                edges_then_nodes(2, 0, False)
                edges_then_nodes(2, 1, True)
                with pool.Fori(2, groups // 2) as turn:
                    for u in range(2):
                        edges_then_nodes(turn * 2, u, True)
                pool.wait_ge(node_idx_ready, groups)
                pool.wait_ge(summed, groups - 2)
                gather_nodes(1)

            def transposes(u, landed):
                pe = nc.tensor
                pe.wait_ge(ea_landed[u], landed)
                for j in range(G):
                    for k in range(KD):
                        last = pe.transpose(t_ps[:, k, j * P:(j + 1) * P], ea[u][:, j, k * P:(k + 1) * P], m.ident[:])
                last.then_inc(turned, 1)

            def hidden(u, g, first):
                pe = nc.tensor
                pe.wait_ge(turned_in, g + 1)
                for c in range(KH):
                    if not (first and c < 2):
                        pe.wait_ge(hid_ready, g * KH + (c - 1))
                    for k in range(KD):
                        last = pe.matmul(h_ps[:, c % 2, :], w1[:, k, c * P:(c + 1) * P], eat[u][:, k, :],
                                         start=k == 0, stop=k == KD - 1)
                    last.then_inc(hid_up, 1)

            def edges_out(u, g, first):
                pe = nc.tensor
                pe.wait_ge(hid_ready, g * KH + KH)
                if not first:
                    pe.wait_ge(summed, g)
                for j in range(G):
                    for k in range(KH):
                        last = pe.matmul(e_ps[:, j, :], hid[u][:, k, j * P:(j + 1) * P], w2[:, k, :],
                                         start=k == 0, stop=k == KH - 1)
                last.then_inc(e_up, 1)

            def scatter(u, g, first):
                pe = nc.tensor
                pe.wait_ge(msg_ready, g + 1)
                pe.wait_ge(hot_ready, g + 1)
                if not first:
                    pe.wait_ge(added, g * G)
                for j in range(G):
                    last = pe.matmul(s_ps[0:LANES, j, :], hot[u][:, j, :], msg[u][:, j, :], start=True, stop=True)
                last.then_inc(scattered, 1)

            @block.tensor
            def _(pe):
                pe.wait_ge(w_in, 48)
                transposes(0, 16 * G)
                hidden(0, 0, True)
                pe.wait_ge(turned_in, 1)
                transposes(1, 16 * G)
                edges_out(0, 0, True)
                hidden(1, 1, False)
                scatter(0, 0, True)
                pe.wait_ge(turned_in, 2)
                transposes(0, 2 * 16 * G)
                edges_out(1, 1, False)
                with pe.Fori(1, groups // 2 - 1) as turn:
                    g = turn * 2
                    for u in range(2):
                        hidden(u, g + u, False)
                        scatter(1 - u, g + (u - 1), False)
                        transposes(1 - u, (g + 2 * u) * (8 * G) + 16 * G)
                        edges_out(u, g + u, False)
                last = groups - 2
                hidden(0, last, False)
                scatter(1, last - 1, False)
                transposes(1, groups // 2 * 16 * G)
                edges_out(0, last, False)
                hidden(1, last + 1, False)
                scatter(0, last, False)
                edges_out(1, last + 1, False)
                scatter(1, last + 1, False)

            def hidden_relu(u, g):
                act = nc.scalar
                for c in range(KH):
                    act.wait_ge(hid_up, g * KH + (c + 1))
                    act.activation(hid[u][:, c, :], h_ps[:, c % 2, :], ACT.Relu, bias=b1[:, c:c + 1]).then_inc(hid_ready, 1)

            def message_relu(u, g):
                act = nc.scalar
                act.wait_ge(summed, g + 1)
                act.activation(msg[u][:], pre[u][:], ACT.Relu).then_inc(msg_ready, 1)

            @block.scalar
            def _(act):
                hidden_relu(0, 0)
                message_relu(0, 0)
                hidden_relu(1, 1)
                message_relu(1, 1)
                with act.Fori(1, groups // 2) as turn:
                    g = turn * 2
                    for u in range(2):
                        hidden_relu(u, g + u)
                        act.wait_ge(scattered, g + (u - 1))
                        message_relu(u, g + u)

            def stage_edge_idx(u, g):
                nc.vector.tensor_copy(edge_idx[u][:], m.edge_of_slot[:, bass.DynSlice(g * G, G)]).then_inc(edge_idx_ready, 1)

            def stage_node_idx(u, g):
                nc.vector.tensor_copy(node_idx[u][:], m.src_of_slot[:, bass.DynSlice(g * G, G)]).then_inc(node_idx_ready, 1)

            def one_hots(u, g):
                for j in range(G):
                    last = nc.vector.tensor_scalar(hot[u][:, j, :], m.count[:, 0:LANES],
                                                   m.dst_lane[:, bass.DynSlice(g * G + j, 1)], None, ALU.is_equal)
                last.then_inc(hot_ready, 1)

            def take_turned(u, g):
                nc.vector.wait_ge(turned, g + 1)
                nc.vector.tensor_copy(eat[u][:], t_ps[:]).then_inc(turned_in, 1)

            def add_nodes(u, g):
                nc.vector.wait_ge(e_up, g + 1)
                nc.vector.wait_ge(nf_landed[u], (g - u) * (8 * G) + 16 * G)
                nc.vector.tensor_tensor(pre[u][:], e_ps[:], nf[u][:], ALU.add).then_inc(summed, 1)

            def accumulate(g, first=False):
                dve = nc.vector
                tiles = [dve.value_load(m.dst_tile[0:1, bass.DynSlice(g * G + j, 1)], min_val=0, max_val=TILES - 1)
                         for j in range(G)]
                dve.wait_ge(scattered, g + 1)
                for j, tile in enumerate(tiles):
                    if not first or j > 0:
                        dve.wait_ge(added, g * G + j)
                    dve.tensor_tensor(m.acc[:, tile, :], s_ps[0:LANES, j, :], m.acc[:, tile, :], ALU.add).then_inc(added, 1)

            @block.vector
            def _(dve):
                zeroed = sem("edge_acc_zeroed")
                nc.vector.memset(m.acc[:], 0.0).then_inc(zeroed, 1)
                for u in range(2):
                    stage_edge_idx(u, u)
                    stage_node_idx(u, u)
                dve.wait_ge(zeroed, 1)
                take_turned(0, 0)
                stage_edge_idx(0, 2)

                def one_group(g, u, start=False, ahead=3):
                    if not start:
                        accumulate(g + (u - 2))
                    one_hots(u, g + u)
                    if ahead > 0:
                        take_turned(1 - u, g + (u + 1))
                    if ahead > 2:
                        stage_edge_idx(1 - u, g + (u + 3))
                    add_nodes(u, g + u)
                    if ahead > 1:
                        stage_node_idx(u, g + (u + 2))

                one_group(0, 0, start=True)
                one_group(0, 1, start=True)
                accumulate(0, first=True)
                one_group(2, 0, start=True)
                one_group(2, 1)
                with dve.Fori(2, groups // 2 - 2) as turn:
                    for u in range(2):
                        one_group(turn * 2, u)
                last = groups - 4
                one_group(last, 0)
                one_group(last, 1, ahead=2)
                one_group(last + 2, 0, ahead=1)
                one_group(last + 2, 1, ahead=0)
                for u in range(2):
                    accumulate(last + 2 + u)


def load_inputs(nc, sem, m, io):
    done = sem("load_done")
    with nc.Block() as block:

        @block.sync
        def _(sp):
            sp.dma_start(m.x[:], io["x"].rearrange("(p t) d -> p t d", t=TILES)).then_inc(done, 16)
            sp.dma_start(m.dst_i[:], io["dst"].rearrange("(p c) -> p c", c=EDGE_COLS)).then_inc(done, 16)
            sp.dma_start(m.src_i[:], io["src"].rearrange("(p c) -> p c", c=EDGE_COLS)).then_inc(done, 16)
            sp.dma_start(m.row_a[:, 0, :], io["be2"].partition_broadcast(LANES)).then_inc(done, 16)
            sp.dma_start(m.row_a[:, 1, :], io["bn2"].partition_broadcast(LANES)).then_inc(done, 16)
            sp.dma_start(m.eps[:], io["eps"].partition_broadcast(LANES)).then_inc(done, 16)
            sp.wait_ge(done, 96)


def node_table(nc, sem, m, name, y, rows, table, bias=None):
    ready = sem(name + "_ready")
    stored = sem(name + "_stored")
    with nc.Block() as block:

        @block.vector
        def _(dve):
            if bias is not None:
                nc.vector.tensor_tensor(rows[:], y[:], bias.unsqueeze(1).to_broadcast(list(y.shape)), ALU.add).then_inc(ready, 1)

        @block.sync
        def _(sp):
            if bias is not None:
                sp.wait_ge(ready, 1)
            sp.dma_start(table.rearrange("(p t) d -> p t d", t=TILES), rows[:] if bias is not None else y[:]).then_inc(stored, 16)
            sp.wait_ge(stored, 16)


def edge_tables(nc, sem, m, name, key_i, other_i, with_edge, out, blocks=EDGE_BLOCKS, unit=P):
    with ExitStack() as ctx:
        def sb(n, dt=F32):
            return ctx.enter_context(nc.sbuf_tensor(f"{name}_{n}", [LANES, EDGE_COLS], dt))

        lane = sb("lane")
        lane1 = sb("lane1")
        key = sb("key")
        bucket = sb("bucket")
        other = sb("other")
        pos = sb("pos")
        blk = sb("blk")
        lane_i = sb("lane_i", I32)
        at = sb("at")
        with nc.Block() as block:

            @block.vector
            def _(dve):
                chain = m.steps
                chain.link(nc.vector.tensor_copy(key[:], key_i[:]))
                chain.link(nc.vector.tensor_copy(other[:], other_i[:]))
                chain.link(nc.vector.tensor_scalar(lane_i[:], key[:], 1 / TILES, -(TILES - 1) / 2 / TILES, ALU.mult, ALU.add))
                chain.link(nc.vector.tensor_copy(lane[:], lane_i[:]))
                chain.link(nc.vector.scalar_tensor_tensor(bucket[:], lane[:], -float(TILES), key[:], ALU.mult, ALU.add))
                chain.link(nc.vector.tensor_scalar(lane1[:], lane[:], 1.0, None, ALU.add))
                chain.link(nc.vector.tensor_scalar(other[:], other[:], -float(NODE_MID), None, ALU.add))
                chain.link(nc.vector.tensor_scalar(at[:], m.count[0:LANES, 0:EDGE_COLS], 0.0, m.lane[0:LANES, :], ALU.mult, ALU.add))
        slots_of_buckets(nc, sem, m, name + "_sort", bucket[:], EDGE_COLS, TILES, blocks,
                         Slots(pos=pos[:], blk=blk[:], tile_row=out.tile_row), unit)
        values = [other, lane1]
        if with_edge:
            values += [at, m.count[0:LANES, 0:EDGE_COLS]]
        column = ctx.enter_context(nc.sbuf_tensor(f"{name}_column", [P, blocks], F32))

        def finish(dve, chain, tables):
            chain.link(nc.vector.tensor_scalar(out.other, tables[:, 0, 0:blocks], float(NODE_MID), None, ALU.add))
            chain.link(nc.vector.tensor_scalar(out.lane, tables[:, 1, 0:blocks], -1.0, None, ALU.add))
            if with_edge:
                chain.link(nc.vector.tensor_copy(column[:], tables[:, 3, 0:blocks]))
                chain.link(nc.vector.scalar_tensor_tensor(out.edge, tables[:, 2, 0:blocks], float(EDGE_COLS), column[:],
                                                     ALU.mult, ALU.add))

        place_in_slots(nc, sem, m, name + "_place", pos, blk, values, EDGE_COLS, blocks, finish)


def node_mlp(nc, sem, m, io):
    w_in = sem("nmlp_weights_in")
    z_ready = sem("nmlp_z_ready")
    turned = sem("nmlp_turned")
    turned_in = sem("nmlp_turned_in")
    hid_up = sem("nmlp_hid_up")
    hid_ready = sem("nmlp_hid_ready")
    out_up = sem("nmlp_out_up")
    out_taken = sem("nmlp_out_taken")
    with ExitStack() as ctx:
        def sb(n, shape, dt=F32):
            return ctx.enter_context(nc.sbuf_tensor(f"nmlp_{n}", shape, dt))

        def ps(n, shape):
            return ctx.enter_context(nc.psum_tensor(f"nmlp_{n}", shape, F32))

        w1 = sb("w1", [P, KD, HID])
        b1 = sb("b1", [P, KH])
        w2 = sb("w2", [P, KH, DIM])
        eps1 = sb("eps1", [LANES, 1])
        z = sb("z", [LANES, CHUNK, DIM])
        zt = sb("zt", [P, KD, CW])
        hid = sb("hid", [P, KH, CW])
        t_ps = ps("t_ps", [P, KD, 512])
        h_ps = ps("h_ps", [P, KH, 512])
        o_ps = ps("o_ps", [P, CHUNK, DIM])
        with nc.Block() as block:

            @block.sync
            def _(sp):
                sp.dma_start(w1[:], io["Wn1"].rearrange("(k p) h -> p k h", p=P)).then_inc(w_in, 16)
                sp.dma_start(w2[:], io["Wn2"].rearrange("(k p) h -> p k h", p=P)).then_inc(w_in, 16)
                sp.dma_start(b1[:], io["bn1"]).then_inc(w_in, 16)

            @block.vector
            def _(dve):
                chain = m.steps
                chain.link(nc.vector.tensor_scalar(eps1[:], m.eps[:], 1.0, None, ALU.add))
                chain.link(nc.vector.tensor_tensor(m.x[:], m.x[:], m.row_a[:, 1, :].unsqueeze(1).to_broadcast([LANES, TILES, DIM]), ALU.add))
                with dve.Fori(0, CHUNKS) as c:
                    tiles = bass.DynSlice(c * CHUNK, CHUNK)
                    nc.vector.scalar_tensor_tensor(z[:], m.y[:, tiles, :], eps1[:, 0:1], m.acc[:, tiles, :],
                                                   ALU.mult, ALU.add).then_inc(z_ready, 1)
                    dve.wait_ge(turned, c + 1)
                    nc.vector.tensor_copy(zt[:], t_ps[:, :, 0:CW]).then_inc(turned_in, 1)
                    dve.wait_ge(out_up, c + 1)
                    nc.vector.tensor_tensor(m.x[:, tiles, :], m.x[:, tiles, :], o_ps[0:LANES, :, :], ALU.add).then_inc(out_taken, 1)

            @block.scalar
            def _(act):
                act.wait_ge(w_in, 48)
                with act.Fori(0, CHUNKS) as c:
                    for k in range(KH):
                        act.wait_ge(hid_up, c * KH + (k + 1))
                        nc.scalar.activation(hid[:, k, :], h_ps[:, k, 0:CW], ACT.Relu, bias=b1[:, k:k + 1]).then_inc(hid_ready, 1)

            @block.tensor
            def _(pe):
                pe.wait_ge(w_in, 48)
                with pe.Fori(0, CHUNKS) as c:
                    pe.wait_ge(z_ready, c + 1)
                    for t in range(CHUNK):
                        for k in range(KD):
                            last = nc.tensor.transpose(t_ps[:, k, t * LANES:(t + 1) * LANES], z[:, t, k * P:(k + 1) * P],
                                                       m.ident[0:LANES, 0:LANES])
                    last.then_inc(turned, 1)
                    pe.wait_ge(turned_in, c + 1)
                    for h in range(KH):
                        for k in range(KD):
                            last = nc.tensor.matmul(h_ps[:, h, 0:CW], w1[:, k, h * P:(h + 1) * P], zt[:, k, :],
                                                    start=k == 0, stop=k == KD - 1)
                        last.then_inc(hid_up, 1)
                    pe.wait_ge(hid_ready, c * KH + KH)
                    for t in range(CHUNK):
                        for k in range(KH):
                            last = nc.tensor.matmul(o_ps[0:LANES, t, :], hid[:, k, t * LANES:(t + 1) * LANES], w2[:, k, :],
                                                    start=k == 0, stop=k == KH - 1)
                    last.then_inc(out_up, 1)


class Routing:
    def __init__(self, sb):
        self.gate = sb("gate", [LANES, TOP, TILES])
        self.expert = sb("expert", [LANES, TOP, TILES])
        self.slot_i = sb("slot_i", [LANES, TOP, TILES], I32)
        self.node_of_slot = sb("node_of_slot", [P, MOE_BLOCKS], I32)
        self.block_expert = sb("block_expert", [1, MOE_BLOCKS], I32)


def moe_gates(nc, sem, m, io, r):
    in_ = sem("gate_in")
    staged = sem("gate_staged")
    turned = sem("gate_turned")
    turned_in = sem("gate_turned_in")
    up = sem("gate_up")
    taken = sem("gate_taken")
    logits_ready = sem("gate_logits_ready")
    exp_ready = sem("gate_exp_ready")
    with ExitStack() as ctx:
        def sb(n, shape, dt=F32):
            return ctx.enter_context(nc.sbuf_tensor(f"gate_{n}", shape, dt))

        w = sb("w", [P, KD, EXPERTS])
        b = sb("b", [LANES, EXPERTS])
        z = sb("z", [LANES, CHUNK, DIM])
        zt = sb("zt", [P, KD, CW])
        logits = sb("logits", [LANES, TILES, EXPERTS])
        top = sb("top", [LANES, TILES, 8])
        which = sb("which", [LANES, TILES, 8], mybir.dt.uint32)
        big = sb("big", [LANES, TILES])
        t_ps = ctx.enter_context(nc.psum_tensor("gate_t_ps", [P, KD, 512], F32))
        g_ps = ctx.enter_context(nc.psum_tensor("gate_g_ps", [P, CHUNK, EXPERTS], F32))
        wide = [LANES, TILES, EXPERTS]
        with nc.Block() as block:

            @block.sync
            def _(sp):
                sp.dma_start(w[:], io["gate_w"].rearrange("(k p) e -> p k e", p=P)).then_inc(in_, 16)
                sp.dma_start(b[:], io["gate_b"].partition_broadcast(LANES)).then_inc(in_, 16)

            @block.tensor
            def _(pe):
                pe.wait_ge(in_, 32)
                with pe.Fori(0, CHUNKS) as c:
                    pe.wait_ge(staged, c + 1)
                    for t in range(CHUNK):
                        for k in range(KD):
                            last = nc.tensor.transpose(t_ps[:, k, t * LANES:(t + 1) * LANES], z[:, t, k * P:(k + 1) * P],
                                                       m.ident[0:LANES, 0:LANES])
                    last.then_inc(turned, 1)
                    pe.wait_ge(turned_in, c + 1)
                    for t in range(CHUNK):
                        for k in range(KD):
                            last = nc.tensor.matmul(g_ps[0:LANES, t, :], zt[:, k, t * LANES:(t + 1) * LANES], w[:, k, :],
                                                    start=k == 0, stop=k == KD - 1)
                    last.then_inc(up, 1)

            @block.scalar
            def _(act):
                act.wait_ge(logits_ready, 1)
                nc.scalar.activation(logits[:], logits[:], ACT.Exp).then_inc(exp_ready, 1)

            @block.vector
            def _(dve):
                dve.wait_ge(in_, 32)
                with dve.Fori(0, CHUNKS) as c:
                    tiles = bass.DynSlice(c * CHUNK, CHUNK)
                    nc.vector.tensor_copy(z[:], m.y[:, tiles, :]).then_inc(staged, 1)
                    dve.wait_ge(turned, c + 1)
                    nc.vector.tensor_copy(zt[:], t_ps[:, :, 0:CW]).then_inc(turned_in, 1)
                    dve.wait_ge(up, c + 1)
                    nc.vector.tensor_tensor(logits[:, tiles, :], g_ps[0:LANES, :, :],
                                            b[:].unsqueeze(1).to_broadcast([LANES, CHUNK, EXPERTS]), ALU.add).then_inc(taken, 1)
                dve.wait_ge(taken, CHUNKS)
                chain = m.steps
                chain.link(nc.vector.tensor_reduce(big[:], logits[:], AX_X, ALU.max))
                nc.vector.tensor_tensor(logits[:], logits[:], big[:].unsqueeze(2).to_broadcast(wide), ALU.subtract).then_inc(logits_ready, 1)
                dve.wait_ge(exp_ready, 1)
                chain.link(nc.vector.tensor_reduce(big[:], logits[:], AX_X, ALU.add))
                chain.link(nc.vector.reciprocal(big[:], big[:]))
                chain.link(nc.vector.tensor_tensor(logits[:], logits[:], big[:].unsqueeze(2).to_broadcast(wide), ALU.mult))
                for t in range(TILES):
                    chain.link(nc.vector.max(top[:, t, :], logits[:, t, :]))
                for t in range(TILES):
                    last = nc.vector.max_index(which[:, t, :], top[:, t, :], logits[:, t, :])
                chain.link(last)
                chain.link(nc.vector.tensor_tensor(big[:], top[:, :, 0], top[:, :, 1], ALU.add))
                chain.link(nc.vector.reciprocal(big[:], big[:]))
                for k in range(TOP):
                    chain.link(nc.vector.tensor_tensor(r.gate[:, k, :], top[:, :, k], big[:], ALU.mult))
                    chain.link(nc.vector.tensor_copy(r.expert[:, k, :], which[:, :, k]))


def moe_experts(nc, sem, m, io, r):
    AB, WB = 2, 3
    idx_ready = sem("moe_idx_ready")
    rows_in = [sem(f"moe_rows_in{u}") for u in range(AB)]
    w_in = [sem(f"moe_w_in{u}") for u in range(WB)]
    turned = sem("moe_turned")
    turned_in = sem("moe_turned_in")
    h_up = sem("moe_h_up")
    silu_ready = sem("moe_silu_ready")
    hid_ready = sem("moe_hid_ready")
    y_up = sem("moe_y_up")
    y_ready = sem("moe_y_ready")
    stored = [sem(f"moe_stored{u}") for u in range(AB)]
    nb = MOE_BLOCKS
    unroll = AB * WB
    assert nb % unroll == 0

    def blocks(eng, body):
        for k in range(unroll):
            body(k, k)
        with eng.Fori(1, nb // unroll - 1) as turn:
            for k in range(unroll):
                body(turn * unroll + k, k)
        for k in range(nb - unroll, nb):
            body(k, k % unroll)

    def begun(b, n):
        return not isinstance(b, int) or b >= n

    with ExitStack() as ctx:
        def sb(n, shape, dt=F32, bufs=AB):
            return [ctx.enter_context(nc.sbuf_tensor(f"moe_{n}{u}", shape, dt)) for u in range(bufs)]

        def ps(n, shape):
            return [ctx.enter_context(nc.psum_tensor(f"moe_{n}{u}", shape, F32)) for u in range(AB)]

        idx = sb("idx", [P, 1], I32)
        rows = sb("rows", [P, DIM])
        xt = sb("xt", [P, KD, P])
        w1 = sb("w1", [P, KD, HID], bufs=WB)
        w2 = sb("w2", [P, KD, HID], bufs=WB)
        w3 = sb("w3", [P, KH, DIM], bufs=WB)
        silu = sb("silu", [P, KH, P])
        hid = sb("hid", [P, KH, P])
        out = sb("out", [P, DIM])
        t_ps = ps("t_ps", [P, KD, 256])
        h1_ps = ps("h1_ps", [P, KH, P])
        h2_ps = ps("h2_ps", [P, KH, P])
        y_ps = ps("y_ps", [P, 512])
        with nc.Block() as block:

            @block.gpsimd
            def _(pool):
                def gather(b, k):
                    pool.wait_ge(idx_ready, b + 1)
                    if begun(b, AB):
                        pool.wait_ge(turned, b - (AB - 1))
                    own_waits(pool, m)
                    pool.indirect_dma_start(rows[k % AB][:], None, m.node_table[:, :],
                                            bass.IndirectOffsetOnAxis(ap=idx[k % AB][:, 0:1], axis=0)).then_inc(rows_in[k % AB], 16)

                blocks(pool, gather)

            @block.sync
            def _(sp):
                def load(b, k):
                    e = sp.value_load(r.block_expert[0:1, bass.DynSlice(b, 1)], min_val=0, max_val=EXPERTS - 1)
                    one = bass.DynSlice(e, 1)
                    u = k % WB
                    if begun(b, WB):
                        sp.wait_ge(y_up, b - (WB - 1))
                    for w, wd in ((w1[u], io["w1"]), (w2[u], io["w2"]), (w3[u], io["w3"])):
                        sp.dma_start(w[:], wd[one, :, :].rearrange("a (k p) h -> p (a k) h", p=P)).then_inc(w_in[u], 16)

                def store(b, k):
                    sp.wait_ge(y_ready, b + 1)
                    sp.dma_start(m.routed[bass.DynSlice(b * P, P), :], out[k % AB][:]).then_inc(stored[k % AB], 16)

                def load_and_store(b, k):
                    load(b, k)
                    if begun(b, WB):
                        store(b - WB, (k - WB) % unroll)

                blocks(sp, load_and_store)
                for b in range(nb - WB, nb):
                    store(b, b % unroll)
                for u in range(AB):
                    sp.wait_ge(stored[u], nb // AB * 16)

            @block.tensor
            def _(pe):
                def transposes(b, k):
                    u = k % AB
                    pe.wait_ge(rows_in[u], (b - u) * (16 // AB) + 16)
                    for kd in range(KD):
                        last = nc.tensor.transpose(t_ps[u][:, kd, 0:P], rows[u][:, kd * P:(kd + 1) * P], m.ident[:])
                    last.then_inc(turned, 1)

                def hidden(b, k):
                    u, v = k % AB, k % WB
                    pe.wait_ge(turned_in, b + 1)
                    pe.wait_ge(w_in[v], (b - v) * (48 // WB) + 48)
                    for w, h_ps in ((w1[v], h1_ps[u]), (w2[v], h2_ps[u])):
                        for c in range(KH):
                            for kd in range(KD):
                                last = nc.tensor.matmul(h_ps[:, c, :], w[:, kd, c * P:(c + 1) * P], xt[u][:, kd, :],
                                                        start=kd == 0, stop=kd == KD - 1)
                        last.then_inc(h_up, 1)

                def rows_out(b, k):
                    u, v = k % AB, k % WB
                    pe.wait_ge(hid_ready, b + 1)
                    if begun(b, AB):
                        pe.wait_ge(y_ready, b - (AB - 1))
                    for kh in range(KH):
                        last = nc.tensor.matmul(y_ps[u][:, 0:DIM], hid[u][:, kh, :], w3[v][:, kh, :], start=kh == 0, stop=kh == KH - 1)
                    last.then_inc(y_up, 1)

                def one_block(b, k):
                    hidden(b, k)
                    if begun(b, 1):
                        rows_out(b - 1, (k - 1) % unroll)
                    if not isinstance(b, int) or b < nb - AB:
                        transposes(b + AB, (k + AB) % unroll)

                for b in range(AB):
                    transposes(b, b)
                blocks(pe, one_block)
                rows_out(nb - 1, unroll - 1)

            @block.scalar
            def _(act):
                def silus(b, k):
                    act.wait_ge(h_up, 2 * b + 1)
                    if begun(b, AB):
                        act.wait_ge(hid_ready, b - (AB - 1))
                    nc.scalar.activation(silu[k % AB][:], h1_ps[k % AB][:], ACT.Silu).then_inc(silu_ready, 1)

                def take_out(b, k):
                    u = k % AB
                    act.wait_ge(y_up, b + 1)
                    if begun(b, AB):
                        act.wait_ge(stored[u], (b - u) * (16 // AB))
                    nc.scalar.activation(out[u][:], y_ps[u][:, 0:DIM], ACT.Copy).then_inc(y_ready, 1)

                def one_block(b, k):
                    silus(b, k)
                    if begun(b, 1):
                        take_out(b - 1, (k - 1) % unroll)

                blocks(act, one_block)
                take_out(nb - 1, unroll - 1)

            @block.vector
            def _(dve):
                def stage(b, k):
                    nc.vector.tensor_copy(idx[k % AB][:], r.node_of_slot[:, bass.DynSlice(b, 1)]).then_inc(idx_ready, 1)

                def take_turned(b, k):
                    dve.wait_ge(turned, b + 1)
                    nc.vector.tensor_copy(xt[k % AB][:], t_ps[k % AB][:, :, 0:P]).then_inc(turned_in, 1)

                def multiply(b, k):
                    dve.wait_ge(silu_ready, b + 1)
                    dve.wait_ge(h_up, 2 * b + 2)
                    nc.vector.tensor_tensor(hid[k % AB][:], silu[k % AB][:], h2_ps[k % AB][:], ALU.mult).then_inc(hid_ready, 1)

                def one_block(b, k):
                    multiply(b, k)
                    if not isinstance(b, int) or b < nb - AB:
                        take_turned(b + AB, (k + AB) % unroll)
                    if not isinstance(b, int) or b < nb - 2 * AB:
                        stage(b + 2 * AB, (k + 2 * AB) % unroll)

                for b in range(AB):
                    stage(b, b)
                for b in range(AB):
                    take_turned(b, b)
                    stage(b + AB, b + AB)
                blocks(dve, one_block)


def moe_combine(nc, sem, m, r):
    idx_ready = sem("comb_idx_ready")
    landed = [sem(f"comb_landed{u}") for u in range(4)]
    done = sem("comb_done")
    with ExitStack() as ctx:
        idx = [ctx.enter_context(nc.sbuf_tensor(f"comb_idx{u}", [LANES, 1], I32)) for u in range(4)]
        got = [ctx.enter_context(nc.sbuf_tensor(f"comb_got{u}", [LANES, DIM], F32)) for u in range(4)]
        with nc.Block() as block:

            @block.gpsimd
            def _(pool):
                def gather(u):
                    own_waits(nc.gpsimd, m)
                    nc.gpsimd.indirect_dma_start(got[u][:], None, m.routed[:, :],
                                                 bass.IndirectOffsetOnAxis(ap=idx[u][:, 0:1], axis=0)).then_inc(landed[u], 16)

                with pool.Fori(0, TILES // 2) as i:
                    for u in range(4):
                        pool.wait_ge(idx_ready, 4 * i + (u + 1))
                        gather(u)

            @block.vector
            def _(dve):
                def stage(i, u):
                    nc.vector.tensor_copy(idx[u][:], r.slot_i[:, u % 2, bass.DynSlice(2 * i + u // 2, 1)]).then_inc(idx_ready, 1)

                def take(i, u):
                    t = bass.DynSlice(2 * i + u // 2, 1)
                    dve.wait_ge(landed[u], 16 * i + 16)
                    if u % 2:
                        dve.wait_ge(done, 4 * i + u)
                    nc.vector.scalar_tensor_tensor(m.x[:, t, :], got[u][:].unsqueeze(1), r.gate[:, u % 2, t], m.x[:, t, :],
                                                   ALU.mult, ALU.add).then_inc(done, 1)

                for u in range(4):
                    stage(0, u)
                with dve.Fori(0, TILES // 2 - 1) as i:
                    for u in range(4):
                        take(i, u)
                        stage(i + 1, u)
                for u in range(4):
                    take(TILES // 2 - 1, u)


def mixture(nc, sem, m, io):
    items = TOP * TILES
    with ExitStack() as ctx:
        def sb(n, shape, dt=F32):
            return ctx.enter_context(nc.sbuf_tensor(f"mix_{n}", shape, dt))

        r = Routing(sb)
        pos = sb("pos", [LANES, items])
        blk = sb("blk", [LANES, items])
        node = sb("node", [LANES, items])
        layer_norm(nc, sem, m, "ln_b", m.x, m.y)
        node_table(nc, sem, m, "norm_table", m.y, None, m.node_table)
        moe_gates(nc, sem, m, io, r)
        slots_of_buckets(nc, sem, m, "mix_sort", r.expert[:].rearrange("p a t -> p (a t)"), items, EXPERTS, MOE_BLOCKS,
                         Slots(pos=pos[:], blk=blk[:], tile_row=r.block_expert[:]))
        with nc.Block() as block:

            @block.vector
            def _(dve):
                chain = m.steps
                for a in range(TOP):
                    chain.link(nc.vector.tensor_scalar(node[:, a * TILES:(a + 1) * TILES], m.node[:], -float(NODE_MID), None, ALU.add))
                chain.link(nc.vector.scalar_tensor_tensor(r.slot_i[:].rearrange("p a t -> p (a t)"), blk[:], float(P), pos[:], ALU.mult, ALU.add))

        def finish(dve, chain, tables):
            chain.link(nc.vector.tensor_scalar(r.node_of_slot[:], tables[:, 0, 0:MOE_BLOCKS], float(NODE_MID), None, ALU.add))

        place_in_slots(nc, sem, m, "mix_place", pos, blk, [node], items, MOE_BLOCKS, finish)
        moe_experts(nc, sem, m, io, r)
        moe_combine(nc, sem, m, r)


def attention_rows(nc, sem, m, io, sl):
    in_ = sem("hrow_in")
    staged = sem("hrow_staged")
    turned = sem("hrow_turned")
    turned_in = sem("hrow_turned_in")
    up = sem("hrow_up")
    chain_s = sem("hrow_chain")
    stored = sem("hrow_stored")
    with ExitStack() as ctx:
        def sb(n, shape, dt=F32):
            return ctx.enter_context(nc.sbuf_tensor(f"hrow_{n}", shape, dt))

        w = sb("w", [P, KD, HEADS * HEAD_C])
        a = sb("a", [LANES, 2, HEADS * HEAD_C])
        z = sb("z", [LANES, CHUNK, DIM])
        zt = sb("zt", [P, KD, CW])
        rows = sb("rows", [LANES, TILES, ROW])
        prod = sb("prod", [LANES, CHUNK, DIM])
        t_ps = ctx.enter_context(nc.psum_tensor("hrow_t_ps", [P, KD, 512], F32))
        h_ps = ctx.enter_context(nc.psum_tensor("hrow_h_ps", [P, CHUNK, DIM], F32))
        with nc.Block() as block:

            @block.sync
            def _(sp):
                for h, (wd, ad) in enumerate(((io["W1"], io["a1"]), (io["W2"], io["a2"]))):
                    part = slice(h * HEAD_C, (h + 1) * HEAD_C)
                    sp.dma_start(w[:, :, part], wd.rearrange("(k p) c -> p k c", p=P)).then_inc(in_, 16)
                    for side in range(2):
                        sp.dma_start(a[:, side, part], ad[0, side * HEAD_C:(side + 1) * HEAD_C].partition_broadcast(LANES)).then_inc(in_, 16)
                sp.wait_ge(chain_s, 5 * CHUNKS)
                sp.dma_start(m.head_table.rearrange("(p t) d -> p t d", t=TILES), rows[:]).then_inc(stored, 16)
                sp.wait_ge(stored, 16)

            @block.tensor
            def _(pe):
                pe.wait_ge(in_, 96)
                with pe.Fori(0, CHUNKS) as c:
                    pe.wait_ge(staged, c + 1)
                    for t in range(CHUNK):
                        for k in range(KD):
                            last = nc.tensor.transpose(t_ps[:, k, t * LANES:(t + 1) * LANES], z[:, t, k * P:(k + 1) * P],
                                                       m.ident[0:LANES, 0:LANES])
                    last.then_inc(turned, 1)
                    pe.wait_ge(turned_in, c + 1)
                    for t in range(CHUNK):
                        for k in range(KD):
                            last = nc.tensor.matmul(h_ps[0:LANES, t, :], zt[:, k, t * LANES:(t + 1) * LANES], w[:, k, :],
                                                    start=k == 0, stop=k == KD - 1)
                    last.then_inc(up, 1)

            @block.vector
            def _(dve):
                dve.wait_ge(in_, 96)
                with dve.Fori(0, CHUNKS) as c:
                    tiles = bass.DynSlice(c * CHUNK, CHUNK)
                    nc.vector.tensor_copy(z[:], m.y[:, tiles, :]).then_inc(staged, 1)
                    dve.wait_ge(turned, c + 1)
                    nc.vector.tensor_copy(zt[:], t_ps[:, :, 0:CW]).then_inc(turned_in, 1)
                    dve.wait_ge(up, c + 1)
                    nc.vector.tensor_copy(rows[:, tiles, 0:DIM], h_ps[0:LANES, :, :]).then_inc(chain_s, 1)
                    for side in range(2):
                        dve.wait_ge(chain_s, 5 * c + (1 + 2 * side))
                        nc.vector.tensor_tensor(prod[:], h_ps[0:LANES, :, :],
                                                a[:, side, :].unsqueeze(1).to_broadcast([LANES, CHUNK, DIM]), ALU.mult).then_inc(chain_s, 1)
                        dve.wait_ge(chain_s, 5 * c + (2 + 2 * side))
                        to = sl[:, tiles, :] if side == 0 else rows[:, tiles, DIM:ROW]
                        nc.vector.tensor_reduce(to, prod[:].rearrange("p t (h c) -> p t h c", h=HEADS), AX_X, ALU.add).then_inc(chain_s, 1)


def split_scores(nc, sem, m, sl, parts):
    with ExitStack() as ctx:
        rest = ctx.enter_context(nc.sbuf_tensor("split_rest", [LANES, TILES, HEADS], F32))
        with nc.Block() as block:

            @block.vector
            def _(dve):
                chain = m.steps
                left = sl[:]
                for n in range(3):
                    part = parts[:, :, n * HEADS:(n + 1) * HEADS]
                    chain.link(nc.vector.tensor_copy(part, left))
                    if n < 2:
                        chain.link(nc.vector.tensor_tensor(rest[:], left, part, ALU.subtract))
                        left = rest[:]


def attend_edges(nc, sem, m, r, sl, acc):
    idx_ready = sem("att_idx_ready")
    landed = [sem(f"att_landed{u}") for u in range(2)]
    hot16_ready = sem("att_hot16_ready")
    hot_ready = sem("att_hot_ready")
    parts_summed = sem("att_parts_summed")
    turned = sem("att_turned")
    turned_in = sem("att_turned_in")
    sl_up = sem("att_sl_up")
    logit = sem("att_logit")
    lrelu_ready = sem("att_lrelu_ready")
    e_ready = sem("att_e_ready")
    scaled = sem("att_scaled")
    scattered = sem("att_scattered")
    added = sem("att_added")
    G = GROUP
    UN = G * P // PAIR
    groups = PAIR_BLOCKS // G
    turns = groups // 2

    def tiles_of(eng, g):
        return [eng.value_load(r.tile_row[0:1, bass.DynSlice(g * UN + n, 1)], min_val=0, max_val=TILES - 1) for n in range(UN)]

    with ExitStack() as ctx:
        def sb(n, shape, dt=F32):
            return [ctx.enter_context(nc.sbuf_tensor(f"att_{n}{u}", shape, dt)) for u in range(2)]

        def ps(n, shape):
            return ctx.enter_context(nc.psum_tensor(f"att_{n}", shape, F32))

        idx = sb("idx", [P, G], I32)
        got = sb("got", [P, G, ROW])
        hot16 = sb("hot16", [P, G, LANES], BF16)
        hot_t = sb("hot_t", [LANES, G, P], BF16)
        hot = sb("hot", [P, G, LANES])
        parts = sb("parts", [P, G, HEADS])
        z = sb("z", [P, G, HEADS])
        lrelu = sb("lrelu", [P, G, HEADS])
        e = sb("e", [P, G, HEADS])
        w = sb("w", [P, G, ROW])
        t_ps = ctx.enter_context(nc.psum_tensor("att_t_ps", [P, G, P], BF16))
        sl_ps = ps("sl_ps", [P, 512])
        s_ps = [ps(f"s_ps{u}", [P, UN, 512]) for u in range(2)]
        with nc.Block() as block:

            @block.gpsimd
            def _(pool):
                def gather(g, u):
                    pool.wait_ge(idx_ready, g + 1)
                    own_waits(pool, m)
                    for j in range(G):
                        pool.indirect_dma_start(got[u][:, j, :], None, m.head_table[:, :],
                                                bass.IndirectOffsetOnAxis(ap=idx[u][:, j:j + 1], axis=0)).then_inc(landed[u], 16)

                with pool.Fori(0, turns) as i:
                    for u in range(2):
                        gather(2 * i + u, u)

            @block.tensor
            def _(pe):
                def source_scores(g, u):
                    tiles = tiles_of(pe, g)
                    pe.wait_ge(hot16_ready, g + 1)
                    for j in range(G):
                        last = nc.tensor.transpose(t_ps[0:LANES, j, :], hot16[u][:, j, :], m.ident16[:])
                    last.then_inc(turned, 1)
                    pe.wait_ge(turned_in, g + 1)
                    if not isinstance(g, int) or g > 0:
                        pe.wait_ge(parts_summed, g)
                    for j in range(G):
                        last = nc.tensor.matmul(sl_ps[:, j * 3 * HEADS:(j + 1) * 3 * HEADS], hot_t[u][:, j, :],
                                                sl[:, tiles[j * UN // G], :], start=True, stop=True)
                    last.then_inc(sl_up, 1)

                def scatter(g, u, wait_added=True):
                    pe.wait_ge(hot_ready, g + 1)
                    pe.wait_ge(scaled, g + 1)
                    if wait_added:
                        pe.wait_ge(added, (g - 1) * UN)
                    for j in range(G):
                        last = nc.tensor.matmul(s_ps[u][0:LANES, j * UN // G, 0:ROW], hot[u][:, j, :], w[u][:, j, :],
                                                start=j % (G // UN) == 0, stop=j % (G // UN) == G // UN - 1)
                    last.then_inc(scattered, 1)

                source_scores(0, 0)
                for u in range(2):
                    source_scores(1 + u, 1 - u)
                    scatter(u, u, False)
                with pe.Fori(1, turns - 1) as i:
                    for u in range(2):
                        source_scores(2 * i + (u + 1), 1 - u)
                        scatter(2 * i + u, u)
                source_scores(groups - 1, 1)
                scatter(groups - 2, 0)
                scatter(groups - 1, 1)

            @block.scalar
            def _(act):
                def one_group(g, u, begun=True):
                    act.wait_ge(turned, g + 1)
                    nc.scalar.activation(hot_t[u][:], t_ps[0:LANES, :, :], ACT.Copy).then_inc(turned_in, 1)
                    if begun:
                        act.wait_ge(scattered, g - 1)
                    nc.scalar.activation(hot[u][:], hot16[u][:], ACT.Copy).then_inc(hot_ready, 1)
                    act.wait_ge(lrelu_ready, g + 1)
                    nc.scalar.activation(e[u][:], lrelu[u][:], ACT.Exp, scale=-1.0).then_inc(e_ready, 1)

                for u in range(2):
                    one_group(u, u, False)
                with act.Fori(1, turns) as i:
                    for u in range(2):
                        one_group(2 * i + u, u)

            @block.vector
            def _(dve):
                def stage_idx(g, u):
                    nc.vector.tensor_copy(idx[u][:], r.other[:, bass.DynSlice(g * G, G)]).then_inc(idx_ready, 1)

                def one_hots(g, u):
                    for j in range(G):
                        last = nc.vector.tensor_scalar(hot16[u][:, j, :], m.count16[:, 0:LANES],
                                                       r.lane[:, bass.DynSlice(g * G + j, 1)], None, ALU.is_equal)
                    last.then_inc(hot16_ready, 1)

                def logits(g, u):
                    dve.wait_ge(sl_up, g + 1)
                    nc.vector.tensor_reduce(parts[u][:], sl_ps[:, 0:3 * G * HEADS].rearrange("p (j s h) -> p j h s", s=3, h=HEADS),
                                            AX_X, ALU.add).then_inc(parts_summed, 1)
                    dve.wait_ge(parts_summed, g + 1)
                    dve.wait_ge(landed[u], (g - u) * (8 * G) + 16 * G)
                    nc.vector.tensor_tensor(z[u][:], parts[u][:], got[u][:, :, DIM:ROW], ALU.add).then_inc(logit, 1)
                    dve.wait_ge(logit, g + 1)
                    nc.vector.scalar_tensor_tensor(lrelu[u][:], z[u][:], NEG_SLOPE, z[u][:], ALU.mult, ALU.max).then_inc(lrelu_ready, 1)

                def scale_rows(g, u):
                    dve.wait_ge(e_ready, g + 1)
                    nc.vector.tensor_tensor(w[u][:, :, 0:DIM].rearrange("p j (h c) -> p j h c", h=HEADS),
                                            got[u][:, :, 0:DIM].rearrange("p j (h c) -> p j h c", h=HEADS),
                                            e[u][:].unsqueeze(3).to_broadcast([P, G, HEADS, HEAD_C]), ALU.mult)
                    nc.vector.tensor_copy(w[u][:, :, DIM:ROW], e[u][:]).then_inc(scaled, 1)

                def accumulate(g, u, first=False):
                    tiles = tiles_of(dve, g)
                    dve.wait_ge(scattered, g + 1)
                    for n, tile in enumerate(tiles):
                        if not first or n > 0:
                            dve.wait_ge(added, g * UN + n)
                        dve.tensor_tensor(acc[:, tile, :], s_ps[u][0:LANES, n, 0:ROW], acc[:, tile, :], ALU.add).then_inc(added, 1)

                def one_group(g, u, after=2, start=False, first=False):
                    if after > 0:
                        if not start:
                            dve.wait_ge(hot_ready, g)
                        one_hots(g + 1, 1 - u)
                    scale_rows(g, u)
                    if after > 1:
                        stage_idx(g + 2, u)
                    if not start:
                        accumulate(g - 1, 1 - u, first)
                    if after > 0:
                        logits(g + 1, 1 - u)

                zeroed = sem("att_acc_zeroed")
                nc.vector.memset(acc[:], 0.0).then_inc(zeroed, 1)
                dve.wait_ge(zeroed, 1)
                for u in range(2):
                    stage_idx(u, u)
                one_hots(0, 0)
                logits(0, 0)
                one_group(0, 0, start=True)
                one_group(1, 1, first=True)
                with dve.Fori(1, turns - 1) as i:
                    for u in range(2):
                        one_group(2 * i + u, u)
                one_group(groups - 2, 0, after=1)
                one_group(groups - 1, 1, after=0)
                accumulate(groups - 1, 1)


def attention_out(nc, sem, m, acc):
    low_ready = sem("atto_low_ready")
    exp_ready = sem("atto_exp_ready")
    with ExitStack() as ctx:
        def sb(n, shape, dt=F32):
            return ctx.enter_context(nc.sbuf_tensor(f"atto_{n}", shape, dt))

        inv = sb("inv", [LANES, TILES, HEADS])
        low = sb("low", [LANES, TILES, DIM])
        feats = acc[:, :, 0:DIM]
        by_head = [LANES, TILES, HEADS, HEAD_C]
        with nc.Block() as block:

            @block.scalar
            def _(act):
                act.wait_ge(low_ready, 1)
                nc.scalar.activation(low[:], low[:], ACT.Exp).then_inc(exp_ready, 1)

            @block.vector
            def _(dve):
                chain = m.steps
                chain.link(nc.vector.reciprocal(inv[:], acc[:, :, DIM:ROW]))
                chain.link(nc.vector.tensor_tensor(feats.rearrange("p t (h c) -> p t h c", h=HEADS),
                                              feats.rearrange("p t (h c) -> p t h c", h=HEADS),
                                              inv[:].unsqueeze(3).to_broadcast(by_head), ALU.mult))
                nc.vector.tensor_scalar(low[:], feats, 0.0, None, ALU.min).then_inc(low_ready, 1)
                chain.link(nc.vector.scalar_tensor_tensor(m.x[:], feats, 0.0, m.x[:], ALU.max, ALU.add))
                dve.wait_ge(exp_ready, 1)
                chain.link(nc.vector.scalar_tensor_tensor(m.x[:], low[:], -1.0, m.x[:], ALU.add, ALU.add))


def graph_attention(nc, sem, m, io):
    with ExitStack() as ctx:
        def sb(n, shape, dt=F32):
            return ctx.enter_context(nc.sbuf_tensor(f"gat_{n}", shape, dt))

        r = Ends(sb("other", [P, PAIR_BLOCKS], I32), sb("lane", [P, PAIR_BLOCKS]), sb("tile_row", [1, PAIR_BLOCKS // 2], I32))
        sl = sb("sl", [LANES, TILES, HEADS])
        edge_tables(nc, sem, m, "by_src", m.src_i, m.dst_i, False,
                    Ends(r.other[:], r.lane[:], r.tile_row[:]), PAIR_BLOCKS, PAIR)
        layer_norm(nc, sem, m, "ln_c", m.x, m.y)
        attention_rows(nc, sem, m, io, sl)
        sl_parts = sb("sl_parts", [LANES, TILES, 3 * HEADS], BF16)
        split_scores(nc, sem, m, sl, sl_parts)
        acc = sb("acc", [LANES, TILES, ROW])
        attend_edges(nc, sem, m, r, sl_parts, acc)
        attention_out(nc, sem, m, acc)


class SliceState:
    def __init__(self, sb):
        self.weights = sb("weights", [LANES, TILES, INNER])
        self.mixed = sb("mixed", [P, PAIRS, DIM])
        self.b_out = sb("b_out", [LANES, DIM])
        self.tokens = sb("tokens", [P, PAIRS, P])
        self.norm = sb("norm", [P, PAIRS])


def slice_attention(nc, sem, m, io):
    with ExitStack() as ctx:
        def sb(n, shape, dt=F32):
            return ctx.enter_context(nc.sbuf_tensor(f"sa_{n}", shape, dt))

        layer_norm(nc, sem, m, "ln_d", m.x, m.y)
        s = SliceState(sb)
        slice_tokens(nc, sem, m, io, s)
        token_attention(nc, sem, m, io, s)
        slices_out(nc, sem, m, io, s)


def slice_tokens(nc, sem, m, io, s):
    in_ = sem("st_in")
    consts = sem("st_consts")
    staged = sem("st_staged")
    turned = sem("st_turned")
    turned_in = sem("st_turned_in")
    xm_up = sem("st_xm_up")
    xm_ready = sem("st_xm_ready")
    logits_up = sem("st_logits_up")
    chain_s = sem("st_chain")
    shifted = sem("st_shifted")
    exp_ready = sem("st_exp_ready")
    fx_up = sem("st_fx_up")
    fx_ready = sem("st_fx_ready")
    w_ready = sem("st_w_ready")
    summed = sem("st_summed")
    taken = sem("st_taken")
    with ExitStack() as ctx:
        def sb(n, shape, dt=F32):
            return ctx.enter_context(nc.sbuf_tensor(f"st_{n}", shape, dt))

        def ps(n, shape):
            return ctx.enter_context(nc.psum_tensor(f"st_{n}", shape, F32))

        wx = sb("wx", [P, KD, INNER])
        wf = sb("wf", [P, KD, INNER])
        bx = sb("bx", [P, PAIRS])
        bf = sb("bf", [LANES, INNER])
        ws = sb("ws", [P, P])
        bs = sb("bs", [LANES, SLICES])
        temp = sb("temp", [LANES, SA_HEADS])
        z = sb("z", [LANES, CHUNK, DIM])
        zt = sb("zt", [P, KD, CW])
        xm = sb("xm", [P, PAIRS, CW])
        fx = sb("fx", [LANES, INNER])
        lg = sb("lg", [LANES, INNER])
        w = sb("w", [LANES, INNER])
        big = sb("big", [LANES, SA_HEADS])
        total = sb("total", [LANES, SA_HEADS])
        ab_ps = ps("ab_ps", [P, 2, 512])
        lg_ps = ps("lg_ps", [P, 512])
        fx_ps = ps("fx_ps", [P, 512])
        tok_ps = ps("tok_ps", [P, PAIRS, 512])
        heads = [LANES, SA_HEADS, SLICES]

        def by_head(ap):
            return ap.rearrange("p (h g) -> p h g", h=SA_HEADS)

        with nc.Block() as block:

            @block.sync
            def _(sp):
                sp.wait_ge(consts, 1)
                sp.dma_start(wx[:], io["W_x"].rearrange("(k p) i -> p k i", p=P)).then_inc(in_, 16)
                sp.dma_start(wf[:], io["W_fx"].rearrange("(k p) i -> p k i", p=P)).then_inc(in_, 16)
                sp.dma_start(bx[:], io["b_x"]).then_inc(in_, 16)
                sp.dma_start(bf[:], io["b_fx"].partition_broadcast(LANES)).then_inc(in_, 16)
                for h in range(2):
                    part = slice(h * SA_D, (h + 1) * SA_D)
                    sp.dma_start(ws[part, part], io["W_slice"]).then_inc(in_, 16)
                sp.dma_start(bs[:], io["b_slice"].partition_broadcast(LANES)).then_inc(in_, 16)
                sp.dma_start(temp[:], io["temperature"].rearrange("a h b c -> (a h b c)").partition_broadcast(LANES)).then_inc(in_, 16)
                sp.dma_start(s.b_out[:], io["b_out"].partition_broadcast(LANES)).then_inc(in_, 16)

            @block.gpsimd
            def _(pool):
                nc.gpsimd.memset(ws[:], 0.0).then_inc(consts, 1)

            @block.tensor
            def _(pe):
                pe.wait_ge(in_, 144)
                with pe.Fori(0, CHUNKS) as c:
                    pe.wait_ge(staged, c + 1)
                    for t in range(CHUNK):
                        for k in range(KD):
                            last = nc.tensor.transpose(ab_ps[:, k, t * LANES:(t + 1) * LANES], z[:, t, k * P:(k + 1) * P],
                                                       m.ident[0:LANES, 0:LANES])
                    last.then_inc(turned, 1)
                    pe.wait_ge(turned_in, c + 1)
                    for p in range(PAIRS):
                        if p >= 2:
                            pe.wait_ge(xm_ready, c * PAIRS + (p - 1))
                        for k in range(KD):
                            last = nc.tensor.matmul(ab_ps[:, p % 2, 0:CW], wx[:, k, p * P:(p + 1) * P], zt[:, k, :],
                                                    start=k == 0, stop=k == KD - 1)
                        last.then_inc(xm_up, 1)
                    pe.wait_ge(xm_ready, c * PAIRS + PAIRS)
                    for t in range(CHUNK):
                        nodes = slice(t * LANES, (t + 1) * LANES)
                        for p in range(PAIRS):
                            last = nc.tensor.matmul(lg_ps[0:LANES, p * P:(p + 1) * P], xm[:, p, nodes], ws[:], start=True, stop=True)
                        last.then_inc(logits_up, 1)
                        for k in range(KD):
                            last = nc.tensor.matmul(fx_ps[0:LANES, :], zt[:, k, nodes], wf[:, k, :], start=k == 0, stop=k == KD - 1)
                        last.then_inc(fx_up, 1)
                        pe.wait_ge(fx_ready, c * CHUNK + (t + 1))
                        pe.wait_ge(w_ready, c * CHUNK + (t + 1))
                        for p in range(PAIRS):
                            part = slice(p * P, (p + 1) * P)
                            nc.tensor.matmul(tok_ps[:, p, 0:P], w[:, part], fx[:, part], start=True, stop=True)
                            last = nc.tensor.matmul(tok_ps[:, p, P:P + 1], w[:, part], m.ones[0:LANES, 0:1], start=True, stop=True)
                        last.then_inc(summed, 1)
                        pe.wait_ge(taken, 2 * (c * CHUNK + t) + 2)

            @block.scalar
            def _(act):
                act.wait_ge(in_, 144)
                with act.Fori(0, CHUNKS) as c:
                    for p in range(PAIRS):
                        act.wait_ge(xm_up, c * PAIRS + (p + 1))
                        nc.scalar.activation(xm[:, p, :], ab_ps[:, p % 2, 0:CW], ACT.Identity, bias=bx[:, p:p + 1]).then_inc(xm_ready, 1)
                    for t in range(CHUNK):
                        act.wait_ge(shifted, c * CHUNK + (t + 1))
                        nc.scalar.activation(lg[:], lg[:], ACT.Exp).then_inc(exp_ready, 1)

            @block.vector
            def _(dve):
                dve.wait_ge(in_, 144)
                setup = m.steps
                setup.link(nc.vector.memset(s.tokens[:], 0.0))
                setup.link(nc.vector.memset(s.norm[:], 0.0))
                setup.link(nc.vector.tensor_scalar(temp[:], temp[:], 0.1, 5.0, ALU.max, ALU.min))
                setup.link(nc.vector.reciprocal(temp[:], temp[:]))
                with dve.Fori(0, CHUNKS) as c:
                    nc.vector.tensor_copy(z[:], m.y[:, bass.DynSlice(c * CHUNK, CHUNK), :]).then_inc(staged, 1)
                    dve.wait_ge(turned, c + 1)
                    nc.vector.tensor_copy(zt[:], ab_ps[:, :, 0:CW]).then_inc(turned_in, 1)
                    for t in range(CHUNK):
                        tile = c * CHUNK + t
                        steps = [6 * tile + n for n in range(1, 7)]
                        dve.wait_ge(logits_up, tile + 1)
                        nc.vector.tensor_tensor(by_head(lg[:]), by_head(lg_ps[0:LANES, :]),
                                                bs[:].unsqueeze(1).to_broadcast(heads), ALU.add).then_inc(chain_s, 1)
                        dve.wait_ge(chain_s, steps[0])
                        nc.vector.tensor_tensor(by_head(lg[:]), by_head(lg[:]), temp[:].unsqueeze(2).to_broadcast(heads),
                                                ALU.mult).then_inc(chain_s, 1)
                        dve.wait_ge(chain_s, steps[1])
                        nc.vector.tensor_reduce(big[:], by_head(lg[:]), AX_X, ALU.max).then_inc(chain_s, 1)
                        dve.wait_ge(chain_s, steps[2])
                        nc.vector.tensor_tensor(by_head(lg[:]), by_head(lg[:]), big[:].unsqueeze(2).to_broadcast(heads),
                                                ALU.subtract).then_inc(shifted, 1)
                        dve.wait_ge(fx_up, tile + 1)
                        nc.vector.tensor_tensor(fx[:], fx_ps[0:LANES, :], bf[:], ALU.add).then_inc(fx_ready, 1)
                        dve.wait_ge(exp_ready, tile + 1)
                        nc.vector.tensor_reduce(total[:], by_head(lg[:]), AX_X, ALU.add).then_inc(chain_s, 1)
                        dve.wait_ge(chain_s, steps[3])
                        nc.vector.reciprocal(total[:], total[:]).then_inc(chain_s, 1)
                        dve.wait_ge(chain_s, steps[4])
                        nc.vector.tensor_tensor(by_head(w[:]), by_head(lg[:]), total[:].unsqueeze(2).to_broadcast(heads),
                                                ALU.mult).then_inc(w_ready, 1)
                        dve.wait_ge(w_ready, tile + 1)
                        nc.vector.tensor_copy(s.weights[:, bass.DynSlice(tile, 1), :], w[:].unsqueeze(1)).then_inc(chain_s, 1)
                        dve.wait_ge(summed, tile + 1)
                        nc.vector.tensor_tensor(s.tokens[:], tok_ps[:, :, 0:P], s.tokens[:], ALU.add).then_inc(taken, 1)
                        nc.vector.tensor_tensor(s.norm[:], tok_ps[:, :, P], s.norm[:], ALU.add).then_inc(taken, 1)


def token_attention(nc, sem, m, io, s):
    in_ = sem("ta_in")
    consts = sem("ta_consts")
    tok_ready = sem("ta_tok_ready")
    pe_up = sem("ta_pe_up")
    taken = sem("ta_taken")
    exp_in = sem("ta_exp_in")
    exp_ready = sem("ta_exp_ready")
    with ExitStack() as ctx:
        def sb(n, shape, dt=F32):
            return ctx.enter_context(nc.sbuf_tensor(f"ta_{n}", shape, dt))

        wq, wk, wv = (sb(n, [P, P]) for n in ("wq", "wk", "wv"))
        wo = sb("wo", [P, PAIRS, DIM])
        inv = sb("inv", [P, PAIRS])
        tok = sb("tok", [P, PAIRS, P])
        tok_t = sb("tok_t", [P, PAIRS, P])
        q_t = sb("q_t", [P, PAIRS, P])
        k_t = sb("k_t", [P, PAIRS, P])
        v = sb("v", [P, PAIRS, P])
        at = sb("at", [P, PAIRS, P])
        at_t = sb("at_t", [P, PAIRS, P])
        mix_t = sb("mix_t", [P, PAIRS, P])
        big = sb("big", [P, PAIRS])
        total = sb("total", [P, PAIRS])
        ps = [ctx.enter_context(nc.psum_tensor(f"ta_ps{n}", [P, PAIRS, P], F32)) for n in range(4)]
        mo_ps = ctx.enter_context(nc.psum_tensor("ta_mo_ps", [P, PAIRS, DIM], F32))
        halves = [slice(0, SA_D), slice(SA_D, P)]
        with nc.Block() as block:

            @block.sync
            def _(sp):
                sp.wait_ge(consts, 3)
                for w, wd in ((wq, io["W_q"]), (wk, io["W_k"]), (wv, io["W_v"])):
                    for part in halves:
                        sp.dma_start(w[part, part], wd).then_inc(in_, 16)
                sp.dma_start(wo[:], io["W_out"].rearrange("(k p) d -> p k d", p=P)).then_inc(in_, 16)

            @block.gpsimd
            def _(pool):
                for w in (wq, wk, wv):
                    nc.gpsimd.memset(w[:], 0.0).then_inc(consts, 1)

            @block.tensor
            def _(pe):
                pe.wait_ge(in_, 112)

                def pairwise(to, left, right, transpose=False):
                    for p in range(PAIRS):
                        if transpose:
                            last = nc.tensor.transpose(to[:, p, :], left(p), m.ident[:])
                        else:
                            last = nc.tensor.matmul(to[:, p, :], left(p), right(p), start=True, stop=True)
                    last.then_inc(pe_up, 1)

                pe.wait_ge(tok_ready, 1)
                pairwise(ps[0], lambda p: tok[:, p, :], None, True)
                pe.wait_ge(taken, 1)
                pairwise(ps[1], lambda p: wq[:], lambda p: tok_t[:, p, :])
                pairwise(ps[2], lambda p: wk[:], lambda p: tok_t[:, p, :])
                pairwise(ps[3], lambda p: tok_t[:, p, :], lambda p: wv[:])
                pe.wait_ge(taken, 3)
                pairwise(ps[0], lambda p: q_t[:, p, :], lambda p: k_t[:, p, :])
                pe.wait_ge(taken, 5)
                pairwise(ps[1], lambda p: at[:, p, :], None, True)
                pe.wait_ge(taken, 6)
                pairwise(ps[2], lambda p: v[:, p, :], lambda p: at_t[:, p, :])
                pe.wait_ge(taken, 7)
                for p in range(PAIRS):
                    last = nc.tensor.matmul(mo_ps[:, p, :], mix_t[:, p, :], wo[:, p, :], start=True, stop=True)
                last.then_inc(pe_up, 1)

            @block.scalar
            def _(act):
                act.wait_ge(exp_in, 1)
                for part in halves:
                    last = nc.scalar.activation(at[part, :, part], at[part, :, part], ACT.Exp)
                last.then_inc(exp_ready, 1)

            @block.vector
            def _(dve):
                chain = m.steps
                chain.link(nc.vector.tensor_scalar(inv[:], s.norm[:], 1e-5, None, ALU.add))
                chain.link(nc.vector.reciprocal(inv[:], inv[:]))
                chain.link(nc.vector.memset(tok[:], 0.0))
                chain.link(nc.vector.memset(at[:], 0.0))
                for part in halves:
                    chain.link(nc.vector.tensor_tensor(tok[part, :, part], s.tokens[part, :, part],
                                                  inv[part, :].unsqueeze(2).to_broadcast([SA_D, PAIRS, SA_D]), ALU.mult))
                nc.vector.memset(total[:], 0.0).then_inc(tok_ready, 1)
                for n, (to, src) in enumerate(((tok_t, ps[0]), (q_t, ps[1]), (k_t, ps[2]), (v, ps[3]))):
                    dve.wait_ge(pe_up, n + 1)
                    nc.vector.tensor_copy(to[:], src[:]).then_inc(taken, 1)
                dve.wait_ge(pe_up, 5)
                for part in halves:
                    wide = [SA_D, PAIRS, SA_D]
                    chain.link(nc.vector.tensor_scalar(at[part, :, part], ps[0][part, :, part], SA_D ** -0.5, None, ALU.mult))
                    chain.link(nc.vector.tensor_reduce(big[part, :], at[part, :, part], AX_X, ALU.max))
                    last = nc.vector.tensor_tensor(at[part, :, part], at[part, :, part], big[part, :].unsqueeze(2).to_broadcast(wide),
                                                   ALU.subtract)
                last.then_inc(exp_in, 1)
                dve.wait_ge(exp_ready, 1)
                for part in halves:
                    chain.link(nc.vector.tensor_reduce(total[part, :], at[part, :, part], AX_X, ALU.add))
                chain.link(nc.vector.reciprocal(total[:], total[:]))
                nc.vector.tensor_tensor(at[:], at[:], total[:].unsqueeze(2).to_broadcast([P, PAIRS, P]), ALU.mult).then_inc(taken, 1)
                dve.wait_ge(pe_up, 6)
                nc.vector.tensor_copy(at_t[:], ps[1][:]).then_inc(taken, 1)
                dve.wait_ge(pe_up, 7)
                nc.vector.tensor_copy(mix_t[:], ps[2][:]).then_inc(taken, 1)
                dve.wait_ge(pe_up, 8)
                nc.vector.tensor_copy(s.mixed[:], mo_ps[:]).then_inc(taken, 1)


def slices_out(nc, sem, m, io, s):
    staged = sem("so_staged")
    turned = sem("so_turned")
    turned_in = sem("so_turned_in")
    up = sem("so_up")
    taken = sem("so_taken")
    biased = sem("so_biased")
    with ExitStack() as ctx:
        w = [ctx.enter_context(nc.sbuf_tensor(f"so_w{u}", [LANES, INNER], F32)) for u in range(2)]
        w_t = [ctx.enter_context(nc.sbuf_tensor(f"so_w_t{u}", [P, PAIRS, P], F32)) for u in range(2)]
        t_ps = [ctx.enter_context(nc.psum_tensor(f"so_t_ps{u}", [P, PAIRS, P], F32)) for u in range(2)]
        o_ps = [ctx.enter_context(nc.psum_tensor(f"so_o_ps{u}", [P, 512], F32)) for u in range(2)]
        turns = TILES // 2
        with nc.Block() as block:

            @block.tensor
            def _(pe):
                with pe.Fori(0, turns) as i:
                    for u in range(2):
                        pe.wait_ge(staged, 2 * i + (u + 1))
                        for p in range(PAIRS):
                            last = nc.tensor.transpose(t_ps[u][:, p, 0:LANES], w[u][:, p * P:(p + 1) * P], m.ident[0:LANES, 0:LANES])
                        last.then_inc(turned, 1)
                    for u in range(2):
                        pe.wait_ge(turned_in, 2 * i + (u + 1))
                        for p in range(PAIRS):
                            last = nc.tensor.matmul(o_ps[u][0:LANES, 0:DIM], w_t[u][:, p, 0:LANES], s.mixed[:, p, :],
                                                    start=p == 0, stop=p == PAIRS - 1)
                        last.then_inc(up, 1)

            @block.scalar
            def _(act):
                with act.Fori(0, turns) as i:
                    for u in range(2):
                        act.wait_ge(turned, 2 * i + (u + 1))
                        nc.scalar.activation(w_t[u][:, :, 0:LANES], t_ps[u][:, :, 0:LANES], ACT.Copy).then_inc(turned_in, 1)

            @block.vector
            def _(dve):
                nc.vector.tensor_tensor(m.x[:], m.x[:], s.b_out[:].unsqueeze(1).to_broadcast([LANES, TILES, DIM]), ALU.add).then_inc(biased, 1)
                dve.wait_ge(biased, 1)

                def stage(t, u):
                    nc.vector.tensor_copy(w[u][:].unsqueeze(1), s.weights[:, bass.DynSlice(t, 1), :]).then_inc(staged, 1)

                def take(t, u):
                    one = bass.DynSlice(t, 1)
                    dve.wait_ge(up, t + 1)
                    nc.vector.tensor_tensor(m.x[:, one, :], o_ps[u][0:LANES, 0:DIM].unsqueeze(1), m.x[:, one, :], ALU.add).then_inc(taken, 1)

                for u in range(2):
                    stage(u, u)
                with dve.Fori(0, turns - 1) as i:
                    for u in range(2):
                        take(2 * i + u, u)
                        stage(2 * i + (u + 2), u)
                for u in range(2):
                    take(TILES - 2 + u, u)


def gather_and_update(nc, sem, m, io):
    with ExitStack() as ctx:
        def sb(n, shape, dt=F32):
            return ctx.enter_context(nc.sbuf_tensor(f"gine_{n}", shape, dt))

        m.edge_of_slot = sb("edge_of_slot", [P, EDGE_BLOCKS], I32)
        m.src_of_slot = sb("src_of_slot", [P, EDGE_BLOCKS], I32)
        m.dst_lane = sb("dst_lane", [P, EDGE_BLOCKS])
        m.dst_tile = sb("dst_tile", [1, EDGE_BLOCKS], I32)
        edge_tables(nc, sem, m, "by_dst", m.dst_i, m.src_i, True,
                    Ends(m.src_of_slot[:], m.dst_lane[:], m.dst_tile[:], edge=m.edge_of_slot[:]))
        m.acc = sb("acc", [LANES, TILES, DIM])
        layer_norm(nc, sem, m, "ln_a", m.x, m.y)
        node_table(nc, sem, m, "biased_table", m.y, m.acc, m.node_table, m.row_a[:, 0, :])
        edge_messages(nc, sem, m, io)
        node_mlp(nc, sem, m, io)


def store_output(nc, sem, m, out):
    stored = sem("out_stored")
    with nc.Block() as block:

        @block.sync
        def _(sp):
            sp.dma_start(out.rearrange("(p t) d -> p t d", t=TILES), m.x[:]).then_inc(stored, 16)
            sp.wait_ge(stored, 16)


def gnn_moe_gat_slice_kernel(nc, io_gine, io_moe, io_gat, io_slice, out):
    with ExitStack() as ctx:
        def sb(n, shape, dt=F32):
            return ctx.enter_context(nc.sbuf_tensor(n, shape, dt))

        def sem(n):
            return ctx.enter_context(nc.semaphore(n))

        m = Shared(nc, sb, sem)
        constants(nc, m, sem)
        load_inputs(nc, sem, m, io_gine)
        gather_and_update(nc, sem, m, io_gine)
        mixture(nc, sem, m, io_moe)
        graph_attention(nc, sem, m, io_gat)
        slice_attention(nc, sem, m, io_slice)
        store_output(nc, sem, m, out)


GINE = ["x", "src", "dst", "edge_attr_256"] + ["L0_gnn_" + n for n in
                                               ("We1", "be1", "We2", "be2", "Wn1", "bn1", "Wn2", "bn2", "eps")]
MOE = ["L0_ffn_" + n for n in ("gate_w", "gate_b", "w1", "w2", "w3")]
GAT = ["L1_gnn_" + n for n in ("W1", "a1", "W2", "a2")]
SLICE = ["L1_ffn_" + n for n in ("W_fx", "b_fx", "W_x", "b_x", "W_slice", "b_slice", "W_q", "W_k", "W_v", "W_out", "b_out",
                                 "temperature")]
BY_PARTITION = ("L0_gnn_be1", "L0_gnn_bn1", "L1_ffn_b_x")


def kernel(**inputs):
    import numpy as _np
    import concourse.bacc as _bacc
    from concourse import mybir as _mybir
    from concourse.bass_utils import run_bass_kernel_spmd as _run

    nc = _bacc.Bacc("TRN2", target_bir_lowering=False, num_devices=1)
    arrays, ios = {}, []
    for names in (GINE, MOE, GAT, SLICE):
        io = {}
        for name in names:
            a = _np.asarray(inputs[name])
            if name in BY_PARTITION:
                a = a.reshape(-1, P).T
            a = _np.ascontiguousarray(a)
            arrays[f"in_{name}_dram"] = a
            io[name.split("_", 2)[2] if name[0] == "L" else name] = nc.dram_tensor(
                f"in_{name}_dram", a.shape, _mybir.dt.from_np(a.dtype), kind="ExternalInput").ap()
        ios.append(io)
    out = nc.dram_tensor("out_0_dram", (N_NODES, DIM), F32, kind="ExternalOutput").ap()
    gnn_moe_gat_slice_kernel(nc, *ios, out)
    r = _run(nc, [arrays], core_ids=[0])
    return r.results[0]["out_0_dram"]
```

```python
from contextlib import ExitStack

import concourse.bass as bass
from concourse import mybir

F32 = mybir.dt.float32
F32R = mybir.dt.float32r
F16 = mybir.dt.float16
BF16 = mybir.dt.bfloat16
I32 = mybir.dt.int32
ALU = mybir.AluOpType
ACT = mybir.ActivationFunctionType
AX_X = mybir.AxisListType.X

N_NODES, DIM = 2500, 256
N_EDGES = 40000
P = 128
LANES = 125
TILES = N_NODES // LANES
EDGE_COLS = N_EDGES // LANES
KD = DIM // P
HID = 2 * DIM
KH = HID // P
LN_EPS = 1e-5

EXPERTS, TOP = 16, 2
GROUP = 4
EDGE_BLOCKS = -(-((N_EDGES + TILES * (P - 1)) // P) // GROUP) * GROUP
PAIR = 2 * P
PAIR_BLOCKS = -(-((N_EDGES + TILES * (PAIR - 1)) // PAIR * 2) // (2 * GROUP)) * 2 * GROUP
MOE_BLOCKS = -(-((N_NODES * TOP + EXPERTS * (P - 1)) // P) // 6) * 6
NODE_MID = N_NODES // 2
SIXTEENS_MID = N_EDGES // 16 // 2

HEADS, HEAD_C = 2, 128
NEG_SLOPE = 0.2
ROW = HEADS * (HEAD_C + 1)
SA_HEADS, SA_D, SLICES = 8, 64, 64
INNER = SA_HEADS * SA_D
PAIRS = INNER // P
ST = 2
SW = ST * LANES
STEPS = TILES // ST


def all_steps(eng, body):
    for n in range(2):
        body(n, n)
    with eng.Fori(1, STEPS // 2 - 1) as turn:
        for n in range(2):
            body(2 * turn + n, n)
    for n in range(STEPS - 2, STEPS):
        body(n, n % 2)


def begun(n, back):
    return not isinstance(n, int) or n >= back


def left(n, ahead, end=STEPS):
    return not isinstance(n, int) or n + ahead < end


class Slots:

    def __init__(self, pos, blk, tile_row):
        self.pos, self.blk, self.tile_row = pos, blk, tile_row


class Ends:

    def __init__(self, other, lane, tile_row, edge=None):
        self.other, self.lane, self.tile_row, self.edge = other, lane, tile_row, edge


class Chain:

    def __init__(self, eng, sem):
        self.eng, self.sem, self.n = eng, sem, 0

    def link(self, ins):
        self.n += 1
        ins.then_inc(self.sem, 1)
        self.eng.wait_ge(self.sem, self.n)


class Shared:

    def __init__(self, nc, sb, sem):
        self.constants_made = sem("constants_made")
        self.gathers_begun = sem("gathers_begun")
        self.rows_landed = sem("rows_landed")
        self.steps = Chain(nc.vector, sem("vector_steps"))
        self.norms = 0
        self.var_ready = sem("norm_var_ready")
        self.std_ready = sem("norm_std_ready")
        self.ident = sb("ident", [P, P])
        self.before = sb("before", [P, P])
        self.ones = sb("ones", [P, P])
        self.count_i = sb("count_i", [P, PAIR_BLOCKS], I32)
        self.count = sb("count", [P, PAIR_BLOCKS])
        self.count16 = sb("count16", [P, PAIR_BLOCKS], F16)
        self.ident16 = sb("ident16", [P, P], BF16)
        self.lane_i = sb("lane_i", [P, 1], I32)
        self.lane = sb("lane", [P, 1])
        self.node_i = sb("node_i", [LANES, TILES], I32)
        self.node = sb("node", [LANES, TILES])
        self.x = sb("x", [LANES, TILES, DIM])
        self.y = sb("y", [LANES, TILES, DIM])
        self.row_a = sb("row_a", [LANES, 2, DIM])
        self.stats = sb("stats", [LANES, TILES, 6])
        self.eps = sb("eps", [LANES, 1])
        self.dst_i = sb("dst_i", [LANES, EDGE_COLS], I32)
        self.src_i = sb("src_i", [LANES, EDGE_COLS], I32)
        self.node_table = nc.dram_tensor("node_table", [N_NODES, DIM], F32, kind="Internal").ap()
        self.routed = nc.dram_tensor("routed", [MOE_BLOCKS * P, DIM], F32, kind="Internal").ap()
        self.head_table = nc.dram_tensor("head_table", [N_NODES, ROW], F32, kind="Internal").ap()


def own_waits(pool, m):
    pool.sem_inc(m.gathers_begun, 1)


def constants(nc, m, sem):
    made = m.constants_made
    with nc.Block() as block:

        @block.gpsimd
        def _(pool):
            chain = Chain(pool, made)
            chain.link(pool.memset(m.ident[:], 0.0))
            chain.link(pool.affine_select(out=m.ident[:], in_=m.ident[:], compare_op=ALU.not_equal, fill=1.0,
                                     base=0, pattern=[[-1, P]], channel_multiplier=1))
            chain.link(pool.memset(m.before[:], 1.0))
            chain.link(pool.affine_select(out=m.before[:], in_=m.before[:], compare_op=ALU.is_gt, fill=0.0,
                                     base=0, pattern=[[1, P]], channel_multiplier=-1))
            chain.link(pool.memset(m.ones[:], 1.0))
            chain.link(pool.iota(m.count_i[:], pattern=[[1, PAIR_BLOCKS]], base=0, channel_multiplier=0))
            chain.link(pool.iota(m.lane_i[:], pattern=[[0, 1]], base=0, channel_multiplier=1))
            chain.link(pool.iota(m.node_i[:], pattern=[[1, TILES]], base=0, channel_multiplier=TILES))

        @block.vector
        def _(dve):
            dve.wait_ge(made, 8)
            nc.vector.tensor_copy(m.ident16[:], m.ident[:])
            nc.vector.tensor_copy(m.count[:], m.count_i[:])
            nc.vector.tensor_copy(m.count16[:], m.count_i[:])
            nc.vector.tensor_copy(m.lane[:], m.lane_i[:])
            nc.vector.tensor_copy(m.node[:], m.node_i[:])


def slots_of_buckets(nc, sem, m, name, bucket, cols, buckets, blocks, out, unit=P):
    units = blocks * P // unit
    counted = sem(name + "_counted")
    summed = sem(name + "_summed")
    with ExitStack() as ctx:
        def sb(n, shape, dt=F32):
            return ctx.enter_context(nc.sbuf_tensor(f"{name}_{n}", shape, dt))

        mask = sb("mask", [LANES, buckets, cols])
        seen = sb("seen", [LANES, buckets, cols])
        ends = sb("ends", [LANES, buckets + 1])
        mine = sb("mine", [LANES, buckets])
        nblk = sb("nblk", [LANES, buckets])
        nblk_i = sb("nblk_i", [LANES, buckets], I32)
        last = sb("last", [LANES, buckets])
        off = sb("off", [LANES, buckets])
        slot = sb("slot", [LANES, cols])
        slot_i = sb("slot_i", [LANES, cols], I32)
        part_i = sb("part_i", [LANES, cols], I32)
        past = sb("past", [1, units, buckets])
        tile_f = sb("tile_f", [1, units])
        sums = ctx.enter_context(nc.psum_tensor(name + "_sums", [P, 2, 512], F32))
        with nc.Block() as block:

            @block.tensor
            def _(pe):
                pe.wait_ge(counted, 1)
                nc.tensor.matmul(sums[0:LANES, 0, 0:buckets], m.before[0:LANES, 0:LANES], mine[:], start=True, stop=True)
                nc.tensor.matmul(sums[0:LANES, 1, 0:buckets], m.ones[0:LANES, 0:LANES], mine[:], start=True, stop=True).then_inc(summed, 1)

            @block.vector
            def _(dve):
                chain = m.steps
                chain.link(nc.vector.memset(ends[:], 0.0))
                for b in range(buckets):
                    last_mask = nc.vector.tensor_scalar(mask[:, b, :], bucket, float(b), None, ALU.is_equal)
                chain.link(last_mask)
                flat = mask[:].rearrange("p b c -> p (b c)")
                chain.link(nc.vector.tensor_tensor_scan(seen[:].rearrange("p b c -> p (b c)"), flat, flat, 0.0, ALU.add, ALU.max))
                chain.link(nc.vector.tensor_copy(ends[:, 1:], seen[:, :, cols - 1]))
                nc.vector.tensor_tensor(mine[:], ends[:, 1:], ends[:, 0:buckets], ALU.subtract).then_inc(counted, 1)
                dve.wait_ge(summed, 1)
                chain.link(nc.vector.tensor_scalar(nblk_i[:], sums[0:LANES, 1, 0:buckets], (unit - 1) / 2, 1 / unit, ALU.add, ALU.mult))
                chain.link(nc.vector.tensor_copy(nblk[:], nblk_i[:]))
                chain.link(nc.vector.tensor_tensor_scan(last[:], nblk[:], nblk[:], 0.0, ALU.add, ALU.max))
                chain.link(nc.vector.tensor_tensor(off[:], last[:], nblk[:], ALU.subtract))
                chain.link(nc.vector.tensor_scalar(off[:], off[:], float(unit), -1.0, ALU.mult, ALU.add))
                chain.link(nc.vector.tensor_tensor(off[:], off[:], sums[0:LANES, 0, 0:buckets], ALU.add))
                chain.link(nc.vector.tensor_tensor(off[:], off[:], ends[:, 0:buckets], ALU.subtract))
                for b in range(buckets):
                    last_slots = nc.vector.scalar_tensor_tensor(seen[:, b, :], seen[:, b, :], off[:, b:b + 1], mask[:, b, :], ALU.add, ALU.mult)
                chain.link(last_slots)
                chain.link(nc.vector.tensor_reduce(slot[:], seen[:].rearrange("p b c -> p c b"), AX_X, ALU.add))
                chain.link(nc.vector.tensor_copy(slot_i[:], slot[:]))
                chain.link(nc.vector.tensor_scalar(part_i[:], slot_i[:], 7, None, ALU.arith_shift_right))
                chain.link(nc.vector.tensor_copy(out.blk, part_i[:]))
                chain.link(nc.vector.tensor_scalar(slot_i[:], slot_i[:], P - 1, None, ALU.bitwise_and))
                chain.link(nc.vector.tensor_copy(out.pos, slot_i[:]))
                chain.link(nc.vector.tensor_tensor(
                    past[:], m.count[0:1, 0:units].unsqueeze(2).to_broadcast([1, units, buckets]),
                    last[0:1, :].unsqueeze(1).to_broadcast([1, units, buckets]), ALU.is_ge))
                chain.link(nc.vector.tensor_reduce(tile_f[:], past[:], AX_X, ALU.add))
                chain.link(nc.vector.tensor_scalar(out.tile_row, tile_f[:], float(buckets - 1), None, ALU.min))


class Placing:

    def __init__(self, nc, sem, ctx, m, name, pos, blk, values, cols, blocks, bufs):
        self.nc, self.m, self.pos, self.blk, self.values = nc, m, pos, blk, values
        self.cols, self.blocks, self.bufs = cols, blocks, bufs
        self.nv = len(values)
        self.on_dve = self.nv % 2
        self.hot_made = sem(name + "_hot_made")
        self.made = sem(name + "_made")
        self.scaled = sem(name + "_scaled")
        self.used = sem(name + "_used")
        self.hot = [ctx.enter_context(nc.sbuf_tensor(f"{name}_hot{u}", [LANES, P], F16)) for u in range(bufs)]
        self.rows = [ctx.enter_context(nc.sbuf_tensor(f"{name}_rows{u}", [LANES, self.nv, P], F16)) for u in range(bufs)]
        self.which = [ctx.enter_context(nc.sbuf_tensor(f"{name}_which{u}", [LANES, blocks], F16)) for u in range(bufs)]
        self.tables = ctx.enter_context(nc.psum_tensor(name + "_tables", [P, self.nv, 512], F32))

    def make(self, dve, c, u, begun=True):
        one = bass.DynSlice(c, 1)
        places = self.m.count16[0:LANES, 0:P]
        if begun:
            dve.wait_ge(self.used, c + (1 - self.bufs))
        self.nc.vector.tensor_scalar(self.hot[u][:], places, self.pos[:, one], None, ALU.is_equal).then_inc(self.hot_made, 1)
        for v in range(self.on_dve):
            self.nc.vector.tensor_scalar(self.rows[u][:, v, :], places, self.pos[:, one], self.values[v][:, one], ALU.is_equal, ALU.mult)
        self.nc.vector.tensor_scalar(self.which[u][:], self.m.count16[0:LANES, 0:self.blocks], self.blk[:, one], None,
                                     ALU.is_equal).then_inc(self.made, 1)

    def scale(self, act, c, u, begun=True):
        if self.on_dve == self.nv:
            return
        act.wait_ge(self.hot_made, c + 1)
        if begun:
            act.wait_ge(self.used, c + (1 - self.bufs))
        for v in range(self.on_dve, self.nv):
            last = self.nc.scalar.activation(self.rows[u][:, v, :], self.hot[u][:], ACT.Copy, scale=self.values[v][:, bass.DynSlice(c, 1)])
        last.then_inc(self.scaled, 1)

    def multiply(self, pe, c, u, start=False, stop=False):
        pe.wait_ge(self.made, c + 1)
        if self.on_dve < self.nv:
            pe.wait_ge(self.scaled, c + 1)
        for v in range(self.nv):
            last = self.nc.tensor.matmul(self.tables[:, v, 0:self.blocks], self.rows[u][:, v, :], self.which[u][:], start=start, stop=stop)
        last.then_inc(self.used, 1)


def place_in_slots(nc, sem, m, name, pos, blk, values, cols, blocks, finish, bufs=8):
    with ExitStack() as ctx:
        p = Placing(nc, sem, ctx, m, name, pos, blk, values, cols, blocks, bufs)
        assert cols % bufs == 0
        with nc.Block() as block:

            @block.vector
            def _(dve):
                for u in range(bufs):
                    p.make(dve, u, u, begun=False)
                with dve.Fori(1, cols // bufs) as i:
                    for u in range(bufs):
                        p.make(dve, i * bufs + u, u)
                dve.wait_ge(p.used, cols)
                finish(dve, m.steps, p.tables)

            @block.scalar
            def _(act):
                for u in range(bufs):
                    p.scale(act, u, u, begun=False)
                if p.on_dve < p.nv:
                    with act.Fori(1, cols // bufs) as i:
                        for u in range(bufs):
                            p.scale(act, i * bufs + u, u)

            @block.tensor
            def _(pe):
                for u in range(bufs):
                    p.multiply(pe, u, u, start=u == 0)
                with pe.Fori(1, cols // bufs - 1) as i:
                    for u in range(bufs):
                        p.multiply(pe, i * bufs + u, u)
                for u in range(bufs):
                    p.multiply(pe, cols - bufs + u, u, stop=u == bufs - 1)


def layer_norm(nc, sem, m, name, x, y, with_stats=True):
    m.norms += 1
    with ExitStack() as ctx:
        mv = ctx.enter_context(nc.sbuf_tensor(name + "_mv", [LANES, TILES, 2], F32))
        var = ctx.enter_context(nc.sbuf_tensor(name + "_var", [LANES, TILES], F32))
        std = ctx.enter_context(nc.sbuf_tensor(name + "_std", [LANES, TILES], F32))
        rstd = ctx.enter_context(nc.sbuf_tensor(name + "_rstd", [LANES, TILES], F32))
        with nc.Block() as block:

            @block.scalar
            def _(act):
                act.wait_ge(m.var_ready, m.norms)
                nc.scalar.activation(std[:], var[:], ACT.Sqrt).then_inc(m.std_ready, 1)

            @block.vector
            def _(dve):
                if with_stats:
                    for t in range(TILES):
                        last = nc.vector.bn_stats(m.stats[:, t, :], x[:, t, :])
                    m.steps.link(last)
                for t in range(TILES):
                    last = nc.vector.bn_aggr(mv[:, t, :], m.stats[:, t, :])
                m.steps.link(last)
                nc.vector.tensor_scalar(var[:], mv[:, :, 1], LN_EPS, None, ALU.add).then_inc(m.var_ready, 1)
                dve.wait_ge(m.std_ready, m.norms)
                m.steps.link(nc.vector.reciprocal(rstd[:], std[:]))
                for t in range(TILES):
                    nc.vector.tensor_scalar(y[:, t, :], x[:, t, :], mv[:, t, 0:1], rstd[:, t:t + 1],
                                            ALU.subtract, ALU.mult)


def split_rounded(nc, chain, whole, high, low):
    chain.link(nc.vector.tensor_copy(high, whole))
    return nc.vector.tensor_tensor(low, whole, high.bitcast(F32), ALU.subtract)


def split_product(pe, out, left, right, start, stop):
    (lh, ll), (rh, rl) = left, right
    pe.matmul(out, ll, rh, start=start, stop=False)
    pe.matmul(out, lh, rl, start=False, stop=False)
    return pe.matmul(out, lh, rh, start=False, stop=stop)


def edge_messages(nc, sem, m, io):
    w_in = sem("edge_weights_in")
    weights_split = sem("edge_weights_split")
    table_rows_ready = sem("edge_table_rows_ready")
    table_stored = sem("edge_table_stored")
    zeroed = sem("edge_acc_zeroed")
    edge_idx_ready = sem("edge_edge_idx_ready")
    node_idx_ready = sem("edge_node_idx_ready")
    ea_landed = [sem(f"edge_ea_landed{u}") for u in range(2)]
    nf_landed = [sem(f"edge_nf_landed{u}") for u in range(2)]
    turned = sem("edge_turned")
    eat_high_ready = sem("edge_eat_high_ready")
    eat_ready = sem("edge_eat_ready")
    hid_up = sem("edge_hid_up")
    hid_whole = sem("edge_hid_whole")
    even_high_ready = sem("edge_even_high_ready")
    odd_high_ready = sem("edge_odd_high_ready")
    hid_ready = sem("edge_hid_ready")
    e_up = sem("edge_e_up")
    summed = sem("edge_msg_summed")
    msg_high_ready = sem("edge_msg_high_ready")
    msg_ready = sem("edge_msg_ready")
    hot_ready = sem("edge_hot_ready")
    scattered = sem("edge_scattered")
    added = sem("edge_added")
    G = GROUP
    groups = EDGE_BLOCKS // G
    tail = (groups - 3) // 2 * 2
    with ExitStack() as ctx:
        def sb(n, shape, dt=F32):
            return ctx.enter_context(nc.sbuf_tensor(f"edge_{n}", shape, dt))

        def parts(n, shape):
            return sb(n + "_high", shape, F32R), sb(n + "_low", shape, F32R)

        def ps(n, shape):
            return ctx.enter_context(nc.psum_tensor(f"edge_{n}", shape, F32))

        table_rows = sb("table_rows", [LANES, TILES, DIM])
        w1 = sb("w1", [P, KD, HID])
        w1h, w1l = parts("w1", [P, KD, HID])
        b1 = sb("b1", [P, KH])
        w2 = sb("w2", [P, KH, DIM])
        w2h, w2l = parts("w2", [P, KH, DIM])
        edge_idx = [sb(f"edge_idx{u}", [P, G], I32) for u in range(2)]
        node_idx = [sb(f"node_idx{u}", [P, G], I32) for u in range(2)]
        ea = [sb(f"ea{u}", [P, G, DIM]) for u in range(2)]
        nf = [sb(f"nf{u}", [P, G, DIM]) for u in range(2)]
        eath, eatl = parts("eat", [P, KD, G * P])
        whole = [sb(f"whole{c}", [P, G * P]) for c in range(KH)]
        hidh, hidl = parts("hid", [P, KH, G * P])
        pre = sb("pre", [P, G, DIM])
        msgh, msgl = parts("msg", [P, G, DIM])
        hot = sb("hot", [P, G, P], F32R)
        t_ps = ps("t_ps", [P, KD, G * P])
        h_ps = ps("h_ps", [P, 2, G * P])
        e_ps = ps("e_ps", [P, G, DIM])
        s_ps = ps("s_ps", [P, G, DIM])

        with nc.Block() as block:

            @block.sync
            def _(sp):
                sp.dma_start(w1[:], io["We1"].rearrange("(k p) h -> p k h", p=P)).then_inc(w_in, 16)
                sp.dma_start(w2[:], io["We2"].rearrange("(k p) h -> p k h", p=P)).then_inc(w_in, 16)
                sp.dma_start(b1[:], io["be1"]).then_inc(w_in, 16)
                sp.wait_ge(table_rows_ready, 1)
                sp.dma_start(m.node_table.rearrange("(p t) d -> p t d", t=TILES), table_rows[:]).then_inc(table_stored, 16)

            def gather_edges(u):
                own_waits(nc.gpsimd, m)
                for j in range(G):
                    nc.gpsimd.indirect_dma_start(ea[u][:, j, :], None, io["edge_attr_256"][:, :],
                                                 bass.IndirectOffsetOnAxis(ap=edge_idx[u][:, j:j + 1], axis=0)).then_inc(ea_landed[u], 16)

            def gather_nodes(u):
                own_waits(nc.gpsimd, m)
                for j in range(G):
                    nc.gpsimd.indirect_dma_start(nf[u][:, j, :], None, m.node_table[:, :],
                                                 bass.IndirectOffsetOnAxis(ap=node_idx[u][:, j:j + 1], axis=0)).then_inc(nf_landed[u], 16)

            @block.gpsimd
            def _(pool):
                def edges_then_nodes(g, u, wait_summed):
                    pool.wait_ge(edge_idx_ready, g + (u + 1))
                    pool.wait_ge(turned, g + (u - 1))
                    gather_edges(u)
                    pool.wait_ge(node_idx_ready, g + u)
                    if wait_summed:
                        pool.wait_ge(summed, g + (u - 2))
                    gather_nodes(1 - u)

                for u in range(2):
                    pool.wait_ge(edge_idx_ready, u + 1)
                    gather_edges(u)
                pool.wait_ge(node_idx_ready, 1)
                pool.wait_ge(table_stored, 16)
                gather_nodes(0)
                edges_then_nodes(2, 0, False)
                edges_then_nodes(2, 1, True)
                with pool.Fori(2, groups // 2) as turn:
                    for u in range(2):
                        edges_then_nodes(turn * 2, u, True)
                if groups % 2:
                    edges_then_nodes(groups - 1, 0, True)
                pool.wait_ge(node_idx_ready, groups)
                pool.wait_ge(summed, groups - 2)
                gather_nodes((groups - 1) % 2)

            def transposes(u, landed):
                pe = nc.tensor
                pe.wait_ge(ea_landed[u], landed)
                for j in range(G):
                    for k in range(KD):
                        last = pe.transpose(t_ps[:, k, j * P:(j + 1) * P], ea[u][:, j, k * P:(k + 1) * P], m.ident[:])
                last.then_inc(turned, 1)

            def hidden(g, first=False):
                pe = nc.tensor
                pe.wait_ge(eat_ready, g + 1)
                for c in range(KH):
                    if not (first and c < 2):
                        pe.wait_ge(hid_whole, g * KH + (c - 1))
                    piece = slice(c * P, (c + 1) * P)
                    for k in range(KD):
                        last = split_product(pe, h_ps[:, c % 2, :], (w1h[:, k, piece], w1l[:, k, piece]),
                                             (eath[:, k, :], eatl[:, k, :]), start=k == 0, stop=k == KD - 1)
                    last.then_inc(hid_up, 1)

            def edges_out(g, first=False):
                pe = nc.tensor
                if not first:
                    pe.wait_ge(summed, g)
                for j in range(G):
                    rows = slice(j * P, (j + 1) * P)
                    for k in range(KH):
                        if j == 0:
                            pe.wait_ge(hid_ready, g * KH + (k + 1))
                        last = split_product(pe, e_ps[:, j, :], (hidh[:, k, rows], hidl[:, k, rows]),
                                             (w2h[:, k, :], w2l[:, k, :]), start=k == 0, stop=k == KH - 1)
                last.then_inc(e_up, 1)

            def scatter(g, first=False):
                pe = nc.tensor
                pe.wait_ge(hot_ready, 2 * g + 1)
                if not first:
                    pe.wait_ge(added, g * G)
                pe.wait_ge(msg_ready, g + 1)
                for j in range(G):
                    pe.matmul(s_ps[:, j, :], hot[:, j, :], msgl[:, j, :], start=True, stop=False)
                    last = pe.matmul(s_ps[:, j, :], hot[:, j, :], msgh[:, j, :], start=False, stop=True)
                last.then_inc(scattered, 1)

            @block.tensor
            def _(pe):
                transposes(0, 16 * G)
                pe.wait_ge(weights_split, 2)
                hidden(0, first=True)
                transposes(1, 16 * G)
                edges_out(0, first=True)
                hidden(1)
                transposes(0, 2 * 16 * G)
                scatter(0, first=True)
                edges_out(1)
                with pe.Fori(1, tail // 2) as turn:
                    g = turn * 2
                    for u in range(2):
                        hidden(g + u)
                        transposes(1 - u, (g + 2 * u) * (8 * G) + 16 * G)
                        scatter(g + (u - 1))
                        edges_out(g + u)
                for g in range(tail, groups):
                    hidden(g)
                    if g + 1 < groups:
                        transposes((g + 1) % 2, ((g + 1) // 2 + 1) * 16 * G)
                    scatter(g - 1)
                    edges_out(g)
                scatter(groups - 1)

            def eat_high(g):
                act = nc.scalar
                act.wait_ge(turned, g + 1)
                act.activation(eath[:], t_ps[:], ACT.Copy).then_inc(eat_high_ready, 1)

            def hidden_relu(g, c, first=False):
                act = nc.scalar
                act.wait_ge(hid_up, g * KH + (c + 1))
                act.activation(whole[c][:], h_ps[:, c % 2, :], ACT.Relu, bias=b1[:, c:c + 1]).then_inc(hid_whole, 1)

            def even_high(g, c):
                act = nc.scalar
                act.wait_ge(hid_whole, g * KH + (c + 1))
                act.activation(hidh[:, c, :], whole[c][:], ACT.Copy).then_inc(even_high_ready, 1)

            def message_high(g):
                act = nc.scalar
                act.wait_ge(summed, g + 1)
                act.activation(msgh[:], pre[:], ACT.Relu).then_inc(msg_high_ready, 1)

            def act_group(g, first=False, ahead=True):
                for c in range(KH):
                    hidden_relu(g, c, first)
                    if c == 1 and not first:
                        message_high(g - 1)
                    if c % 2 == 0:
                        even_high(g, c)
                if ahead:
                    eat_high(g + 1)

            @block.scalar
            def _(act):
                act.wait_ge(w_in, 48)
                eat_high(0)
                act_group(0, first=True)
                act_group(1)
                with act.Fori(1, tail // 2) as turn:
                    for u in range(2):
                        act_group(turn * 2 + u)
                for g in range(tail, groups):
                    act_group(g, ahead=g + 1 < groups)
                message_high(groups - 1)

            def stage_edge_idx(u, g):
                nc.vector.tensor_copy(edge_idx[u][:], m.edge_of_slot[:, bass.DynSlice(g * G, G)]).then_inc(edge_idx_ready, 1)

            def stage_node_idx(u, g):
                nc.vector.tensor_copy(node_idx[u][:], m.src_of_slot[:, bass.DynSlice(g * G, G)]).then_inc(node_idx_ready, 1)

            def eat_low(g):
                nc.vector.wait_ge(eat_high_ready, g + 1)
                nc.vector.tensor_tensor(eatl[:], t_ps[:], eath[:].bitcast(F32), ALU.subtract).then_inc(eat_ready, 1)

            def hidden_low(g, c):
                if c % 2 == 0:
                    nc.vector.wait_ge(even_high_ready, g * (KH // 2) + (c // 2 + 1))
                else:
                    nc.vector.wait_ge(hid_whole, g * KH + (c + 1))
                    nc.vector.tensor_copy(hidh[:, c, :], whole[c][:]).then_inc(odd_high_ready, 1)
                    nc.vector.wait_ge(odd_high_ready, g * (KH // 2) + (c // 2 + 1))
                nc.vector.tensor_tensor(hidl[:, c, :], whole[c][:], hidh[:, c, :].bitcast(F32), ALU.subtract).then_inc(hid_ready, 1)

            def add_nodes(u, g):
                nc.vector.wait_ge(e_up, g + 1)
                nc.vector.wait_ge(nf_landed[u], (g - u) * (8 * G) + 16 * G)
                nc.vector.tensor_tensor(pre[:], e_ps[:], nf[u][:], ALU.add).then_inc(summed, 1)

            def message_low(g):
                nc.vector.wait_ge(msg_high_ready, g + 1)
                nc.vector.scalar_tensor_tensor(msgl[:], pre[:], 0.0, msgh[:].bitcast(F32), ALU.max, ALU.subtract).then_inc(msg_ready, 1)

            def one_hots(g, blocks):
                for j in blocks:
                    last = nc.vector.tensor_scalar(hot[:, j, :], m.count[:, 0:P],
                                                   m.dst_lane[:, bass.DynSlice(g * G + j, 1)], None, ALU.is_equal)
                last.then_inc(hot_ready, 1)

            def tile_of(g, j):
                return nc.vector.value_load(m.dst_tile[0:1, bass.DynSlice(g * G + j, 1)], min_val=0, max_val=TILES - 1)

            def accumulate(g, j, tile, first=False):
                if not first or j > 0:
                    nc.vector.wait_ge(added, g * G + j)
                nc.vector.tensor_tensor(m.acc[:, tile, :], s_ps[0:LANES, j, :], m.acc[:, tile, :], ALU.add).then_inc(added, 1)

            @block.vector
            def _(dve):
                for u in range(2):
                    stage_edge_idx(u, u)
                    stage_node_idx(u, u)
                nc.vector.tensor_tensor(table_rows[:], m.y[:], m.row_a[:, 0, :].unsqueeze(1).to_broadcast([LANES, TILES, DIM]),
                                        ALU.add).then_inc(table_rows_ready, 1)
                dve.wait_ge(w_in, 48)
                split_rounded(nc, m.steps, w1[:], w1h[:], w1l[:]).then_inc(weights_split, 1)
                split_rounded(nc, m.steps, w2[:], w2h[:], w2l[:]).then_inc(weights_split, 1)
                eat_low(0)
                nc.vector.memset(m.acc[:], 0.0).then_inc(zeroed, 1)
                stage_edge_idx(0, 2)

                def one_group(g, u, ahead=3, first=False):
                    add_nodes(1 - u, g - 1)
                    if ahead > 0:
                        stage_node_idx(1 - u, g + 1)
                    tiles = [tile_of(g - 1, 0)]
                    hidden_low(g, 0)
                    tiles.append(tile_of(g - 1, 1))
                    hidden_low(g, 1)
                    message_low(g - 1)
                    tiles.append(tile_of(g - 1, 2))
                    hidden_low(g, 2)
                    tiles.append(tile_of(g - 1, 3))
                    hidden_low(g, 3)
                    dve.wait_ge(scattered, g)
                    accumulate(g - 1, 0, tiles[0], first)
                    one_hots(g, range(0, G // 2))
                    accumulate(g - 1, 1, tiles[1])
                    if ahead > 0:
                        eat_low(g + 1)
                    accumulate(g - 1, 2, tiles[2])
                    one_hots(g, range(G // 2, G))
                    accumulate(g - 1, 3, tiles[3])
                    if ahead > 2:
                        stage_edge_idx(1 - u, g + 3)

                for c in range(KH):
                    hidden_low(0, c)
                eat_low(1)
                stage_edge_idx(1, 3)
                one_hots(0, range(G))
                dve.wait_ge(zeroed, 1)
                one_group(1, 1, first=True)
                with dve.Fori(1, tail // 2) as turn:
                    for u in range(2):
                        one_group(turn * 2 + u, u)
                for g in range(tail, groups):
                    one_group(g, g % 2, ahead=min(3, groups - 1 - g))
                add_nodes((groups - 1) % 2, groups - 1)
                message_low(groups - 1)
                dve.wait_ge(scattered, groups)
                for j in range(G):
                    accumulate(groups - 1, j, tile_of(groups - 1, j))


def load_inputs(nc, sem, m, io):
    ends_landed = sem("ends_landed")
    with nc.Block() as block:

        @block.sync
        def _(sp):
            sp.dma_start(m.dst_i[:], io["dst"].rearrange("(p c) -> p c", c=EDGE_COLS)).then_inc(ends_landed, 16)
            sp.dma_start(m.src_i[:], io["src"].rearrange("(p c) -> p c", c=EDGE_COLS)).then_inc(ends_landed, 16)
            sp.dma_start(m.x[:], io["x"].rearrange("(p t) d -> p t d", t=TILES)).then_inc(m.rows_landed, 16)
            sp.dma_start(m.row_a[:, 0, :], io["be2"].partition_broadcast(LANES)).then_inc(m.rows_landed, 16)
            sp.dma_start(m.row_a[:, 1, :], io["bn2"].partition_broadcast(LANES)).then_inc(m.rows_landed, 16)
            sp.dma_start(m.eps[:], io["eps"].partition_broadcast(LANES)).then_inc(m.rows_landed, 16)
            sp.wait_ge(ends_landed, 32)


def wait_for_rows(nc, m):
    with nc.Block() as block:

        @block.sync
        def _(sp):
            sp.wait_ge(m.rows_landed, 64)


def node_table(nc, sem, m, name, y, table):
    stored = sem(name + "_stored")
    with nc.Block() as block:

        @block.sync
        def _(sp):
            sp.dma_start(table.rearrange("(p t) d -> p t d", t=TILES), y[:]).then_inc(stored, 16)
            sp.wait_ge(stored, 16)


class EdgeSort:

    def __init__(self, nc, ctx, name, with_edge, out, blocks, unit):
        def sb(n, shape, dt=F32):
            return ctx.enter_context(nc.sbuf_tensor(f"{name}_{n}", shape, dt))

        self.name, self.with_edge, self.out, self.blocks, self.unit = name, with_edge, out, blocks, unit
        wide = [LANES, EDGE_COLS]
        self.pos = sb("pos", wide)
        self.blk = sb("blk", wide)
        self.other = sb("other", wide)
        self.lane1 = sb("lane1", wide)
        self.values = [self.other, self.lane1]
        if with_edge:
            self.sixteens = sb("sixteens", wide)
            self.values.append(self.sixteens)
            self.column = sb("column", [P, blocks])
            self.packed = sb("packed", [P, 2, blocks], I32)

    def finish(self, nc, chain, tables):
        out, blocks = self.out, self.blocks
        chain.link(nc.vector.tensor_scalar(out.other, tables[:, 0, 0:blocks], float(NODE_MID), None, ALU.add))
        if not self.with_edge:
            chain.link(nc.vector.tensor_scalar(out.lane, tables[:, 1, 0:blocks], -1.0, None, ALU.add))
            return
        packed, column = self.packed, self.column
        chain.link(nc.vector.tensor_copy(packed[:, 0, :], tables[:, 1, 0:blocks]))
        chain.link(nc.vector.tensor_scalar(packed[:, 1, :], packed[:, 0, :], 4, None, ALU.arith_shift_right))
        chain.link(nc.vector.tensor_scalar(out.lane, packed[:, 1, :], -1.0, None, ALU.add))
        chain.link(nc.vector.tensor_scalar(packed[:, 1, :], packed[:, 0, :], 15, None, ALU.bitwise_and))
        chain.link(nc.vector.tensor_scalar(column[:], tables[:, 2, 0:blocks], 16.0, 16.0 * SIXTEENS_MID, ALU.mult, ALU.add))
        chain.link(nc.vector.tensor_tensor(out.edge, column[:], packed[:, 1, :], ALU.add))


def sort_edges(nc, sem, m, s, key_i, other_i):
    with ExitStack() as ctx:
        def sb(n, dt=F32):
            return ctx.enter_context(nc.sbuf_tensor(f"{s.name}_{n}", [LANES, EDGE_COLS], dt))

        lane = sb("lane")
        key = sb("key")
        bucket = sb("bucket")
        lane_i = sb("lane_i", I32)
        at = ctx.enter_context(nc.sbuf_tensor(f"{s.name}_at", [LANES, 1], F32))
        lane1, other = s.lane1, s.other
        count = m.count[0:LANES, 0:EDGE_COLS]
        with nc.Block() as block:

            @block.vector
            def _(dve):
                chain = m.steps
                nc.vector.tensor_copy(other[:], other_i[:])
                chain.link(nc.vector.tensor_copy(key[:], key_i[:]))
                chain.link(nc.vector.tensor_scalar(lane_i[:], key[:], 1 / TILES, -(TILES - 1) / 2 / TILES, ALU.mult, ALU.add))
                chain.link(nc.vector.tensor_copy(lane[:], lane_i[:]))
                nc.vector.scalar_tensor_tensor(bucket[:], lane[:], -float(TILES), key[:], ALU.mult, ALU.add)
                nc.vector.tensor_scalar(other[:], other[:], -float(NODE_MID), None, ALU.add)
                chain.link(nc.vector.tensor_scalar(lane1[:], lane[:], 1.0, None, ALU.add))
                if s.with_edge:
                    chain.link(nc.vector.tensor_scalar(lane_i[:], m.count_i[0:LANES, 0:EDGE_COLS], 4, None, ALU.arith_shift_right))
                    nc.vector.tensor_scalar(at[:], m.lane[0:LANES, :], EDGE_COLS / 16, -float(SIXTEENS_MID), ALU.mult, ALU.add)
                    chain.link(nc.vector.tensor_copy(s.sixteens[:], lane_i[:]))
                    chain.link(nc.vector.scalar_tensor_tensor(lane[:], s.sixteens[:], -16.0, count, ALU.mult, ALU.add))
                    nc.vector.scalar_tensor_tensor(lane1[:], lane1[:], 16.0, lane[:], ALU.mult, ALU.add)
                    chain.link(nc.vector.tensor_scalar(s.sixteens[:], s.sixteens[:], at[:], None, ALU.add))
        slots_of_buckets(nc, sem, m, s.name + "_sort", bucket[:], EDGE_COLS, TILES, s.blocks,
                         Slots(pos=s.pos[:], blk=s.blk[:], tile_row=s.out.tile_row), s.unit)


def stage_rows(nc, pool, m, z, turned, staged):
    def stage(n, u):
        if begun(n, 2):
            pool.wait_ge(turned, n - 1)
        nc.gpsimd.tensor_copy(z[u][:], m.y[:, bass.DynSlice(n * ST, ST), :]).then_inc(staged, 1)

    all_steps(pool, stage)


def turn_rows(nc, pe, m, n, z, t_ps, staged, turned_in, turned):
    pe.wait_ge(staged, n + 1)
    if begun(n, 2):
        pe.wait_ge(turned_in, n - 1)
    for t in range(ST):
        for k in range(KD):
            last = nc.tensor.transpose(t_ps[:, k, t * LANES:(t + 1) * LANES], z[:, t, k * P:(k + 1) * P], m.ident[0:LANES, 0:LANES])
    last.then_inc(turned, 1)


def node_mlp(nc, sem, m, io):
    w_in = sem("nmlp_weights_in")
    z_ready = sem("nmlp_z_ready")
    turned = sem("nmlp_turned")
    weights_split = sem("nmlp_weights_split")
    high_ready = sem("nmlp_high_ready")
    turned_in = sem("nmlp_turned_in")
    hid_whole = sem("nmlp_hid_whole")
    hid_high_ready = sem("nmlp_hid_high_ready")
    hid_up = sem("nmlp_hid_up")
    hid_ready = sem("nmlp_hid_ready")
    out_up = sem("nmlp_out_up")
    out_taken = sem("nmlp_out_taken")
    with ExitStack() as ctx:
        def sb(n, shape, dt=F32):
            return ctx.enter_context(nc.sbuf_tensor(f"nmlp_{n}", shape, dt))

        def two(n, shape, dt=F32):
            return [sb(f"{n}{u}", shape, dt) for u in range(2)]

        w1 = sb("w1", [P, KD, HID])
        w1h, w1l = (sb(f"w1_{part}", [P, KD, HID], F32R) for part in ("high", "low"))
        b1 = sb("b1", [P, KH])
        w2 = sb("w2", [P, KH, DIM])
        w2h, w2l = (sb(f"w2_{part}", [P, KH, DIM], F32R) for part in ("high", "low"))
        eps1 = sb("eps1", [LANES, 1])
        z = two("z", [LANES, ST, DIM])
        zth, ztl = (two(f"zt_{part}", [P, KD, SW], F32R) for part in ("high", "low"))
        hid = two("hid", [P, KH, SW])
        hidh, hidl = (two(f"hid_{part}", [P, KH, SW], F32R) for part in ("high", "low"))
        t_ps = [ctx.enter_context(nc.psum_tensor(f"nmlp_t_ps{u}", [P, KD, 256], F32)) for u in range(2)]
        h_ps = ctx.enter_context(nc.psum_tensor("nmlp_h_ps", [P, KH, 256], F32))
        o_ps = [ctx.enter_context(nc.psum_tensor(f"nmlp_o_ps{u}", [P, ST, DIM], F32)) for u in range(2)]
        with nc.Block() as block:

            @block.sync
            def _(sp):
                sp.dma_start(w1[:], io["Wn1"].rearrange("(k p) h -> p k h", p=P)).then_inc(w_in, 16)
                sp.dma_start(w2[:], io["Wn2"].rearrange("(k p) h -> p k h", p=P)).then_inc(w_in, 16)
                sp.dma_start(b1[:], io["bn1"]).then_inc(w_in, 16)

            @block.vector
            def _(dve):
                def combine(n, u):
                    if begun(n, 2):
                        dve.wait_ge(turned, n - 1)
                    tiles = bass.DynSlice(n * ST, ST)
                    nc.vector.scalar_tensor_tensor(z[u][:], m.y[:, tiles, :], eps1[:, 0:1], m.acc[:, tiles, :],
                                                   ALU.mult, ALU.add).then_inc(z_ready, 1)

                def take_turned(n, u):
                    dve.wait_ge(turned, n + 1)
                    nc.vector.tensor_copy(zth[u][:], t_ps[u][:, :, 0:SW]).then_inc(high_ready, 1)
                    dve.wait_ge(high_ready, n + 1)
                    nc.vector.tensor_tensor(ztl[u][:], t_ps[u][:, :, 0:SW], zth[u][:].bitcast(F32), ALU.subtract).then_inc(turned_in, 1)

                def hidden_low(n, u):
                    for half in range(2):
                        pieces = slice(2 * half, 2 * half + 2)
                        dve.wait_ge(hid_high_ready, 2 * n + (half + 1))
                        nc.vector.tensor_tensor(hidl[u][:, pieces, :], hid[u][:, pieces, :], hidh[u][:, pieces, :].bitcast(F32),
                                                ALU.subtract).then_inc(hid_ready, 1)

                def add_out(n, u):
                    tiles = bass.DynSlice(n * ST, ST)
                    dve.wait_ge(out_up, n + 1)
                    nc.vector.tensor_tensor(m.x[:, tiles, :], m.x[:, tiles, :], o_ps[u][0:LANES, :, :], ALU.add).then_inc(out_taken, 1)

                def statistics(n):
                    dve.wait_ge(out_taken, n + 1)
                    for t in range(ST):
                        one = bass.DynSlice(n * ST + t, 1)
                        nc.vector.bn_stats(m.stats[:, one, :].rearrange("p a s -> p (a s)"), m.x[:, one, :].rearrange("p a d -> p (a d)"))

                def one_step(n, u):
                    if left(n, 1):
                        take_turned(n + 1, 1 - u)
                    if left(n, 2):
                        combine(n + 2, u)
                    hidden_low(n, u)
                    if begun(n, 1):
                        add_out(n - 1, 1 - u)
                        statistics(n - 1)

                m.steps.link(nc.vector.tensor_scalar(eps1[:], m.eps[:], 1.0, None, ALU.add))
                combine(0, 0)
                combine(1, 1)
                take_turned(0, 0)
                dve.wait_ge(w_in, 48)
                split_rounded(nc, m.steps, w1[:], w1h[:], w1l[:]).then_inc(weights_split, 1)
                split_rounded(nc, m.steps, w2[:], w2h[:], w2l[:]).then_inc(weights_split, 1)
                m.steps.link(nc.vector.tensor_tensor(m.x[:], m.x[:], m.row_a[:, 1, :].unsqueeze(1).to_broadcast([LANES, TILES, DIM]), ALU.add))
                all_steps(dve, one_step)
                add_out(STEPS - 1, 1)
                statistics(STEPS - 1)

            @block.scalar
            def _(act):
                def one_step(n, u):
                    for half in range(2):
                        pieces = slice(2 * half, 2 * half + 2)
                        act.wait_ge(hid_up, 2 * n + (half + 1))
                        for h in (2 * half, 2 * half + 1):
                            last = nc.scalar.activation(hid[u][:, h, :], h_ps[:, h, 0:SW], ACT.Relu, bias=b1[:, h:h + 1])
                        last.then_inc(hid_whole, 1)
                        act.wait_ge(hid_whole, 2 * n + (half + 1))
                        nc.scalar.activation(hidh[u][:, pieces, :], hid[u][:, pieces, :], ACT.Copy).then_inc(hid_high_ready, 1)

                act.wait_ge(w_in, 48)
                all_steps(act, one_step)

            @block.tensor
            def _(pe):
                def hidden(n, u):
                    pe.wait_ge(turned_in, n + 1)
                    for h in range(KH):
                        if h % 2 == 0 and begun(n, 1):
                            pe.wait_ge(hid_whole, 2 * n + (h // 2 - 1))
                        piece = slice(h * P, (h + 1) * P)
                        for k in range(KD):
                            last = split_product(nc.tensor, h_ps[:, h, 0:SW], (w1h[:, k, piece], w1l[:, k, piece]),
                                                 (zth[u][:, k, :], ztl[u][:, k, :]), start=k == 0, stop=k == KD - 1)
                        if h % 2 == 1:
                            last.then_inc(hid_up, 1)

                def rows_out(n, u):
                    pe.wait_ge(hid_ready, 2 * n + 2)
                    if begun(n, 2):
                        pe.wait_ge(out_taken, n - 1)
                    for t in range(ST):
                        nodes = slice(t * LANES, (t + 1) * LANES)
                        for k in range(KH):
                            last = split_product(nc.tensor, o_ps[u][0:LANES, t, :], (hidh[u][:, k, nodes], hidl[u][:, k, nodes]),
                                                 (w2h[:, k, :], w2l[:, k, :]), start=k == 0, stop=k == KH - 1)
                    last.then_inc(out_up, 1)

                def one_step(n, u):
                    if left(n, 1):
                        turn_rows(nc, pe, m, n + 1, z[1 - u], t_ps[1 - u], z_ready, turned_in, turned)
                    hidden(n, u)
                    if begun(n, 1):
                        rows_out(n - 1, 1 - u)

                turn_rows(nc, pe, m, 0, z[0], t_ps[0], z_ready, turned_in, turned)
                pe.wait_ge(weights_split, 2)
                all_steps(pe, one_step)
                rows_out(STEPS - 1, 1)


class Routing:
    def __init__(self, sb):
        self.gate = sb("gate", [LANES, TOP, TILES])
        self.expert = sb("expert", [LANES, TOP, TILES])
        self.slot_i = sb("slot_i", [LANES, TOP, TILES], I32)
        self.node_of_slot = sb("node_of_slot", [P, MOE_BLOCKS], I32)
        self.block_expert = sb("block_expert", [1, MOE_BLOCKS], I32)


def moe_gates(nc, sem, m, io, r):
    in_ = sem("gate_in")
    staged = sem("gate_staged")
    turned = sem("gate_turned")
    turned_in = sem("gate_turned_in")
    up = sem("gate_up")
    taken = sem("gate_taken")
    logits_ready = sem("gate_logits_ready")
    exp_ready = sem("gate_exp_ready")
    with ExitStack() as ctx:
        def sb(n, shape, dt=F32):
            return ctx.enter_context(nc.sbuf_tensor(f"gate_{n}", shape, dt))

        w = sb("w", [P, KD, EXPERTS])
        b = sb("b", [LANES, EXPERTS])
        z = [sb(f"z{u}", [LANES, ST, DIM]) for u in range(2)]
        zt = [sb(f"zt{u}", [P, KD, SW]) for u in range(2)]
        logits = sb("logits", [LANES, TILES, EXPERTS])
        top = sb("top", [LANES, TILES, 8])
        which = sb("which", [LANES, TILES, 8], mybir.dt.uint32)
        big = sb("big", [LANES, TILES])
        t_ps = [ctx.enter_context(nc.psum_tensor(f"gate_t_ps{u}", [P, KD, 256], F32)) for u in range(2)]
        g_ps = [ctx.enter_context(nc.psum_tensor(f"gate_g_ps{u}", [P, ST, 256], F32)) for u in range(2)]
        wide = [LANES, TILES, EXPERTS]
        with nc.Block() as block:

            @block.sync
            def _(sp):
                sp.dma_start(w[:], io["gate_w"].rearrange("(k p) e -> p k e", p=P)).then_inc(in_, 16)
                sp.dma_start(b[:], io["gate_b"].partition_broadcast(LANES)).then_inc(in_, 16)

            @block.gpsimd
            def _(pool):
                stage_rows(nc, pool, m, z, turned, staged)

            @block.tensor
            def _(pe):
                def one_step(n, u):
                    if left(n, 1):
                        turn_rows(nc, pe, m, n + 1, z[1 - u], t_ps[1 - u], staged, turned_in, turned)
                    pe.wait_ge(turned_in, n + 1)
                    if begun(n, 2):
                        pe.wait_ge(taken, n - 1)
                    for t in range(ST):
                        for k in range(KD):
                            last = nc.tensor.matmul(g_ps[u][0:LANES, t, 0:EXPERTS], zt[u][:, k, t * LANES:(t + 1) * LANES], w[:, k, :],
                                                    start=k == 0, stop=k == KD - 1)
                    last.then_inc(up, 1)

                pe.wait_ge(in_, 32)
                turn_rows(nc, pe, m, 0, z[0], t_ps[0], staged, turned_in, turned)
                all_steps(pe, one_step)

            @block.scalar
            def _(act):
                def take_turned(n, u):
                    act.wait_ge(turned, n + 1)
                    if begun(n, 2):
                        act.wait_ge(up, n - 1)
                    nc.scalar.activation(zt[u][:], t_ps[u][:, :, 0:SW], ACT.Copy).then_inc(turned_in, 1)

                all_steps(act, take_turned)
                act.wait_ge(logits_ready, 1)
                nc.scalar.activation(logits[:], logits[:], ACT.Exp).then_inc(exp_ready, 1)

            @block.vector
            def _(dve):
                def take_logits(n, u):
                    dve.wait_ge(up, n + 1)
                    nc.vector.tensor_tensor(logits[:, bass.DynSlice(n * ST, ST), :], g_ps[u][0:LANES, :, 0:EXPERTS],
                                            b[:].unsqueeze(1).to_broadcast([LANES, ST, EXPERTS]), ALU.add).then_inc(taken, 1)

                dve.wait_ge(in_, 32)
                all_steps(dve, take_logits)
                dve.wait_ge(taken, STEPS)
                chain = m.steps
                chain.link(nc.vector.tensor_reduce(big[:], logits[:], AX_X, ALU.max))
                nc.vector.tensor_tensor(logits[:], logits[:], big[:].unsqueeze(2).to_broadcast(wide), ALU.subtract).then_inc(logits_ready, 1)
                dve.wait_ge(exp_ready, 1)
                chain.link(nc.vector.tensor_reduce(big[:], logits[:], AX_X, ALU.add))
                chain.link(nc.vector.reciprocal(big[:], big[:]))
                chain.link(nc.vector.tensor_tensor(logits[:], logits[:], big[:].unsqueeze(2).to_broadcast(wide), ALU.mult))
                for t in range(TILES):
                    last = nc.vector.max(top[:, t, :], logits[:, t, :])
                chain.link(last)
                for t in range(TILES):
                    last = nc.vector.max_index(which[:, t, :], top[:, t, :], logits[:, t, :])
                chain.link(last)
                chain.link(nc.vector.tensor_tensor(big[:], top[:, :, 0], top[:, :, 1], ALU.add))
                chain.link(nc.vector.reciprocal(big[:], big[:]))
                for k in range(TOP):
                    chain.link(nc.vector.tensor_tensor(r.gate[:, k, :], top[:, :, k], big[:], ALU.mult))
                    chain.link(nc.vector.tensor_copy(r.expert[:, k, :], which[:, :, k]))


def moe_experts(nc, sem, m, io, r, s):
    AB, WB = 2, 3
    idx_ready = sem("moe_idx_ready")
    rows_in = [sem(f"moe_rows_in{u}") for u in range(AB)]
    w_in = [sem(f"moe_w_in{u}") for u in range(WB)]
    turned = sem("moe_turned")
    turned_in = sem("moe_turned_in")
    h_up = sem("moe_h_up")
    silu_ready = sem("moe_silu_ready")
    hid_ready = sem("moe_hid_ready")
    y_up = sem("moe_y_up")
    y_ready = sem("moe_y_ready")
    stored = [sem(f"moe_stored{u}") for u in range(AB)]
    nb = MOE_BLOCKS
    unroll = AB * WB
    per_block = -(-EDGE_COLS // nb)
    assert nb % unroll == 0

    def blocks(eng, body):
        for k in range(unroll):
            body(k, k)
        with eng.Fori(1, nb // unroll - 1) as turn:
            for k in range(unroll):
                body(turn * unroll + k, k)
        for k in range(nb - unroll, nb):
            body(k, k % unroll)

    with ExitStack() as ctx:
        def sb(n, shape, dt=F32, bufs=AB):
            return [ctx.enter_context(nc.sbuf_tensor(f"moe_{n}{u}", shape, dt)) for u in range(bufs)]

        def ps(n, shape):
            return [ctx.enter_context(nc.psum_tensor(f"moe_{n}{u}", shape, F32)) for u in range(AB)]

        idx = sb("idx", [P, 1], I32)
        rows = sb("rows", [P, DIM])
        xt = sb("xt", [P, KD, P])
        w1 = sb("w1", [P, KD, HID], bufs=WB)
        w2 = sb("w2", [P, KD, HID], bufs=WB)
        w3 = sb("w3", [P, KH, DIM], bufs=WB)
        silu = sb("silu", [P, KH, P])
        hid = sb("hid", [P, KH, P])
        out = sb("out", [P, DIM])
        t_ps = ctx.enter_context(nc.psum_tensor("moe_t_ps", [P, KD, 256], F32))
        h1_ps = ps("h1_ps", [P, KH, P])
        h2_ps = ps("h2_ps", [P, KH, P])
        y_ps = ctx.enter_context(nc.psum_tensor("moe_y_ps", [P, 512], F32))
        placing = Placing(nc, sem, ctx, m, s.name + "_place", s.pos, s.blk, s.values, EDGE_COLS, s.blocks, bufs=2 * per_block)

        def columns(b, k):
            for n in range(per_block):
                c = b * per_block + n
                if not isinstance(c, int) or c < EDGE_COLS:
                    yield c, (k * per_block + n) % placing.bufs

        with nc.Block() as block:

            @block.gpsimd
            def _(pool):
                def gather(b, k):
                    pool.wait_ge(idx_ready, b + 1)
                    if begun(b, AB):
                        pool.wait_ge(turned, b - (AB - 1))
                    own_waits(pool, m)
                    pool.indirect_dma_start(rows[k % AB][:], None, m.node_table[:, :],
                                            bass.IndirectOffsetOnAxis(ap=idx[k % AB][:, 0:1], axis=0)).then_inc(rows_in[k % AB], 16)

                blocks(pool, gather)

            @block.sync
            def _(sp):
                def load(b, k):
                    e = sp.value_load(r.block_expert[0:1, bass.DynSlice(b, 1)], min_val=0, max_val=EXPERTS - 1)
                    one = bass.DynSlice(e, 1)
                    u = k % WB
                    if begun(b, WB):
                        sp.wait_ge(y_up, b - (WB - 1))
                    for w, wd in ((w1[u], io["w1"]), (w2[u], io["w2"]), (w3[u], io["w3"])):
                        sp.dma_start(w[:], wd[one, :, :].rearrange("a (k p) h -> p (a k) h", p=P)).then_inc(w_in[u], 16)

                def store(b, k):
                    sp.wait_ge(y_ready, b + 1)
                    sp.dma_start(m.routed[bass.DynSlice(b * P, P), :], out[k % AB][:]).then_inc(stored[k % AB], 16)

                def load_and_store(b, k):
                    load(b, k)
                    if begun(b, WB):
                        store(b - WB, (k - WB) % unroll)

                blocks(sp, load_and_store)
                for b in range(nb - WB, nb):
                    store(b, b % unroll)
                for u in range(AB):
                    sp.wait_ge(stored[u], nb // AB * 16)

            @block.tensor
            def _(pe):
                def transposes(b, k):
                    u = k % AB
                    if begun(b, 1):
                        pe.wait_ge(turned_in, b)
                    pe.wait_ge(rows_in[u], (b - u) * (16 // AB) + 16)
                    for kd in range(KD):
                        last = nc.tensor.transpose(t_ps[:, kd, 0:P], rows[u][:, kd * P:(kd + 1) * P], m.ident[:])
                    last.then_inc(turned, 1)

                def hidden(b, k):
                    u, v = k % AB, k % WB
                    pe.wait_ge(turned_in, b + 1)
                    pe.wait_ge(w_in[v], (b - v) * (48 // WB) + 48)
                    for w, h_ps in ((w1[v], h1_ps[u]), (w2[v], h2_ps[u])):
                        for c in range(KH):
                            for kd in range(KD):
                                last = nc.tensor.matmul(h_ps[:, c, :], w[:, kd, c * P:(c + 1) * P], xt[u][:, kd, :],
                                                        start=kd == 0, stop=kd == KD - 1)
                        last.then_inc(h_up, 1)

                def rows_out(b, k):
                    u, v = k % AB, k % WB
                    pe.wait_ge(hid_ready, b + 1)
                    if begun(b, 1):
                        pe.wait_ge(y_ready, b)
                    for kh in range(KH):
                        last = nc.tensor.matmul(y_ps[:, 0:DIM], hid[u][:, kh, :], w3[v][:, kh, :], start=kh == 0, stop=kh == KH - 1)
                    last.then_inc(y_up, 1)

                def place(b, k):
                    for c, u in columns(b, k):
                        static = isinstance(c, int)
                        placing.multiply(pe, c, u, start=static and c == 0, stop=static and c == EDGE_COLS - 1)

                def one_block(b, k):
                    hidden(b, k)
                    if begun(b, 1):
                        place(b - 1, (k - 1) % unroll)
                        rows_out(b - 1, (k - 1) % unroll)
                    if left(b, AB, nb):
                        transposes(b + AB, (k + AB) % unroll)

                for b in range(AB):
                    transposes(b, b)
                blocks(pe, one_block)
                place(nb - 1, unroll - 1)
                rows_out(nb - 1, unroll - 1)

            @block.scalar
            def _(act):
                def silus(b, k):
                    act.wait_ge(h_up, 2 * b + 1)
                    if begun(b, AB):
                        act.wait_ge(hid_ready, b - (AB - 1))
                    nc.scalar.activation(silu[k % AB][:], h1_ps[k % AB][:], ACT.Silu).then_inc(silu_ready, 1)

                def take_out(b, k):
                    u = k % AB
                    act.wait_ge(y_up, b + 1)
                    if begun(b, AB):
                        act.wait_ge(stored[u], (b - u) * (16 // AB))
                    nc.scalar.activation(out[u][:], y_ps[:, 0:DIM], ACT.Copy).then_inc(y_ready, 1)

                def one_block(b, k):
                    silus(b, k)
                    if begun(b, 1):
                        take_out(b - 1, (k - 1) % unroll)
                    for c, u in columns(b, k):
                        placing.scale(act, c, u, begun(b, 2))

                blocks(act, one_block)
                take_out(nb - 1, unroll - 1)

            @block.vector
            def _(dve):
                def stage(b, k):
                    nc.vector.tensor_copy(idx[k % AB][:], r.node_of_slot[:, bass.DynSlice(b, 1)]).then_inc(idx_ready, 1)

                def take_turned(b, k):
                    dve.wait_ge(turned, b + 1)
                    nc.vector.tensor_copy(xt[k % AB][:], t_ps[:, :, 0:P]).then_inc(turned_in, 1)

                def multiply(b, k):
                    dve.wait_ge(silu_ready, b + 1)
                    dve.wait_ge(h_up, 2 * b + 2)
                    nc.vector.tensor_tensor(hid[k % AB][:], silu[k % AB][:], h2_ps[k % AB][:], ALU.mult).then_inc(hid_ready, 1)

                def one_block(b, k):
                    multiply(b, k)
                    if left(b, AB, nb):
                        take_turned(b + AB, (k + AB) % unroll)
                    if left(b, 2 * AB, nb):
                        stage(b + 2 * AB, (k + 2 * AB) % unroll)
                    for c, u in columns(b, k):
                        placing.make(dve, c, u, begun(b, 2))

                for b in range(AB):
                    stage(b, b)
                for b in range(AB):
                    take_turned(b, b)
                    stage(b + AB, b + AB)
                blocks(dve, one_block)
                dve.wait_ge(placing.used, EDGE_COLS)
                s.finish(nc, m.steps, placing.tables)


def moe_combine(nc, sem, m, r):
    idx_ready = sem("comb_idx_ready")
    landed = [sem(f"comb_landed{u}") for u in range(4)]
    done = sem("comb_done")
    with ExitStack() as ctx:
        idx = [ctx.enter_context(nc.sbuf_tensor(f"comb_idx{u}", [LANES, 1], I32)) for u in range(4)]
        got = [ctx.enter_context(nc.sbuf_tensor(f"comb_got{u}", [LANES, DIM], F32)) for u in range(4)]
        with nc.Block() as block:

            @block.gpsimd
            def _(pool):
                def gather(u):
                    own_waits(nc.gpsimd, m)
                    nc.gpsimd.indirect_dma_start(got[u][:], None, m.routed[:, :],
                                                 bass.IndirectOffsetOnAxis(ap=idx[u][:, 0:1], axis=0)).then_inc(landed[u], 16)

                with pool.Fori(0, TILES // 2) as i:
                    for u in range(4):
                        pool.wait_ge(idx_ready, 4 * i + (u + 1))
                        gather(u)

            @block.vector
            def _(dve):
                def stage(i, u):
                    nc.vector.tensor_copy(idx[u][:], r.slot_i[:, u % 2, bass.DynSlice(2 * i + u // 2, 1)]).then_inc(idx_ready, 1)

                def take(i, u):
                    t = bass.DynSlice(2 * i + u // 2, 1)
                    dve.wait_ge(landed[u], 16 * i + 16)
                    if u % 2:
                        dve.wait_ge(done, 4 * i + u)
                    nc.vector.scalar_tensor_tensor(m.x[:, t, :], got[u][:].unsqueeze(1), r.gate[:, u % 2, t], m.x[:, t, :],
                                                   ALU.mult, ALU.add).then_inc(done, 1)

                def statistics(i, u):
                    one = bass.DynSlice(2 * i + u // 2, 1)
                    dve.wait_ge(done, 4 * i + (u + 1))
                    nc.vector.bn_stats(m.stats[:, one, :].rearrange("p a s -> p (a s)"), m.x[:, one, :].rearrange("p a d -> p (a d)"))

                for u in range(4):
                    stage(0, u)
                with dve.Fori(0, TILES // 2 - 1) as i:
                    for u in range(4):
                        take(i, u)
                        stage(i + 1, u)
                        if u % 2:
                            statistics(i, u)
                for u in range(4):
                    take(TILES // 2 - 1, u)
                    if u % 2:
                        statistics(TILES // 2 - 1, u)


def mixture(nc, sem, m, io, s):
    items = TOP * TILES
    with ExitStack() as ctx:
        def sb(n, shape, dt=F32):
            return ctx.enter_context(nc.sbuf_tensor(f"mix_{n}", shape, dt))

        r = Routing(sb)
        pos = sb("pos", [LANES, items])
        blk = sb("blk", [LANES, items])
        node = sb("node", [LANES, items])
        layer_norm(nc, sem, m, "ln_b", m.x, m.y, with_stats=False)
        node_table(nc, sem, m, "norm_table", m.y, m.node_table)
        moe_gates(nc, sem, m, io, r)
        slots_of_buckets(nc, sem, m, "mix_sort", r.expert[:].rearrange("p a t -> p (a t)"), items, EXPERTS, MOE_BLOCKS,
                         Slots(pos=pos[:], blk=blk[:], tile_row=r.block_expert[:]))
        with nc.Block() as block:

            @block.vector
            def _(dve):
                chain = m.steps
                for a in range(TOP):
                    chain.link(nc.vector.tensor_scalar(node[:, a * TILES:(a + 1) * TILES], m.node[:], -float(NODE_MID), None, ALU.add))
                chain.link(nc.vector.scalar_tensor_tensor(r.slot_i[:].rearrange("p a t -> p (a t)"), blk[:], float(P), pos[:], ALU.mult, ALU.add))

        def finish(dve, chain, tables):
            chain.link(nc.vector.tensor_scalar(r.node_of_slot[:], tables[:, 0, 0:MOE_BLOCKS], float(NODE_MID), None, ALU.add))

        place_in_slots(nc, sem, m, "mix_place", pos, blk, [node], items, MOE_BLOCKS, finish)
        moe_experts(nc, sem, m, io, r, s)
        moe_combine(nc, sem, m, r)


def attention_rows(nc, sem, m, io, sl):
    in_ = sem("hrow_in")
    staged = sem("hrow_staged")
    turned = sem("hrow_turned")
    turned_in = sem("hrow_turned_in")
    up = sem("hrow_up")
    copied = sem("hrow_copied")
    multiplied = sem("hrow_multiplied")
    summed = sem("hrow_summed")
    stored = sem("hrow_stored")
    with ExitStack() as ctx:
        def sb(n, shape, dt=F32):
            return ctx.enter_context(nc.sbuf_tensor(f"hrow_{n}", shape, dt))

        w = sb("w", [P, KD, HEADS * HEAD_C])
        a = sb("a", [LANES, 2, HEADS * HEAD_C])
        z = [sb(f"z{u}", [LANES, ST, DIM]) for u in range(2)]
        zt = [sb(f"zt{u}", [P, KD, SW]) for u in range(2)]
        rows = sb("rows", [LANES, TILES, ROW])
        prod = [sb(f"prod{u}", [LANES, ST, DIM]) for u in range(2)]
        t_ps = [ctx.enter_context(nc.psum_tensor(f"hrow_t_ps{u}", [P, KD, 256], F32)) for u in range(2)]
        h_ps = [ctx.enter_context(nc.psum_tensor(f"hrow_h_ps{u}", [P, ST, DIM], F32)) for u in range(2)]
        with nc.Block() as block:

            @block.sync
            def _(sp):
                for h, (wd, ad) in enumerate(((io["W1"], io["a1"]), (io["W2"], io["a2"]))):
                    part = slice(h * HEAD_C, (h + 1) * HEAD_C)
                    sp.dma_start(w[:, :, part], wd.rearrange("(k p) c -> p k c", p=P)).then_inc(in_, 16)
                    for side in range(2):
                        sp.dma_start(a[:, side, part], ad[0, side * HEAD_C:(side + 1) * HEAD_C].partition_broadcast(LANES)).then_inc(in_, 16)
                sp.wait_ge(copied, STEPS)
                sp.wait_ge(summed, 2 * STEPS)
                sp.dma_start(m.head_table.rearrange("(p t) d -> p t d", t=TILES), rows[:]).then_inc(stored, 16)
                sp.wait_ge(stored, 16)

            @block.gpsimd
            def _(pool):
                stage_rows(nc, pool, m, z, turned, staged)

            @block.tensor
            def _(pe):
                def one_step(n, u):
                    if left(n, 1):
                        turn_rows(nc, pe, m, n + 1, z[1 - u], t_ps[1 - u], staged, turned_in, turned)
                    pe.wait_ge(turned_in, n + 1)
                    if begun(n, 2):
                        pe.wait_ge(copied, n - 1)
                    for t in range(ST):
                        for k in range(KD):
                            last = nc.tensor.matmul(h_ps[u][0:LANES, t, :], zt[u][:, k, t * LANES:(t + 1) * LANES], w[:, k, :],
                                                    start=k == 0, stop=k == KD - 1)
                    last.then_inc(up, 1)

                pe.wait_ge(in_, 96)
                turn_rows(nc, pe, m, 0, z[0], t_ps[0], staged, turned_in, turned)
                all_steps(pe, one_step)

            @block.scalar
            def _(act):
                def one_step(n, u):
                    act.wait_ge(turned, n + 1)
                    if begun(n, 2):
                        act.wait_ge(up, n - 1)
                    nc.scalar.activation(zt[u][:], t_ps[u][:, :, 0:SW], ACT.Copy).then_inc(turned_in, 1)
                    if begun(n, 1):
                        take_rows(n - 1, 1 - u)

                def take_rows(n, u):
                    act.wait_ge(up, n + 1)
                    nc.scalar.activation(rows[:, bass.DynSlice(n * ST, ST), 0:DIM], h_ps[u][0:LANES, :, :], ACT.Copy).then_inc(copied, 1)

                all_steps(act, one_step)
                take_rows(STEPS - 1, 1)

            @block.vector
            def _(dve):
                def one_step(n, u):
                    tiles = bass.DynSlice(n * ST, ST)
                    dve.wait_ge(copied, n + 1)
                    for side in range(2):
                        if begun(n, 1):
                            dve.wait_ge(summed, 2 * n + (side - 1))
                        nc.vector.tensor_tensor(prod[side][:], rows[:, tiles, 0:DIM],
                                                a[:, side, :].unsqueeze(1).to_broadcast([LANES, ST, DIM]), ALU.mult).then_inc(multiplied, 1)
                    for side in range(2):
                        dve.wait_ge(multiplied, 2 * n + (side + 1))
                        to = sl[:, tiles, :] if side == 0 else rows[:, tiles, DIM:ROW]
                        nc.vector.tensor_reduce(to, prod[side][:].rearrange("p t (h c) -> p t h c", h=HEADS), AX_X, ALU.add).then_inc(summed, 1)

                dve.wait_ge(in_, 96)
                all_steps(dve, one_step)
                dve.wait_ge(summed, 2 * STEPS)


def split_scores(nc, sem, m, sl, parts):
    with ExitStack() as ctx:
        rest = ctx.enter_context(nc.sbuf_tensor("split_rest", [LANES, TILES, HEADS], F32))
        with nc.Block() as block:

            @block.vector
            def _(dve):
                chain = m.steps
                left = sl[:]
                for n in range(3):
                    part = parts[:, :, n * HEADS:(n + 1) * HEADS]
                    chain.link(nc.vector.tensor_copy(part, left))
                    if n < 2:
                        chain.link(nc.vector.tensor_tensor(rest[:], left, part, ALU.subtract))
                        left = rest[:]


def attend_edges(nc, sem, m, r, sl, acc):
    RB = 4
    idx_ready = sem("att_idx_ready")
    landed = [sem(f"att_landed{v}") for v in range(RB)]
    hot16_ready = sem("att_hot16_ready")
    hot_ready = sem("att_hot_ready")
    parts_summed = sem("att_parts_summed")
    turned = sem("att_turned")
    turned_in = sem("att_turned_in")
    sl_up = sem("att_sl_up")
    logit = sem("att_logit")
    lrelu_ready = sem("att_lrelu_ready")
    e_ready = sem("att_e_ready")
    scaled = sem("att_scaled")
    scattered = sem("att_scattered")
    added = sem("att_added")
    G = GROUP
    UN = G * P // PAIR
    groups = PAIR_BLOCKS // G
    turns = groups // RB
    assert groups % RB == 0

    def tiles_of(eng, g):
        return [eng.value_load(r.tile_row[0:1, bass.DynSlice(g * UN + n, 1)], min_val=0, max_val=TILES - 1) for n in range(UN)]

    with ExitStack() as ctx:
        def sb(n, shape, dt=F32, bufs=2):
            return [ctx.enter_context(nc.sbuf_tensor(f"att_{n}{u}", shape, dt)) for u in range(bufs)]

        def ps(n, shape):
            return ctx.enter_context(nc.psum_tensor(f"att_{n}", shape, F32))

        idx = sb("idx", [P, G], I32, RB)
        got = sb("got", [P, G, ROW], bufs=RB)
        hot16 = sb("hot16", [P, G, LANES], BF16)
        hot_t = sb("hot_t", [LANES, G, P], BF16)
        hot = sb("hot", [P, G, LANES])
        parts = sb("parts", [P, G, HEADS])
        z = sb("z", [P, G, HEADS])
        lrelu = sb("lrelu", [P, G, HEADS])
        e = sb("e", [P, G, HEADS])
        w = sb("w", [P, G, ROW])
        t_ps = ctx.enter_context(nc.psum_tensor("att_t_ps", [P, G, P], BF16))
        sl_ps = ps("sl_ps", [P, 512])
        s_ps = [ps(f"s_ps{u}", [P, UN, 512]) for u in range(2)]
        with nc.Block() as block:

            @block.gpsimd
            def _(pool):
                def gather(g, v):
                    pool.wait_ge(idx_ready, g + 1)
                    own_waits(pool, m)
                    for j in range(G):
                        pool.indirect_dma_start(got[v][:, j, :], None, m.head_table[:, :],
                                                bass.IndirectOffsetOnAxis(ap=idx[v][:, j:j + 1], axis=0)).then_inc(landed[v], 16)

                with pool.Fori(0, turns) as i:
                    for v in range(RB):
                        gather(RB * i + v, v)

            @block.tensor
            def _(pe):
                def source_scores(g, u):
                    tiles = tiles_of(pe, g)
                    pe.wait_ge(hot16_ready, g + 1)
                    for j in range(G):
                        last = nc.tensor.transpose(t_ps[0:LANES, j, :], hot16[u][:, j, :], m.ident16[:])
                    last.then_inc(turned, 1)
                    pe.wait_ge(turned_in, g + 1)
                    if not isinstance(g, int) or g > 0:
                        pe.wait_ge(parts_summed, g)
                    for j in range(G):
                        last = nc.tensor.matmul(sl_ps[:, j * 3 * HEADS:(j + 1) * 3 * HEADS], hot_t[u][:, j, :],
                                                sl[:, tiles[j * UN // G], :], start=True, stop=True)
                    last.then_inc(sl_up, 1)

                def scatter(g, u, wait_added=True):
                    pe.wait_ge(hot_ready, g + 1)
                    pe.wait_ge(scaled, g + 1)
                    if wait_added:
                        pe.wait_ge(added, (g - 1) * UN)
                    for j in range(G):
                        last = nc.tensor.matmul(s_ps[u][0:LANES, j * UN // G, 0:ROW], hot[u][:, j, :], w[u][:, j, :],
                                                start=j % (G // UN) == 0, stop=j % (G // UN) == G // UN - 1)
                    last.then_inc(scattered, 1)

                source_scores(0, 0)
                for v in range(RB):
                    source_scores(v + 1, (v + 1) % 2)
                    scatter(v, v % 2, v >= 2)
                with pe.Fori(1, turns - 1) as i:
                    for v in range(RB):
                        source_scores(RB * i + (v + 1), (v + 1) % 2)
                        scatter(RB * i + v, v % 2)
                for g in range(groups - RB, groups):
                    if g + 1 < groups:
                        source_scores(g + 1, (g + 1) % 2)
                    scatter(g, g % 2)

            @block.scalar
            def _(act):
                def one_group(g, u, begun=True):
                    act.wait_ge(turned, g + 1)
                    nc.scalar.activation(hot_t[u][:], t_ps[0:LANES, :, :], ACT.Copy).then_inc(turned_in, 1)
                    if begun:
                        act.wait_ge(scattered, g - 1)
                    nc.scalar.activation(hot[u][:], hot16[u][:], ACT.Copy).then_inc(hot_ready, 1)
                    act.wait_ge(lrelu_ready, g + 1)
                    nc.scalar.activation(e[u][:], lrelu[u][:], ACT.Exp, scale=-1.0).then_inc(e_ready, 1)

                for v in range(RB):
                    one_group(v, v % 2, v >= 2)
                with act.Fori(1, turns) as i:
                    for v in range(RB):
                        one_group(RB * i + v, v % 2)

            @block.vector
            def _(dve):
                def stage_idx(g, v):
                    nc.vector.tensor_copy(idx[v][:], r.other[:, bass.DynSlice(g * G, G)]).then_inc(idx_ready, 1)

                def one_hots(g, u):
                    for j in range(G):
                        last = nc.vector.tensor_scalar(hot16[u][:, j, :], m.count16[:, 0:LANES],
                                                       r.lane[:, bass.DynSlice(g * G + j, 1)], None, ALU.is_equal)
                    last.then_inc(hot16_ready, 1)

                def logits(g, u, v):
                    dve.wait_ge(sl_up, g + 1)
                    nc.vector.tensor_reduce(parts[u][:], sl_ps[:, 0:3 * G * HEADS].rearrange("p (j s h) -> p j h s", s=3, h=HEADS),
                                            AX_X, ALU.add).then_inc(parts_summed, 1)
                    dve.wait_ge(parts_summed, g + 1)
                    dve.wait_ge(landed[v], (g - v) * (16 * G // RB) + 16 * G)
                    nc.vector.tensor_tensor(z[u][:], parts[u][:], got[v][:, :, DIM:ROW], ALU.add).then_inc(logit, 1)
                    dve.wait_ge(logit, g + 1)
                    nc.vector.scalar_tensor_tensor(lrelu[u][:], z[u][:], NEG_SLOPE, z[u][:], ALU.mult, ALU.max).then_inc(lrelu_ready, 1)

                def scale_rows(g, u, v):
                    dve.wait_ge(e_ready, g + 1)
                    nc.vector.tensor_tensor(w[u][:, :, 0:DIM].rearrange("p j (h c) -> p j h c", h=HEADS),
                                            got[v][:, :, 0:DIM].rearrange("p j (h c) -> p j h c", h=HEADS),
                                            e[u][:].unsqueeze(3).to_broadcast([P, G, HEADS, HEAD_C]), ALU.mult)
                    nc.vector.tensor_copy(w[u][:, :, DIM:ROW], e[u][:]).then_inc(scaled, 1)

                def accumulate(g, u, first=False):
                    tiles = tiles_of(dve, g)
                    dve.wait_ge(scattered, g + 1)
                    for n, tile in enumerate(tiles):
                        if not first or n > 0:
                            dve.wait_ge(added, g * UN + n)
                        dve.tensor_tensor(acc[:, tile, :], s_ps[u][0:LANES, n, 0:ROW], acc[:, tile, :], ALU.add).then_inc(added, 1)

                def one_group(g, v, first=False, start=False):
                    u = v % 2
                    if left(g, 1, groups):
                        if not start:
                            dve.wait_ge(hot_ready, g)
                        one_hots(g + 1, 1 - u)
                    scale_rows(g, u, v)
                    if left(g, RB, groups):
                        stage_idx(g + RB, v)
                    if not start:
                        accumulate(g - 1, 1 - u, first)
                    if left(g, 1, groups):
                        logits(g + 1, 1 - u, (v + 1) % RB)

                zeroed = sem("att_acc_zeroed")
                for v in range(RB):
                    stage_idx(v, v)
                nc.vector.memset(acc[:], 0.0).then_inc(zeroed, 1)
                dve.wait_ge(zeroed, 1)
                one_hots(0, 0)
                logits(0, 0, 0)
                for v in range(RB):
                    one_group(v, v, first=v == 1, start=v == 0)
                with dve.Fori(1, turns - 1) as i:
                    for v in range(RB):
                        one_group(RB * i + v, v)
                for v in range(RB):
                    one_group(groups - RB + v, v)
                accumulate(groups - 1, 1)


def attention_out(nc, sem, m, acc):
    low_ready = sem("atto_low_ready")
    exp_ready = sem("atto_exp_ready")
    with ExitStack() as ctx:
        def sb(n, shape, dt=F32):
            return ctx.enter_context(nc.sbuf_tensor(f"atto_{n}", shape, dt))

        inv = sb("inv", [LANES, TILES, HEADS])
        low = sb("low", [LANES, TILES, DIM])
        feats = acc[:, :, 0:DIM]
        by_head = [LANES, TILES, HEADS, HEAD_C]
        with nc.Block() as block:

            @block.scalar
            def _(act):
                act.wait_ge(low_ready, 1)
                nc.scalar.activation(low[:], low[:], ACT.Exp).then_inc(exp_ready, 1)

            @block.vector
            def _(dve):
                chain = m.steps
                chain.link(nc.vector.reciprocal(inv[:], acc[:, :, DIM:ROW]))
                chain.link(nc.vector.tensor_tensor(feats.rearrange("p t (h c) -> p t h c", h=HEADS),
                                              feats.rearrange("p t (h c) -> p t h c", h=HEADS),
                                              inv[:].unsqueeze(3).to_broadcast(by_head), ALU.mult))
                nc.vector.tensor_scalar(low[:], feats, 0.0, None, ALU.min).then_inc(low_ready, 1)
                chain.link(nc.vector.scalar_tensor_tensor(m.x[:], feats, 0.0, m.x[:], ALU.max, ALU.add))
                dve.wait_ge(exp_ready, 1)
                chain.link(nc.vector.scalar_tensor_tensor(m.x[:], low[:], -1.0, m.x[:], ALU.add, ALU.add))


def graph_attention(nc, sem, m, io, r):
    with ExitStack() as ctx:
        def sb(n, shape, dt=F32):
            return ctx.enter_context(nc.sbuf_tensor(f"gat_{n}", shape, dt))

        sl = sb("sl", [LANES, TILES, HEADS])
        layer_norm(nc, sem, m, "ln_c", m.x, m.y, with_stats=False)
        attention_rows(nc, sem, m, io, sl)
        sl_parts = sb("sl_parts", [LANES, TILES, 3 * HEADS], BF16)
        split_scores(nc, sem, m, sl, sl_parts)
        acc = sb("acc", [LANES, TILES, ROW])
        attend_edges(nc, sem, m, r, sl_parts, acc)
        attention_out(nc, sem, m, acc)


class SliceState:
    def __init__(self, sb):
        self.weights = sb("weights", [LANES, TILES, INNER])
        self.mixed = sb("mixed", [P, PAIRS, DIM])
        self.b_out = sb("b_out", [LANES, DIM])
        self.tokens = sb("tokens", [P, PAIRS, P])
        self.norm = sb("norm", [P, PAIRS])


def slice_attention(nc, sem, m, io):
    with ExitStack() as ctx:
        def sb(n, shape, dt=F32):
            return ctx.enter_context(nc.sbuf_tensor(f"sa_{n}", shape, dt))

        layer_norm(nc, sem, m, "ln_d", m.x, m.y)
        s = SliceState(sb)
        slice_tokens(nc, sem, m, io, s)
        token_attention(nc, sem, m, io, s)
        slices_out(nc, sem, m, io, s)


def slice_tokens(nc, sem, m, io, s):
    in_ = sem("st_in")
    consts = sem("st_consts")
    weights_split = sem("st_weights_split")
    staged = sem("st_staged")
    turned = sem("st_turned")
    high_ready = sem("st_high_ready")
    turned_in = sem("st_turned_in")
    xm_up = sem("st_xm_up")
    xm_ready = sem("st_xm_ready")
    logits_up = sem("st_logits_up")
    logits_in = sem("st_logits_in")
    chain_s = sem("st_chain")
    shifted = sem("st_shifted")
    exp_ready = sem("st_exp_ready")
    fx_up = sem("st_fx_up")
    fx_ready = sem("st_fx_ready")
    w_ready = sem("st_w_ready")
    kept = sem("st_weights_kept")
    summed = sem("st_summed")
    with ExitStack() as ctx:
        def sb(n, shape, dt=F32):
            return ctx.enter_context(nc.sbuf_tensor(f"st_{n}", shape, dt))

        def two(n, shape):
            return [sb(f"{n}{u}", shape) for u in range(2)]

        def ps(n, shape):
            return ctx.enter_context(nc.psum_tensor(f"st_{n}", shape, F32))

        wx = sb("wx", [P, KD, INNER])
        wxh, wxl = (sb(f"wx_{part}", [P, KD, INNER], F32R) for part in ("high", "low"))
        wf = sb("wf", [P, KD, INNER])
        wfh, wfl = (sb(f"wf_{part}", [P, KD, INNER], F32R) for part in ("high", "low"))
        bx = sb("bx", [P, PAIRS])
        bf = sb("bf", [LANES, INNER])
        ws = sb("ws", [P, P])
        wst = sb("wst", [P, PAIRS, P])
        bs = sb("bs", [LANES, SLICES])
        bst = sb("bst", [LANES, INNER])
        temp = sb("temp", [P, SA_HEADS])
        z = two("z", [LANES, ST, DIM])
        zth, ztl = ([sb(f"zt_{part}{u}", [P, KD, SW], F32R) for u in range(2)] for part in ("high", "low"))
        xm = two("xm", [P, PAIRS, SW])
        fx = two("fx", [LANES, PAIRS, P + 1])
        w = two("w", [LANES, INNER])
        lg = two("lg", [LANES, INNER])
        big = sb("big", [LANES, SA_HEADS])
        total = sb("total", [LANES, SA_HEADS])
        xm_ps = ps("xm_ps", [P, PAIRS, 256])
        t_ps = xm_ps[:, KD:2 * KD, :]
        lg_ps = ps("lg_ps", [P, 512])
        fx_ps = ps("fx_ps", [P, 512])
        tok_ps = ps("tok_ps", [P, PAIRS, 512])
        heads = [LANES, SA_HEADS, SLICES]

        def by_head(ap):
            return ap.rearrange("p (h g) -> p h g", h=SA_HEADS)

        def by_pair(ap):
            return ap.rearrange("p (a c) -> p a c", a=PAIRS)

        with nc.Block() as block:

            @block.sync
            def _(sp):
                sp.dma_start(wx[:], io["W_x"].rearrange("(k p) i -> p k i", p=P)).then_inc(in_, 16)
                sp.dma_start(wf[:], io["W_fx"].rearrange("(k p) i -> p k i", p=P)).then_inc(in_, 16)
                sp.dma_start(bx[:], io["b_x"]).then_inc(in_, 16)
                sp.dma_start(bf[:], io["b_fx"].partition_broadcast(LANES)).then_inc(in_, 16)
                sp.dma_start(bs[:], io["b_slice"].partition_broadcast(LANES)).then_inc(in_, 16)
                sp.dma_start(temp[:], io["temperature"].rearrange("a h b c -> (a h b c)").partition_broadcast(P)).then_inc(in_, 16)
                sp.dma_start(s.b_out[:], io["b_out"].partition_broadcast(LANES)).then_inc(in_, 16)
                sp.wait_ge(consts, 1)
                for h in range(2):
                    part = slice(h * SA_D, (h + 1) * SA_D)
                    sp.dma_start(ws[part, part], io["W_slice"]).then_inc(in_, 16)

            @block.gpsimd
            def _(pool):
                nc.gpsimd.memset(ws[:], 0.0).then_inc(consts, 1)
                for u in range(2):
                    nc.gpsimd.memset(fx[u][:], 1.0).then_inc(consts, 1)
                stage_rows(nc, pool, m, z, turned, staged)

            @block.tensor
            def _(pe):
                def turn_rows(n, u):
                    pe.wait_ge(staged, n + 1)
                    if begun(n, 1):
                        pe.wait_ge(xm_ready, n * PAIRS)
                    for t in range(ST):
                        for k in range(KD):
                            last = nc.tensor.transpose(t_ps[:, k, t * LANES:(t + 1) * LANES], z[u][:, t, k * P:(k + 1) * P],
                                                       m.ident[0:LANES, 0:LANES])
                    last.then_inc(turned, 1)

                def x_mid(n, u, pairs):
                    for p in pairs:
                        if p == 0:
                            pe.wait_ge(turned_in, n + 1)
                        piece = slice(p * P, (p + 1) * P)
                        for k in range(KD):
                            last = split_product(nc.tensor, xm_ps[:, p, 0:SW], (wxh[:, k, piece], wxl[:, k, piece]),
                                                 (zth[u][:, k, :], ztl[u][:, k, :]), start=k == 0, stop=k == KD - 1)
                    last.then_inc(xm_up, 1)

                def logits_and_fx(n, u, t):
                    tile = n * ST + t
                    nodes = slice(t * LANES, (t + 1) * LANES)
                    if t == 0:
                        pe.wait_ge(xm_ready, n * PAIRS + PAIRS)
                    if begun(tile, 1):
                        pe.wait_ge(logits_in, tile)
                    for p in range(PAIRS):
                        last = nc.tensor.matmul(lg_ps[0:LANES, p * P:(p + 1) * P], xm[u][:, p, nodes], wst[:, p, :], start=True, stop=True)
                    last.then_inc(logits_up, 1)
                    if begun(tile, 1):
                        pe.wait_ge(fx_ready, tile)
                    for k in range(KD):
                        last = split_product(nc.tensor, fx_ps[0:LANES, :], (zth[u][:, k, nodes], ztl[u][:, k, nodes]),
                                             (wfh[:, k, :], wfl[:, k, :]), start=k == 0, stop=k == KD - 1)
                    last.then_inc(fx_up, 1)

                def sum_tokens(tile, t):
                    pe.wait_ge(fx_ready, tile + 1)
                    pe.wait_ge(w_ready, tile + 1)
                    static = isinstance(tile, int)
                    for p in range(PAIRS):
                        last = nc.tensor.matmul(tok_ps[:, p, 0:P + 1], w[t][:, p * P:(p + 1) * P], fx[t][:, p, :],
                                                start=static and tile == 0, stop=static and tile == TILES - 1)
                    last.then_inc(summed, 1)

                def one_step(n, u):
                    if left(n, 1):
                        turn_rows(n + 1, 1 - u)
                    for t in range(ST):
                        logits_and_fx(n, u, t)
                        if left(n, 1):
                            x_mid(n + 1, 1 - u, range(2 * t, 2 * t + 2))
                        if begun(n, 1) or t > 0:
                            sum_tokens(n * ST + (t - 1), 1 - t)

                turn_rows(0, 0)
                pe.wait_ge(weights_split, 2)
                for t in range(ST):
                    x_mid(0, 0, range(2 * t, 2 * t + 2))
                pe.wait_ge(consts, 4)
                all_steps(pe, one_step)
                sum_tokens(TILES - 1, ST - 1)

            @block.scalar
            def _(act):
                def take_x_mid(n, u, t):
                    act.wait_ge(xm_up, n * ST + (t + 1))
                    for p in (2 * t, 2 * t + 1):
                        nc.scalar.activation(xm[u][:, p, :], xm_ps[:, p, 0:SW], ACT.Identity, bias=bx[:, p:p + 1]).then_inc(xm_ready, 1)

                def one_step(n, u):
                    for t in range(ST):
                        act.wait_ge(shifted, n * ST + (t + 1))
                        nc.scalar.activation(lg[t][:], lg[t][:], ACT.Exp).then_inc(exp_ready, 1)
                        if left(n, 1):
                            take_x_mid(n + 1, 1 - u, t)
                        if begun(n, 1) or t > 0:
                            keep_weights(n * ST + (t - 1), 1 - t)

                def keep_weights(tile, t):
                    act.wait_ge(w_ready, tile + 1)
                    nc.scalar.activation(s.weights[:, bass.DynSlice(tile, 1), :], w[t][:].unsqueeze(1), ACT.Identity).then_inc(kept, 1)

                act.wait_ge(in_, 144)
                for t in range(ST):
                    take_x_mid(0, 0, t)
                all_steps(act, one_step)
                keep_weights(TILES - 1, ST - 1)

            @block.vector
            def _(dve):
                def take_turned(n, u):
                    dve.wait_ge(turned, n + 1)
                    nc.vector.tensor_copy(zth[u][:], t_ps[:, :, 0:SW]).then_inc(high_ready, 1)
                    dve.wait_ge(high_ready, n + 1)
                    nc.vector.tensor_tensor(ztl[u][:], t_ps[:, :, 0:SW], zth[u][:].bitcast(F32), ALU.subtract).then_inc(turned_in, 1)

                def softmax(tile, t):
                    dve.wait_ge(logits_up, tile + 1)
                    if begun(tile, 2):
                        dve.wait_ge(w_ready, tile - 1)
                    nc.vector.tensor_tensor(lg[t][:], lg_ps[0:LANES, :], bst[:], ALU.add).then_inc(logits_in, 1)
                    dve.wait_ge(logits_in, tile + 1)
                    nc.vector.tensor_reduce(big[:], by_head(lg[t][:]), AX_X, ALU.max).then_inc(chain_s, 1)
                    dve.wait_ge(chain_s, 3 * tile + 1)
                    nc.vector.tensor_tensor(by_head(lg[t][:]), by_head(lg[t][:]), big[:].unsqueeze(2).to_broadcast(heads),
                                            ALU.subtract).then_inc(shifted, 1)
                    dve.wait_ge(fx_up, tile + 1)
                    if begun(tile, 2):
                        dve.wait_ge(summed, tile - 1)
                    nc.vector.tensor_tensor(fx[t][:, :, 0:P], by_pair(fx_ps[0:LANES, :]), by_pair(bf[:]), ALU.add).then_inc(fx_ready, 1)
                    dve.wait_ge(exp_ready, tile + 1)
                    if begun(tile, 1):
                        dve.wait_ge(w_ready, tile)
                    nc.vector.tensor_reduce(total[:], by_head(lg[t][:]), AX_X, ALU.add).then_inc(chain_s, 1)
                    dve.wait_ge(chain_s, 3 * tile + 2)
                    nc.vector.reciprocal(total[:], total[:]).then_inc(chain_s, 1)
                    dve.wait_ge(chain_s, 3 * tile + 3)
                    if begun(tile, 2):
                        dve.wait_ge(kept, tile - 1)
                    nc.vector.tensor_tensor(by_head(w[t][:]), by_head(lg[t][:]), total[:].unsqueeze(2).to_broadcast(heads),
                                            ALU.mult).then_inc(w_ready, 1)

                def one_step(n, u):
                    if left(n, 1):
                        take_turned(n + 1, 1 - u)
                    for t in range(ST):
                        softmax(n * ST + t, t)

                take_turned(0, 0)
                setup = m.steps
                dve.wait_ge(in_, 144)
                split_rounded(nc, setup, wx[:], wxh[:], wxl[:]).then_inc(weights_split, 1)
                split_rounded(nc, setup, wf[:], wfh[:], wfl[:]).then_inc(weights_split, 1)
                setup.link(nc.vector.tensor_scalar(temp[:], temp[:], 0.1, 5.0, ALU.max, ALU.min))
                setup.link(nc.vector.reciprocal(temp[:], temp[:]))
                nc.vector.tensor_tensor(by_head(bst[:]), bs[:].unsqueeze(1).to_broadcast(heads),
                                        temp[0:LANES, :].unsqueeze(2).to_broadcast(heads), ALU.mult)
                setup.link(nc.vector.tensor_tensor(
                    wst[:].rearrange("p a (h g) -> p a h g", h=2), ws[:].rearrange("p (h g) -> p h g", h=2).unsqueeze(1).to_broadcast([P, PAIRS, 2, SLICES]),
                    temp[:].rearrange("p (a h) -> p a h", h=2).unsqueeze(3).to_broadcast([P, PAIRS, 2, SLICES]), ALU.mult))
                dve.wait_ge(consts, 3)
                dve.sem_inc(consts, 1)
                all_steps(dve, one_step)
                dve.wait_ge(summed, TILES)
                nc.vector.tensor_copy(s.tokens[:], tok_ps[:, :, 0:P])
                nc.vector.tensor_copy(s.norm[:], tok_ps[:, :, P])


def token_attention(nc, sem, m, io, s):
    in_ = sem("ta_in")
    consts = sem("ta_consts")
    tok_ready = sem("ta_tok_ready")
    pe_up = sem("ta_pe_up")
    taken = sem("ta_taken")
    exp_in = sem("ta_exp_in")
    exp_ready = sem("ta_exp_ready")
    with ExitStack() as ctx:
        def sb(n, shape, dt=F32):
            return ctx.enter_context(nc.sbuf_tensor(f"ta_{n}", shape, dt))

        wq, wk, wv = (sb(n, [P, P]) for n in ("wq", "wk", "wv"))
        wo = sb("wo", [P, PAIRS, DIM])
        inv = sb("inv", [P, PAIRS])
        tok = sb("tok", [P, PAIRS, P])
        tok_t = sb("tok_t", [P, PAIRS, P])
        q_t = sb("q_t", [P, PAIRS, P])
        k_t = sb("k_t", [P, PAIRS, P])
        v = sb("v", [P, PAIRS, P])
        at = sb("at", [P, PAIRS, P])
        at_t = sb("at_t", [P, PAIRS, P])
        mix_t = sb("mix_t", [P, PAIRS, P])
        big = sb("big", [P, PAIRS])
        total = sb("total", [P, PAIRS])
        ps = [ctx.enter_context(nc.psum_tensor(f"ta_ps{n}", [P, PAIRS, P], F32)) for n in range(4)]
        mo_ps = ctx.enter_context(nc.psum_tensor("ta_mo_ps", [P, PAIRS, DIM], F32))
        halves = [slice(0, SA_D), slice(SA_D, P)]
        with nc.Block() as block:

            @block.sync
            def _(sp):
                sp.wait_ge(consts, 3)
                for w, wd in ((wq, io["W_q"]), (wk, io["W_k"]), (wv, io["W_v"])):
                    for part in halves:
                        sp.dma_start(w[part, part], wd).then_inc(in_, 16)
                sp.dma_start(wo[:], io["W_out"].rearrange("(k p) d -> p k d", p=P)).then_inc(in_, 16)

            @block.gpsimd
            def _(pool):
                for w in (wq, wk, wv):
                    nc.gpsimd.memset(w[:], 0.0).then_inc(consts, 1)

            @block.tensor
            def _(pe):
                pe.wait_ge(in_, 112)

                def pairwise(to, left, right, transpose=False):
                    for p in range(PAIRS):
                        if transpose:
                            last = nc.tensor.transpose(to[:, p, :], left(p), m.ident[:])
                        else:
                            last = nc.tensor.matmul(to[:, p, :], left(p), right(p), start=True, stop=True)
                    last.then_inc(pe_up, 1)

                pe.wait_ge(tok_ready, 1)
                pairwise(ps[0], lambda p: tok[:, p, :], None, True)
                pe.wait_ge(taken, 1)
                pairwise(ps[1], lambda p: wq[:], lambda p: tok_t[:, p, :])
                pairwise(ps[2], lambda p: wk[:], lambda p: tok_t[:, p, :])
                pairwise(ps[3], lambda p: tok_t[:, p, :], lambda p: wv[:])
                pe.wait_ge(taken, 3)
                pairwise(ps[0], lambda p: q_t[:, p, :], lambda p: k_t[:, p, :])
                pe.wait_ge(taken, 5)
                pairwise(ps[1], lambda p: at[:, p, :], None, True)
                pe.wait_ge(taken, 6)
                pairwise(ps[2], lambda p: v[:, p, :], lambda p: at_t[:, p, :])
                pe.wait_ge(taken, 7)
                for p in range(PAIRS):
                    last = nc.tensor.matmul(mo_ps[:, p, :], mix_t[:, p, :], wo[:, p, :], start=True, stop=True)
                last.then_inc(pe_up, 1)

            @block.scalar
            def _(act):
                act.wait_ge(exp_in, 1)
                for part in halves:
                    last = nc.scalar.activation(at[part, :, part], at[part, :, part], ACT.Exp)
                last.then_inc(exp_ready, 1)

            @block.vector
            def _(dve):
                chain = m.steps
                chain.link(nc.vector.tensor_scalar(inv[:], s.norm[:], 1e-5, None, ALU.add))
                chain.link(nc.vector.reciprocal(inv[:], inv[:]))
                chain.link(nc.vector.memset(tok[:], 0.0))
                chain.link(nc.vector.memset(at[:], 0.0))
                for part in halves:
                    chain.link(nc.vector.tensor_tensor(tok[part, :, part], s.tokens[part, :, part],
                                                  inv[part, :].unsqueeze(2).to_broadcast([SA_D, PAIRS, SA_D]), ALU.mult))
                nc.vector.memset(total[:], 0.0).then_inc(tok_ready, 1)
                for n, (to, src) in enumerate(((tok_t, ps[0]), (q_t, ps[1]), (k_t, ps[2]), (v, ps[3]))):
                    dve.wait_ge(pe_up, n + 1)
                    nc.vector.tensor_copy(to[:], src[:]).then_inc(taken, 1)
                dve.wait_ge(pe_up, 5)
                for part in halves:
                    wide = [SA_D, PAIRS, SA_D]
                    chain.link(nc.vector.tensor_scalar(at[part, :, part], ps[0][part, :, part], SA_D ** -0.5, None, ALU.mult))
                    chain.link(nc.vector.tensor_reduce(big[part, :], at[part, :, part], AX_X, ALU.max))
                    last = nc.vector.tensor_tensor(at[part, :, part], at[part, :, part], big[part, :].unsqueeze(2).to_broadcast(wide),
                                                   ALU.subtract)
                last.then_inc(exp_in, 1)
                dve.wait_ge(exp_ready, 1)
                for part in halves:
                    chain.link(nc.vector.tensor_reduce(total[part, :], at[part, :, part], AX_X, ALU.add))
                chain.link(nc.vector.reciprocal(total[:], total[:]))
                nc.vector.tensor_tensor(at[:], at[:], total[:].unsqueeze(2).to_broadcast([P, PAIRS, P]), ALU.mult).then_inc(taken, 1)
                dve.wait_ge(pe_up, 6)
                nc.vector.tensor_copy(at_t[:], ps[1][:]).then_inc(taken, 1)
                dve.wait_ge(pe_up, 7)
                nc.vector.tensor_copy(mix_t[:], ps[2][:]).then_inc(taken, 1)
                dve.wait_ge(pe_up, 8)
                nc.vector.tensor_copy(s.mixed[:], mo_ps[:]).then_inc(taken, 1)


def slices_out(nc, sem, m, io, s):
    staged = sem("so_staged")
    turned = sem("so_turned")
    turned_in = sem("so_turned_in")
    up = sem("so_up")
    taken = sem("so_taken")
    biased = sem("so_biased")
    with ExitStack() as ctx:
        w = [ctx.enter_context(nc.sbuf_tensor(f"so_w{u}", [LANES, INNER], F32)) for u in range(2)]
        w_t = [ctx.enter_context(nc.sbuf_tensor(f"so_w_t{u}", [P, PAIRS, P], F32)) for u in range(2)]
        t_ps = [ctx.enter_context(nc.psum_tensor(f"so_t_ps{u}", [P, PAIRS, P], F32)) for u in range(2)]
        o_ps = [ctx.enter_context(nc.psum_tensor(f"so_o_ps{u}", [P, 512], F32)) for u in range(2)]
        turns = TILES // 2
        with nc.Block() as block:

            @block.tensor
            def _(pe):
                def turn(t, u):
                    pe.wait_ge(staged, t + 1)
                    for p in range(PAIRS):
                        last = nc.tensor.transpose(t_ps[u][:, p, 0:LANES], w[u][:, p * P:(p + 1) * P], m.ident[0:LANES, 0:LANES])
                    last.then_inc(turned, 1)

                def products(t, u):
                    pe.wait_ge(turned_in, t + 1)
                    if begun(t, 2):
                        pe.wait_ge(taken, t - 1)
                    for p in range(PAIRS):
                        last = nc.tensor.matmul(o_ps[u][0:LANES, 0:DIM], w_t[u][:, p, 0:LANES], s.mixed[:, p, :],
                                                start=p == 0, stop=p == PAIRS - 1)
                    last.then_inc(up, 1)

                turn(0, 0)
                for t in range(2):
                    turn(t + 1, 1 - t)
                    products(t, t)
                with pe.Fori(1, turns - 1) as i:
                    for u in range(2):
                        turn(2 * i + (u + 1), 1 - u)
                        products(2 * i + u, u)
                turn(TILES - 1, 1)
                products(TILES - 2, 0)
                products(TILES - 1, 1)

            @block.scalar
            def _(act):
                with act.Fori(0, turns) as i:
                    for u in range(2):
                        act.wait_ge(turned, 2 * i + (u + 1))
                        nc.scalar.activation(w_t[u][:, :, 0:LANES], t_ps[u][:, :, 0:LANES], ACT.Copy).then_inc(turned_in, 1)

            @block.vector
            def _(dve):
                def stage(t, u):
                    nc.vector.tensor_copy(w[u][:].unsqueeze(1), s.weights[:, bass.DynSlice(t, 1), :]).then_inc(staged, 1)

                def take(t, u):
                    one = bass.DynSlice(t, 1)
                    dve.wait_ge(up, t + 1)
                    nc.vector.tensor_tensor(m.x[:, one, :], o_ps[u][0:LANES, 0:DIM].unsqueeze(1), m.x[:, one, :], ALU.add).then_inc(taken, 1)

                for u in range(2):
                    stage(u, u)
                nc.vector.tensor_tensor(m.x[:], m.x[:], s.b_out[:].unsqueeze(1).to_broadcast([LANES, TILES, DIM]), ALU.add).then_inc(biased, 1)
                dve.wait_ge(biased, 1)
                with dve.Fori(0, turns - 1) as i:
                    for u in range(2):
                        dve.wait_ge(turned, 2 * i + (u + 1))
                        stage(2 * i + (u + 2), u)
                        take(2 * i + u, u)
                for u in range(2):
                    take(TILES - 2 + u, u)


def gather_and_update(nc, sem, m, io):
    with ExitStack() as ctx:
        def sb(n, shape, dt=F32):
            return ctx.enter_context(nc.sbuf_tensor(f"gine_{n}", shape, dt))

        m.edge_of_slot = sb("edge_of_slot", [P, EDGE_BLOCKS], I32)
        m.src_of_slot = sb("src_of_slot", [P, EDGE_BLOCKS], I32)
        m.dst_lane = sb("dst_lane", [P, EDGE_BLOCKS])
        m.dst_tile = sb("dst_tile", [1, EDGE_BLOCKS], I32)
        with ExitStack() as sorting:
            s = EdgeSort(nc, sorting, "by_dst", True,
                         Ends(m.src_of_slot[:], m.dst_lane[:], m.dst_tile[:], edge=m.edge_of_slot[:]), EDGE_BLOCKS, P)
            sort_edges(nc, sem, m, s, m.dst_i, m.src_i)

            def finish(dve, chain, tables):
                s.finish(nc, chain, tables)

            place_in_slots(nc, sem, m, "by_dst_place", s.pos, s.blk, s.values, EDGE_COLS, EDGE_BLOCKS, finish, bufs=16)
        m.acc = sb("acc", [LANES, TILES, DIM])
        wait_for_rows(nc, m)
        layer_norm(nc, sem, m, "ln_a", m.x, m.y)
        edge_messages(nc, sem, m, io)
        node_mlp(nc, sem, m, io)


def store_output(nc, sem, m, out):
    stored = sem("out_stored")
    with nc.Block() as block:

        @block.sync
        def _(sp):
            sp.dma_start(out.rearrange("(p t) d -> p t d", t=TILES), m.x[:]).then_inc(stored, 16)
            sp.wait_ge(stored, 16)


def gnn_moe_gat_slice_kernel(nc, io_gine, io_moe, io_gat, io_slice, out):
    with ExitStack() as ctx:
        def sb(n, shape, dt=F32):
            return ctx.enter_context(nc.sbuf_tensor(n, shape, dt))

        def sem(n):
            return ctx.enter_context(nc.semaphore(n))

        m = Shared(nc, sb, sem)
        by_src = Ends(sb("slots_by_src_other", [P, PAIR_BLOCKS], I32)[:], sb("slots_by_src_lane", [P, PAIR_BLOCKS])[:],
                      sb("slots_by_src_tile_row", [1, PAIR_BLOCKS // 2], I32)[:])
        constants(nc, m, sem)
        load_inputs(nc, sem, m, io_gine)
        gather_and_update(nc, sem, m, io_gine)
        with ExitStack() as sorting:
            s = EdgeSort(nc, sorting, "by_src", False, by_src, PAIR_BLOCKS, PAIR)
            sort_edges(nc, sem, m, s, m.src_i, m.dst_i)
            mixture(nc, sem, m, io_moe, s)
        graph_attention(nc, sem, m, io_gat, by_src)
        slice_attention(nc, sem, m, io_slice)
        store_output(nc, sem, m, out)


GINE = ["x", "src", "dst", "edge_attr_256"] + ["L0_gnn_" + n for n in
                                               ("We1", "be1", "We2", "be2", "Wn1", "bn1", "Wn2", "bn2", "eps")]
MOE = ["L0_ffn_" + n for n in ("gate_w", "gate_b", "w1", "w2", "w3")]
GAT = ["L1_gnn_" + n for n in ("W1", "a1", "W2", "a2")]
SLICE = ["L1_ffn_" + n for n in ("W_fx", "b_fx", "W_x", "b_x", "W_slice", "b_slice", "W_q", "W_k", "W_v", "W_out", "b_out",
                                 "temperature")]
BY_PARTITION = ("L0_gnn_be1", "L0_gnn_bn1", "L1_ffn_b_x")


def kernel(**inputs):
    import numpy as _np
    import concourse.bacc as _bacc
    from concourse import mybir as _mybir
    from concourse.bass_utils import run_bass_kernel_spmd as _run

    nc = _bacc.Bacc("TRN2", target_bir_lowering=False, num_devices=1)
    arrays, ios = {}, []
    for names in (GINE, MOE, GAT, SLICE):
        io = {}
        for name in names:
            a = _np.asarray(inputs[name])
            if name in BY_PARTITION:
                a = a.reshape(-1, P).T
            a = _np.ascontiguousarray(a)
            arrays[f"in_{name}_dram"] = a
            io[name.split("_", 2)[2] if name[0] == "L" else name] = nc.dram_tensor(
                f"in_{name}_dram", a.shape, _mybir.dt.from_np(a.dtype), kind="ExternalInput").ap()
        ios.append(io)
    out = nc.dram_tensor("out_0_dram", (N_NODES, DIM), F32, kind="ExternalOutput").ap()
    gnn_moe_gat_slice_kernel(nc, *ios, out)
    r = _run(nc, [arrays], core_ids=[0])
    return r.results[0]["out_0_dram"]
```
